# Optimizing a Trainium2 kernel written in Bass

```python
import numpy as np
import jax
import jax.numpy as jnp

def _softmax(x, axis=-1):
    return jax.nn.softmax(x, axis=axis)

def _gelu(x):
    return jax.nn.gelu(x, approximate=True)

def _silu(x):
    return jax.nn.silu(x)

def _sigmoid(x):
    return jax.nn.sigmoid(x)

def _layernorm(x, axis=-1, eps=1e-05):
    m = jnp.mean(x, axis=axis, keepdims=True)
    v = jnp.var(x, axis=axis, keepdims=True)
    return (x - m) / jnp.sqrt(v + eps)

def _scatter_add(tgt, idx, src, axis=0):
    return tgt.at[idx].add(src)

def _segment_sum(src, seg, n):
    return jax.ops.segment_sum(src, seg, n)
kernel_name = 'mk_gnn_ffn_d2_gnn_r32_8d2dfb'

def setup_inputs(seed: int=0):
    np.random.seed(seed)
    _w = jnp.asarray

    def _rec_inputs():
        import jax
        import jax.numpy as jnp
        _gk = jax.random.key(seed)
        x = -0.0006008 + 1.001 * jax.random.normal(jax.random.fold_in(_gk, 1), (3125, 256), jnp.float32)
        src = jax.random.randint(jax.random.fold_in(_gk, 2), (50000,), 0, 3125, jnp.int32)
        dst = jnp.minimum((3125 * jax.random.uniform(jax.random.fold_in(_gk, 3), (50000,)) ** 2.0).astype(jnp.int32), 99999)
        _o = jnp.argsort(dst, stable=True)
        src = src[_o]
        dst = dst[_o]
        edge_attr_64 = 0.000151818 + 1.00006 * jax.random.normal(jax.random.fold_in(_gk, 12), (50000, 64), jnp.float32)
        edge_weight = jax.random.uniform(jax.random.fold_in(_gk, 14), (50000,), jnp.float32, 0.0, 0.999998)
        return (x, src, dst, edge_attr_64, edge_weight)
    x, src, dst, edge_attr_64, edge_weight = _rec_inputs()

    def _L0_gnn_setup():
        import jax, jax.numpy as jnp
        import numpy as np
        import math
        HIDDEN = 256
        NUM_GAUSSIANS = 64
        NUM_FILTERS = 256
        CUTOFF = 1.0
        COSINE_OFFSET = 0.0
        N_NODES = 10000
        N_EDGES = 10000

        def ssp(x):
            return jax.nn.softplus(x) - jnp.log(2.0).astype(x.dtype)
        key = jax.random.key(seed)
        ks = jax.random.split(key, 12)

        def xavier(k, fan_out, fan_in):
            a = math.sqrt(6.0 / (fan_in + fan_out))
            return jax.random.uniform(k, (fan_out, fan_in), jnp.float32, -a, a)
        x = jax.random.normal(ks[0], (N_NODES, HIDDEN), jnp.float32)
        ji_pairs = jax.random.randint(ks[1], (2, N_EDGES), 0, N_NODES, jnp.int64)
        e_ji = jax.random.uniform(ks[2], (N_EDGES,), jnp.float32)
        e_ji_basis = jax.random.normal(ks[3], (N_EDGES, NUM_GAUSSIANS), jnp.float32)
        return {'x': x, 'ji_pairs': ji_pairs, 'e_ji': e_ji, 'e_ji_basis': e_ji_basis, 'fw1': xavier(ks[4], NUM_FILTERS, NUM_GAUSSIANS), 'fb1': jnp.zeros((NUM_FILTERS,), jnp.float32), 'fw2': xavier(ks[5], NUM_FILTERS, NUM_FILTERS), 'fb2': jnp.zeros((NUM_FILTERS,), jnp.float32), 'w1': xavier(ks[6], NUM_FILTERS, HIDDEN), 'w2': xavier(ks[7], HIDDEN, NUM_FILTERS), 'b2': jnp.zeros((HIDDEN,), jnp.float32), 'w3': xavier(ks[8], HIDDEN, HIDDEN), 'b3': jnp.zeros((HIDDEN,), jnp.float32)}
    _L0_gnn_all = _L0_gnn_setup()
    _L0_gnn_in = {k: v for k, v in _L0_gnn_all.items() if k in ('fw1', 'fb1', 'fw2', 'fb2', 'w1', 'w2', 'b2', 'w3', 'b3')}
    del _L0_gnn_all

    def _L0_ffn_setup():
        import jax, jax.numpy as jnp
        import numpy as np
        NUM_EXPERTS = 8
        TOP_K = 2
        B, S, D = (8, 256, 256)

        def _moe(tokens, router_w, w1, b1, w2, b2):
            N = tokens.shape[0]
            E = router_w.shape[0]
            logits = tokens.astype(jnp.float32) @ router_w.astype(jnp.float32).T
            probs = jax.nn.softmax(logits, axis=-1)
            rw, re = jax.lax.top_k(probs, TOP_K)
            if TOP_K > 1:
                rw = rw / jnp.maximum(rw.sum(-1, keepdims=True), 1e-12)
            rw = rw.astype(tokens.dtype)
            combine = jnp.zeros((N, E), tokens.dtype).at[jnp.arange(N)[:, None], re].set(rw)
            out = tokens
            for e in range(E):
                h = jax.nn.gelu(tokens @ w1[e] + b1[e], approximate=False)
                y = h @ w2[e] + b2[e]
                out = out + combine[:, e:e + 1] * y
            return out
        key = jax.random.key(seed)
        ks = jax.random.split(key, 4)
        scale = 1.0 / np.sqrt(D).astype(np.float32)
        return {'input_embeddings': jax.random.normal(ks[0], (B, S, D), jnp.float32), 'router_w': jax.random.normal(ks[1], (NUM_EXPERTS, D), jnp.float32) * scale, 'w1': jax.random.normal(ks[2], (NUM_EXPERTS, D, D), jnp.float32) * scale, 'b1': jnp.zeros((NUM_EXPERTS, D), jnp.float32), 'w2': jax.random.normal(ks[3], (NUM_EXPERTS, D, D), jnp.float32) * scale, 'b2': jnp.zeros((NUM_EXPERTS, D), jnp.float32)}
    _L0_ffn_all = _L0_ffn_setup()
    _L0_ffn_in = {k: v for k, v in _L0_ffn_all.items() if k in ('router_w', 'w1', 'b1', 'w2', 'b2')}
    del _L0_ffn_all

    def _L1_gnn_setup():
        import jax, jax.numpy as jnp
        import numpy as np
        N = 50000
        E = 25000
        DIM = 256
        H = 8
        DH = DIM // H
        SCALE = DH ** (-0.5)
        key = jax.random.key(seed)
        ks = jax.random.split(key, 7)
        h = jax.random.normal(ks[0], (N, DIM), dtype=jnp.float32)
        src = jax.random.randint(ks[1], (E,), 0, N, dtype=jnp.int32)
        dst = jax.random.randint(ks[2], (E,), 0, N, dtype=jnp.int32)
        W_qkv = jax.random.normal(ks[3], (DIM, 3 * DIM), dtype=jnp.float32) * DIM ** (-0.5)
        b_qkv = jnp.zeros((3 * DIM,), dtype=jnp.float32)
        W_out = jax.random.normal(ks[4], (DIM, DIM), dtype=jnp.float32) * DIM ** (-0.5)
        b_out = jnp.zeros((DIM,), dtype=jnp.float32)
        return {'h': h, 'src': src, 'dst': dst, 'W_qkv': W_qkv, 'b_qkv': b_qkv, 'W_out': W_out, 'b_out': b_out}
    _L1_gnn_all = _L1_gnn_setup()
    _L1_gnn_in = {k: v for k, v in _L1_gnn_all.items() if k in ('W_qkv', 'b_qkv', 'W_out', 'b_out')}
    del _L1_gnn_all

    def _L1_ffn_setup():
        import jax, jax.numpy as jnp
        import numpy as np
        B, S, D = (8, 128, 256)
        H = 4 * D
        CAPACITY = 0.5
        key = jax.random.key(seed)
        ks = jax.random.split(key, 6)
        x = jax.random.normal(ks[0], (B, S, D), dtype=jnp.float32)
        attention_mask = jnp.zeros((B, 1, 1, S), dtype=jnp.float32)
        wr = jax.random.normal(ks[1], (D, 1), dtype=jnp.float32) * 0.02
        br = jnp.zeros((1,), dtype=jnp.float32)
        w1 = jax.random.normal(ks[2], (D, H), dtype=jnp.float32) * 0.02
        b1 = jnp.zeros((H,), dtype=jnp.float32)
        w2 = jax.random.normal(ks[3], (H, D), dtype=jnp.float32) * 0.02
        b2 = jnp.zeros((D,), dtype=jnp.float32)
        return {'x': x, 'attention_mask': attention_mask, 'wr': wr, 'br': br, 'w1': w1, 'b1': b1, 'w2': w2, 'b2': b2}
    _L1_ffn_all = _L1_ffn_setup()
    _L1_ffn_in = {k: v for k, v in _L1_ffn_all.items() if k in ('attention_mask', 'wr', 'br', 'w1', 'b1', 'w2', 'b2')}
    del _L1_ffn_all
    return {'x': x, 'src': src, 'dst': dst, 'edge_attr_64': edge_attr_64, 'edge_weight': edge_weight, 'L0_gnn_fw1': _L0_gnn_in['fw1'], 'L0_gnn_fb1': _L0_gnn_in['fb1'], 'L0_gnn_fw2': _L0_gnn_in['fw2'], 'L0_gnn_fb2': _L0_gnn_in['fb2'], 'L0_gnn_w1': _L0_gnn_in['w1'], 'L0_gnn_w2': _L0_gnn_in['w2'], 'L0_gnn_b2': _L0_gnn_in['b2'], 'L0_gnn_w3': _L0_gnn_in['w3'], 'L0_gnn_b3': _L0_gnn_in['b3'], 'L0_ffn_router_w': _L0_ffn_in['router_w'], 'L0_ffn_w1': _L0_ffn_in['w1'], 'L0_ffn_b1': _L0_ffn_in['b1'], 'L0_ffn_w2': _L0_ffn_in['w2'], 'L0_ffn_b2': _L0_ffn_in['b2'], 'L1_gnn_W_qkv': _L1_gnn_in['W_qkv'], 'L1_gnn_b_qkv': _L1_gnn_in['b_qkv'], 'L1_gnn_W_out': _L1_gnn_in['W_out'], 'L1_gnn_b_out': _L1_gnn_in['b_out'], 'L1_ffn_attention_mask': _L1_ffn_in['attention_mask'], 'L1_ffn_wr': _L1_ffn_in['wr'], 'L1_ffn_br': _L1_ffn_in['br'], 'L1_ffn_w1': _L1_ffn_in['w1'], 'L1_ffn_b1': _L1_ffn_in['b1'], 'L1_ffn_w2': _L1_ffn_in['w2'], 'L1_ffn_b2': _L1_ffn_in['b2']}

def reference(x, src, dst, edge_attr_64, edge_weight, L0_gnn_fw1, L0_gnn_fb1, L0_gnn_fw2, L0_gnn_fb2, L0_gnn_w1, L0_gnn_w2, L0_gnn_b2, L0_gnn_w3, L0_gnn_b3, L0_ffn_router_w, L0_ffn_w1, L0_ffn_b1, L0_ffn_w2, L0_ffn_b2, L1_gnn_W_qkv, L1_gnn_b_qkv, L1_gnn_W_out, L1_gnn_b_out, L1_ffn_attention_mask, L1_ffn_wr, L1_ffn_br, L1_ffn_w1, L1_ffn_b1, L1_ffn_w2, L1_ffn_b2):
    import jax
    import jax.numpy as jnp

    def _L0_gnn_ref(x, ji_pairs, e_ji, e_ji_basis, fw1, fb1, fw2, fb2, w1, w2, b2, w3, b3):
        import jax, jax.numpy as jnp
        import numpy as np
        import math
        HIDDEN = 256
        NUM_GAUSSIANS = 64
        NUM_FILTERS = 256
        CUTOFF = 1.0
        COSINE_OFFSET = 0.0
        N_NODES = 10000
        N_EDGES = 10000

        def ssp(x):
            return jax.nn.softplus(x) - jnp.log(2.0).astype(x.dtype)
        pi = jnp.asarray(math.pi, x.dtype)
        C = 0.25 * (jnp.cos((e_ji - COSINE_OFFSET) * pi / (CUTOFF - COSINE_OFFSET)) + 1.0)
        W = ssp(e_ji_basis @ fw1.T + fb1) @ fw2.T + fb2
        W = W * C[:, None]
        h = x @ w1.T
        src, dst = (ji_pairs[0], ji_pairs[1])
        msg = h[src] * W
        agg = jax.ops.segment_sum(msg, dst, num_segments=x.shape[0])
        out = agg @ w2.T + b2
        out = ssp(out) @ w3.T + b3
        return out

    def _L0_ffn_ref(input_embeddings, router_w, w1, b1, w2, b2):
        import jax, jax.numpy as jnp
        import numpy as np
        NUM_EXPERTS = 8
        TOP_K = 2
        B, S, D = (8, 256, 256)

        def _moe(tokens, router_w, w1, b1, w2, b2):
            N = tokens.shape[0]
            E = router_w.shape[0]
            logits = tokens.astype(jnp.float32) @ router_w.astype(jnp.float32).T
            probs = jax.nn.softmax(logits, axis=-1)
            rw, re = jax.lax.top_k(probs, TOP_K)
            if TOP_K > 1:
                rw = rw / jnp.maximum(rw.sum(-1, keepdims=True), 1e-12)
            rw = rw.astype(tokens.dtype)
            combine = jnp.zeros((N, E), tokens.dtype).at[jnp.arange(N)[:, None], re].set(rw)
            out = tokens
            for e in range(E):
                h = jax.nn.gelu(tokens @ w1[e] + b1[e], approximate=False)
                y = h @ w2[e] + b2[e]
                out = out + combine[:, e:e + 1] * y
            return out
        b, s, d = input_embeddings.shape
        tokens = input_embeddings.reshape(b * s, d)
        return _moe(tokens, router_w, w1, b1, w2, b2).reshape(b, s, d)

    def _L1_gnn_ref(h, src, dst, W_qkv, b_qkv, W_out, b_out):
        import jax, jax.numpy as jnp
        import numpy as np
        N = 50000
        E = 25000
        DIM = 256
        H = 8
        DH = DIM // H
        SCALE = DH ** (-0.5)
        n = h.shape[0]
        qkv = (h @ W_qkv + b_qkv).reshape(n, 3, H, DH)
        q, k, v = (qkv[:, 0], qkv[:, 1], qkv[:, 2])
        score = jnp.einsum('ehd,ehd->eh', q[dst], k[src]) * SCALE
        mx = jax.ops.segment_max(score, dst, num_segments=n)
        ex = jnp.exp(score - mx[dst])
        denom = jax.ops.segment_sum(ex, dst, num_segments=n)
        attn = ex / denom[dst]
        msg = attn[:, :, None] * v[src]
        h_new = jax.ops.segment_sum(msg, dst, num_segments=n)
        h_out = jnp.transpose(h_new, (0, 2, 1)).reshape(n, DIM)
        return (h_out + h) @ W_out + b_out

    def _L1_ffn_ref(x, attention_mask, wr, br, w1, b1, w2, b2):
        import jax, jax.numpy as jnp
        import numpy as np
        B, S, D = (8, 128, 256)
        H = 4 * D
        CAPACITY = 0.5
        b, s, d = x.shape
        weights = (jnp.einsum('bsd,do->bso', x, wr) + br)[..., 0]
        k = max(1, int(CAPACITY * s))
        kk = k - 1 if k > 1 else 1
        _, idx = jax.lax.top_k(weights, k)
        sel_idx = idx[:, :kk]
        sel = jnp.take_along_axis(x, sel_idx[:, :, None], axis=1)
        h = jax.nn.gelu(jnp.einsum('bkd,dh->bkh', sel, w1) + b1)
        y = jnp.einsum('bkh,hd->bkd', h, w2) + b2
        w_sel = jnp.take_along_axis(weights, sel_idx, axis=1)
        y = y * w_sel[..., None]
        batch_idx = jnp.arange(b)[:, None]
        processed = jnp.zeros_like(x).at[batch_idx, sel_idx].set(y)
        return processed + x
    edge_index = jnp.stack([src, dst])
    x = x + _L0_gnn_ref(_layernorm(x, axis=-1), edge_index, edge_weight, edge_attr_64, L0_gnn_fw1, L0_gnn_fb1, L0_gnn_fw2, L0_gnn_fb2, L0_gnn_w1, L0_gnn_w2, L0_gnn_b2, L0_gnn_w3, L0_gnn_b3)
    x = x + _L0_ffn_ref(_layernorm(x, axis=-1)[None], L0_ffn_router_w, L0_ffn_w1, L0_ffn_b1, L0_ffn_w2, L0_ffn_b2)[0]
    x = x + _L1_gnn_ref(_layernorm(x, axis=-1), src, dst, L1_gnn_W_qkv, L1_gnn_b_qkv, L1_gnn_W_out, L1_gnn_b_out)
    x = x + _L1_ffn_ref(_layernorm(x, axis=-1)[None], L1_ffn_attention_mask, L1_ffn_wr, L1_ffn_br, L1_ffn_w1, L1_ffn_b1, L1_ffn_w2, L1_ffn_b2)[0]
    return x

_drawn_inputs = setup_inputs


def setup_inputs(seed=0):
    import zlib

    import numpy as np

    out = dict(_drawn_inputs(seed))
    spreads = {'L0_gnn_fb1': (0.0, 0.1),
     'L0_gnn_fb2': (0.0, 0.1),
     'L0_gnn_b2': (0.0, 0.1),
     'L0_gnn_b3': (0.0, 0.1),
     'L0_ffn_b1': (0.0, 0.316),
     'L0_ffn_b2': (0.0, 0.1),
     'L1_gnn_b_qkv': (0.0, 0.1),
     'L1_gnn_b_out': (0.0, 0.1),
     'L1_ffn_b1': (0.0, 0.8),
     'L1_ffn_b2': (0.0, 0.8)}
    factors = {'L1_ffn_wr': 6.587, 'L1_ffn_w1': 8.0, 'L1_ffn_w2': 7.474}
    for name, (base, spread) in spreads.items():
        noise = np.random.default_rng([zlib.crc32(name.encode()), seed]).standard_normal(out[name].shape)
        drawn = base * np.exp(spread * noise) if base else spread * noise
        out[name] = jnp.asarray(drawn.astype(out[name].dtype))
    for name, factor in factors.items():
        out[name] = (out[name] * factor).astype(out[name].dtype)
    return out
```

```python
from contextlib import ExitStack

import numpy as np
import concourse.bass as bass
from concourse import mybir

F32 = mybir.dt.float32
I32 = mybir.dt.int32
ALU = mybir.AluOpType
ACT = mybir.ActivationFunctionType
AX = mybir.AxisListType

P = 128
N, D, E = 3125, 256, 50000
KC = D // P
NW = -(-N // P)
NP = NW * P
GT = 5
NG = NW // GT
GN = GT * P
HALF = GN // 2
NT = 392
EP = NT * P
NI = NT + NW - 1
RT, RC = 98, 4
GA = 64
IG = 4
NIG = NI // IG
H, DH = 8, 32
SCALE = DH ** -0.5
CH = 16
CI = NI // CH
CE = CI * P
BIG = 3.0e38
LN2 = float(np.log(np.float32(2.0)))
EPS = 1e-5
NEXP = 8
TOPK = 2
HF = 4 * D
KEEP = N // 2 - 1
SP_CAP = 80.0
assert NW % GT == 0 and RT * RC == NT and NI % (2 * IG) == 0 and NI % CH == 0 and EP >= E + 1


class Core:

    def __init__(self, nc):
        self.nc = nc
        self.keep = ExitStack()
        self.gates = {}

    def sb(self, name, shape, dt=F32, scope=None):
        return (scope or self.keep).enter_context(self.nc.sbuf_tensor(name, shape, dt))

    def ps(self, name, shape, dt=F32, scope=None):
        return (scope or self.keep).enter_context(self.nc.psum_tensor(name, shape, dt))

    def sem(self, name):
        kind = name.rsplit("_", 1)[-1]
        if not kind.endswith("gate"):
            return self.keep.enter_context(self.nc.semaphore(name))
        if kind not in self.gates:
            self.gates[kind] = self.keep.enter_context(self.nc.semaphore(kind))
        return self.gates[kind]


class Chain:

    def __init__(self, eng, sem):
        self.eng, self.sem, self.n = eng, sem, 0

    def __call__(self, ins):
        self.n += 1
        ins.then_inc(self.sem, 1)
        self.eng.wait_ge(self.sem, self.n)


def alone(eng, gate, *waits):
    for sem, value in waits:
        eng.wait_ge(sem, value)
    eng.sem_inc(gate, 1)


def bcast_rows(ap, parts):
    n = ap.shape[-1]
    return ap.rearrange("(a n) -> a n", a=1).broadcast_to([parts, n]) if len(ap.shape) == 1 else ap.broadcast_to([parts, n])


def prepare(c, A):
    nc = c.nc
    c.ident = c.sb("ident", [P, P])
    c.iota_n = c.sb("iota_n", [P, P])
    c.src_i = c.sb("src_i", [P, NI], I32)
    c.dst_rel = c.sb("dst_rel", [P, NI])
    c.coef = c.sb("coef", [P, NI])
    c.node_id = c.sb("node_id", [P, NI])
    c.seg_id = c.sb("seg_id", [P, NI])
    c.t_row = c.sb("t_row", [1, NI], I32)
    c.w_row = c.sb("w_row", [1, NI], I32)
    with ExitStack() as s:
        rows_i = c.sb("rows_i", [RT, 2, RC, P], I32, s)
        rows_f = c.sb("rows_f", [RT, 3, RC, P], F32, s)
        whi = c.sb("whi", [RT, RC], I32, s)
        key = c.sb("key", [RT, RC], F32, s)
        tcol = c.sb("tcol", [RT, RC], F32, s)
        iota_i = c.sb("iota_i", [P, NI], F32, s)
        part = c.sb("part", [P, 1], F32, s)
        after = c.sb("after", [RT, RC, NI], F32, s)
        pick = c.sb("pick", [RT, RC, NI], F32, s)
        ones = c.sb("prep_ones", [RT, P], F32, s)
        t_all = c.sb("t_all", [P, NI], F32, s)
        w_all = c.sb("w_all", [P, NI], F32, s)
        w128 = c.sb("w128", [P, NI], F32, s)
        cols = c.sb("prep_cols", [P, 3, NI], F32, s)
        tmp = c.sb("prep_tmp", [P, NI], F32, s)
        tmp2 = c.sb("prep_tmp2", [P, NI], F32, s)
        period = c.sb("period", [P, NI], F32, s)
        whole = c.sb("whole", [P, NI], I32, s)
        sine = c.sb("sine", [P, NI], F32, s)
        p_t = c.ps("prep_t", [P, 512], F32, s)
        p_c = c.ps("prep_c", [P, 3, 512], F32, s)
        s_in, s_io = c.sem("prep_loaded"), c.sem("prep_iotas")
        s_d, s_a = c.sem("prep_chain"), c.sem("prep_after")
        s_t, s_pick, s_c = c.sem("prep_tiles"), c.sem("prep_picked"), c.sem("prep_columns")
        s_m, s_sin = c.sem("prep_phase"), c.sem("prep_sine")
        with nc.Block() as block:
            @block.sync
            def _(sp):
                sp.dma_start(rows_i[:, 0], A["src"].rearrange("(c p) e -> p c e", p=RT)).then_inc(s_in, 16)
                sp.dma_start(rows_i[:, 1], A["dst"].rearrange("(c p) e -> p c e", p=RT)).then_inc(s_in, 16)
                sp.dma_start(rows_f[:, 2], A["edge_weight"].rearrange("(c p) e -> p c e", p=RT)).then_inc(s_in, 16)

            @block.gpsimd
            def _(pool):
                pool.memset(c.ident[:, :], 0.0).then_inc(s_io, 1)
                pool.iota(iota_i[:, :], pattern=[[1, NI]], base=0, channel_multiplier=0, allow_small_or_imprecise_dtypes=True).then_inc(s_io, 1)
                pool.iota(c.iota_n[:, :], pattern=[[1, P]], base=0, channel_multiplier=0, allow_small_or_imprecise_dtypes=True).then_inc(s_io, 1)
                pool.iota(tcol[:, :], pattern=[[RT, RC]], base=0, channel_multiplier=1, allow_small_or_imprecise_dtypes=True).then_inc(s_io, 1)
                pool.iota(part[:, :], pattern=[[1, 1]], base=0, channel_multiplier=1, allow_small_or_imprecise_dtypes=True).then_inc(s_io, 1)
                pool.memset(ones[:, :], 1.0).then_inc(s_io, 1)
                pool.wait_ge(s_io, 6)
                pool.affine_select(out=c.ident[:, :], in_=c.ident[:, :], compare_op=ALU.not_equal, fill=1.0,
                                   base=0, pattern=[[-1, P]], channel_multiplier=1).then_inc(s_io, 1)

            @block.vector
            def _(dve):
                link = Chain(dve, s_d)
                v = nc.vector
                dve.wait_ge(s_in, 48)
                dve.wait_ge(s_io, 7)
                link(v.tensor_scalar(whi[:, :], rows_i[:, 1, :, P - 1], 7, None, ALU.logical_shift_right))
                link(v.tensor_copy(rows_f[:, 0:2], rows_i[:, :]))
                link(v.tensor_tensor(key[:, :], whi[:, :], tcol[:, :], ALU.add))
                for k in range(RC):
                    v.tensor_scalar(after[:, k, :], iota_i[0:RT, :], key[:, k:k + 1], None, ALU.is_gt).then_inc(s_a, 1)
                dve.wait_ge(s_t, 1)
                link(v.tensor_copy(t_all[:, :], p_t[:, 0:NI]))
                link(v.tensor_tensor(w_all[:, :], iota_i[:, :], t_all[:, :], ALU.subtract))
                link(v.tensor_scalar(w_all[:, :], w_all[:, :], 0.0, float(NW - 1), ALU.max, ALU.min))
                v.tensor_copy(c.t_row[:, :], t_all[0:1, :]).then_inc(s_pick, 1)
                v.tensor_copy(c.w_row[:, :], w_all[0:1, :]).then_inc(s_pick, 1)
                for k in range(RC):
                    v.tensor_scalar(pick[:, k, :], t_all[0:RT, :], tcol[:, k:k + 1], None, ALU.is_equal).then_inc(s_pick, 1)
                link(v.tensor_scalar(w128[:, :], w_all[:, :], float(P), None, ALU.mult))
                link(v.tensor_scalar(c.node_id[:, :], w128[:, :], part[:, 0:1], None, ALU.add))
                dve.wait_ge(s_c, 3)
                link(v.tensor_copy(cols[:, :, :], p_c[:, :, 0:NI]))
                link(v.tensor_scalar(period[:, :], cols[:, 2, :], 0.5, None, ALU.mult))
                link(v.tensor_copy(whole[:, :], period[:, :]))
                v.tensor_tensor(period[:, :], period[:, :], whole[:, :], ALU.subtract).then_inc(s_m, 1)
                link(v.tensor_copy(c.src_i[:, :], cols[:, 0, :]))
                link(v.tensor_tensor(c.dst_rel[:, :], cols[:, 1, :], w128[:, :], ALU.subtract))
                link(v.tensor_scalar(tmp[:, :], c.dst_rel[:, :], 0.0, None, ALU.is_ge))
                link(v.tensor_scalar(tmp2[:, :], c.dst_rel[:, :], float(P), None, ALU.is_lt))
                link(v.tensor_tensor(tmp[:, :], tmp[:, :], tmp2[:, :], ALU.mult))
                link(v.tensor_scalar(tmp2[:, :], cols[:, 1, :], 1.0, None, ALU.add))
                link(v.tensor_tensor(c.seg_id[:, :], tmp[:, :], tmp2[:, :], ALU.mult))
                dve.wait_ge(s_sin, 1)
                link(v.tensor_tensor(tmp[:, :], sine[:, :], sine[:, :], ALU.mult))
                link(v.tensor_scalar(c.coef[:, :], tmp[:, :], -0.5, 0.5, ALU.mult, ALU.add))

            @block.scalar
            def _(act):
                act.wait_ge(s_m, 1)
                nc.scalar.activation(sine[:, :], period[:, :], ACT.Sin, scale=float(np.pi)).then_inc(s_sin, 1)

            @block.tensor
            def _(pe):
                pe.wait_ge(s_io, 7)
                for k in range(RC):
                    pe.wait_ge(s_a, k + 1)
                    last = nc.tensor.matmul(p_t[:, 0:NI], ones[:, :], after[:, k, :], start=(k == 0), stop=(k == RC - 1))
                last.then_inc(s_t, 1)
                pe.wait_ge(s_pick, 2 + RC)
                for a in range(3):
                    for k in range(RC):
                        last = nc.tensor.matmul(p_c[:, a, 0:NI], rows_f[:, a, k, :], pick[:, k, :], start=(k == 0), stop=(k == RC - 1))
                    last.then_inc(s_c, 1)


class Norm:

    def __init__(self, c, name, scope):
        self.c = c
        self.stat = c.sb(f"{name}_stat", [P, NW, 6], F32, scope)
        self.mv = c.sb(f"{name}_mv", [P, NW, 2], F32, scope)
        self.var = c.sb(f"{name}_var", [P, NW], F32, scope)
        self.rstd = c.sb(f"{name}_rstd", [P, NW], F32, scope)
        self.s_stat, self.s_inv, self.s_rstd = c.sem(f"{name}_stats"), c.sem(f"{name}_inv"), c.sem(f"{name}_rstd")
        self.s_gate, self.s_xn = c.sem(f"{name}_gate"), c.sem(f"{name}_normed")

    def moments(self, dve):
        v = self.c.nc.vector
        with dve.Fori(0, NW) as t:
            v.bn_stats(self.stat[:, bass.ds(t, 1), :].rearrange("p a d -> p (a d)"), window(self.c.x, t)).then_inc(self.s_stat, 1)
        dve.wait_ge(self.s_stat, NW)
        for t in range(NW):
            last = v.bn_aggr(self.mv[:, t, :], self.stat[:, t, :])
        last.then_inc(self.s_stat, 1)
        dve.wait_ge(self.s_stat, NW + 1)
        v.tensor_scalar(self.var[:, :], self.mv[:, :, 1], EPS, None, ALU.add).then_inc(self.s_stat, 1)
        dve.wait_ge(self.s_stat, NW + 2)
        v.reciprocal(self.var[:, :], self.var[:, :]).then_inc(self.s_inv, 1)

    def root(self, act):
        act.wait_ge(self.s_inv, 1)
        self.c.nc.scalar.activation(self.rstd[:, :], self.var[:, :], ACT.Sqrt).then_inc(self.s_rstd, 1)

    def apply(self, dve, g, out, *after):
        alone(dve, self.s_gate, *after)
        for j in range(GT):
            last = self.c.nc.vector.tensor_scalar(
                out(j), window(self.c.x, g * GT + j), self.mv[:, bass.ds(g * GT + j, 1), 0:1].rearrange("p a b -> p (a b)"),
                self.rstd[:, bass.ds(g * GT + j, 1)], ALU.subtract, ALU.mult)
        last.then_inc(self.s_xn, 1)


def window(t, n):
    return t[:, bass.ds(n, 1), :].rearrange("p a d -> p (a d)")


def transpose_group(nc, tp, src, ident):
    for k in range(KC):
        for j in range(GT):
            at = (k * GT + j) * P
            last = nc.tensor.transpose(tp[:, at:at + P], src(j, k), ident[:, :])
    return last


def source_features(c, A):
    nc = c.nc
    with ExitStack() as s:
        nrm = Norm(c, "n0", s)
        xn = c.sb("n0_xn", [P, GT, D], F32, s)
        xT = c.sb("n0_xT", [P, KC * GN], F32, s)
        w = c.sb("n0_w", [P, KC, D], F32, s)
        ho = c.sb("n0_h", [P, GT, D], F32, s)
        tp = c.ps("n0_tp", [P, 3 * 512], F32, s)
        hp = c.ps("n0_hp", [P, 3 * 512], F32, s)
        s_x = [c.sem(f"n0_x{g}") for g in range(NG)]
        s_w, s_t, s_xT, s_h, s_ho, s_st = (c.sem("n0_" + n) for n in ("weights", "transposed", "xT", "h", "hout", "stored"))
        s_gate = c.sem("n0_agate")
        with nc.Block() as block:
            @block.sync
            def _(sp):
                sp.dma_start(w[:, :, :], A["g_w1T"].rearrange("(k p) n -> p k n", p=P)).then_inc(s_w, 16)
                for g in range(NG):
                    sp.dma_start(c.x[:, g * GT:(g + 1) * GT, :], A["x"].rearrange("(t p) d -> p t d", p=P)[:, g * GT:(g + 1) * GT, :]).then_inc(s_x[g], 16)
                for g in range(NG):
                    sp.wait_ge(s_ho, g + 1)
                    sp.dma_start(c.h_dram.rearrange("(t p) d -> p t d", p=P)[:, g * GT:(g + 1) * GT, :], ho[:, :, :]).then_inc(s_st, 16)
                sp.wait_ge(s_st, 16 * NG)

            @block.vector
            def _(dve):
                for g in range(NG):
                    dve.wait_ge(s_x[g], 16)
                nrm.moments(dve)
                dve.wait_ge(nrm.s_rstd, 1)
                with dve.Fori(0, NG) as g:
                    nrm.apply(dve, g, lambda j: xn[:, j, :], (s_t, g))

            @block.tensor
            def _(pe):
                pe.wait_ge(s_w, 16)
                with pe.Fori(0, NG) as g:
                    alone(pe, s_gate, (nrm.s_xn, g + 1), (s_xT, g))
                    transpose_group(nc, tp, lambda j, k: xn[:, j, k * P:(k + 1) * P], c.ident).then_inc(s_t, 1)
                    alone(pe, s_gate, (s_xT, g + 1), (s_ho, g))
                    for j in range(GT):
                        for k in range(KC):
                            last = nc.tensor.matmul(hp[:, j * D:(j + 1) * D], xT[:, k * GN + j * P:k * GN + (j + 1) * P], w[:, k, :],
                                                    start=(k == 0), stop=(k == KC - 1))
                    last.then_inc(s_h, 1)

            @block.scalar
            def _(act):
                nrm.root(act)
                with act.Fori(0, NG) as g:
                    alone(act, s_gate, (s_t, g + 1), (s_h, g))
                    nc.scalar.copy(xT[:, :], tp[:, 0:KC * GN]).then_inc(s_xT, 1)
                    alone(act, s_gate, (s_h, g + 1), (s_st, 16 * g))
                    nc.scalar.copy(ho[:, :, :].rearrange("p t d -> p (t d)"), hp[:, 0:GT * D]).then_inc(s_ho, 1)


def edges_first(c, A):
    nc = c.nc
    with ExitStack() as s:
        fw1 = c.sb("e1_fw1", [GA + 1, D], F32, s)
        fw2 = c.sb("e1_fw2", [P, KC, D], F32, s)
        bias = c.sb("e1_bias", [P, D], F32, s)
        mln2 = c.sb("e1_mln2", [P, P], F32, s)
        ea = c.sb("e1_ea", [GA + 1, 2, IG * P], F32, s)
        soft = c.sb("e1_soft", [P, 2, KC * IG * P], F32, s)
        hid = c.sb("e1_hid", [P, 2, KC * IG * P], F32, s)
        idx = c.sb("e1_idx", [P, 2, IG], I32, s)
        rows = c.sb("e1_rows", [P, 2, IG, D], F32, s)
        msg = c.sb("e1_msg", [P, 2, IG, D], F32, s)
        hot = c.sb("e1_hot", [P, 2, IG, P], F32, s)
        zp = [c.ps(f"e1_z{p}", [P, KC * IG * P], F32, s) for p in range(2)]
        wp = c.ps("e1_w", [P, IG * D], F32, s)
        ap = c.ps("e1_agg", [P, IG * D], F32, s)
        s_ld, s_b, s_bd, s_cst = (c.sem("e1_" + n) for n in ("loaded", "biassum", "biasready", "constants"))
        s_ea = [c.sem(f"e1_ea{p}") for p in range(2)]
        s_rows = [c.sem(f"e1_rows{p}") for p in range(2)]
        s_idx, s_gate, s_ggate = c.sem("e1_idx"), c.sem("e1_gate"), c.sem("e1_poolgate")
        s_z, s_exp, s_ln, s_hid = (c.sem("e1_" + n) for n in ("z", "exp", "ln", "hid"))
        s_hot, s_w, s_wb, s_msg, s_agg, s_acc = (c.sem("e1_" + n) for n in ("hot", "w", "wbias", "msg", "agg", "acc"))
        with nc.Block() as block:
            @block.sync
            def _(sp):
                sp.dma_start(fw1[:, :], A["g_fw1T"]).then_inc(s_ld, 16)
                sp.dma_start(fw2[:, :, :], A["g_fw2T"].rearrange("(k p) n -> p k n", p=P)).then_inc(s_ld, 16)
                sp.dma_start(bias[:, :], bcast_rows(A["g_fb2"], P)).then_inc(s_ld, 16)

                def load(g, p):
                    tiles = [sp.value_load(c.t_row[0:1, bass.ds(g * IG + j, 1)], min_val=0, max_val=NT - 1) for j in range(IG)]
                    if isinstance(g, int):
                        if g >= 2:
                            sp.wait_ge(s_z, g - 1)
                    else:
                        sp.wait_ge(s_z, g - 1)
                    for j in range(IG):
                        sp.dma_start(ea[0:GA, p, j * P:(j + 1) * P], A["eaT"][:, bass.ds(tiles[j] * P, P)]).then_inc(s_ea[p], 16)
                load(0, 0)
                load(1, 1)
                with sp.Fori(0, NIG // 2 - 1) as it:
                    for q in (2, 3):
                        load(it * 2 + q, q % 2)

            @block.gpsimd
            def _(pool):
                nc.gpsimd.memset(mln2[:, :], -LN2).then_inc(s_cst, 1)
                pool.wait_ge(s_cst, 1)
                nc.gpsimd.memset(ea[GA:GA + 1, :, :], 1.0).then_inc(s_cst, 1)
                pool.wait_ge(s_cst, 2)
                nc.gpsimd.memset(c.agg[:, :, 0:D], 0.0).then_inc(s_cst, 1)

                def gather(it, p):
                    g = it * 2 + p
                    alone(pool, s_ggate, (s_msg, it * 2 + p - 1) if not isinstance(it, int) else (s_cst, 3), (s_rows[p], it * 64))
                    nc.gpsimd.tensor_copy(idx[:, p, :], c.src_i[:, bass.ds(g * IG, IG)]).then_inc(s_idx, 1)
                    alone(pool, s_ggate, (s_idx, g + 1))
                    for j in range(IG):
                        nc.gpsimd.indirect_dma_start(out=rows[:, p, j, :], out_offset=None, in_=c.h_dram,
                                                     in_offset=bass.IndirectOffsetOnAxis(ap=idx[:, p, j:j + 1], axis=0)).then_inc(s_rows[p], 16)
                gather(0, 0)
                gather(0, 1)
                with pool.Fori(1, NIG // 2) as it:
                    for p in range(2):
                        gather(it, p)

            @block.tensor
            def _(pe):
                pe.wait_ge(s_ld, 48)
                pe.wait_ge(s_cst, 3)
                for k in range(KC):
                    last = nc.tensor.matmul(wp[:, 0:D], mln2[:, :], fw2[:, k, :], start=(k == 0), stop=(k == KC - 1))
                last.then_inc(s_b, 1)
                pe.wait_ge(s_bd, 1)

                def first_layer(g, it, p, steady=True):
                    pe.wait_ge(s_ea[p], (it + 1) * 64)
                    if steady:
                        pe.wait_ge(s_hid, g - 1)
                    for m in range(KC):
                        last = nc.tensor.matmul(zp[p][:, m * IG * P:(m + 1) * IG * P], fw1[:, m * P:(m + 1) * P], ea[:, p, :], start=True, stop=True)
                    last.then_inc(s_z, 1)

                def second_layer(g, p):
                    pe.wait_ge(s_hid, g + 1)
                    pe.wait_ge(s_wb, g)
                    for j in range(IG):
                        for k in range(KC):
                            at = (k * IG + j) * P
                            last = nc.tensor.matmul(wp[:, j * D:(j + 1) * D], hid[:, p, at:at + P], fw2[:, k, :], start=(k == 0), stop=(k == KC - 1))
                    last.then_inc(s_w, 1)

                def aggregate(g, p):
                    pe.wait_ge(s_msg, g + 1)
                    pe.wait_ge(s_acc, g * IG)
                    for j in range(IG):
                        last = nc.tensor.matmul(ap[:, j * D:(j + 1) * D], hot[:, p, j, :], msg[:, p, j, :], start=True, stop=True)
                    last.then_inc(s_agg, 1)
                first_layer(0, 0, 0, False)
                first_layer(1, 0, 1, False)
                second_layer(0, 0)
                with pe.Fori(0, NIG // 2 - 1) as it:
                    for q in (0, 1):
                        first_layer(it * 2 + q + 2, it + 1, q)
                        second_layer(it * 2 + q + 1, (q + 1) % 2)
                        aggregate(it * 2 + q, q)
                second_layer(NIG - 1, 1)
                aggregate(NIG - 2, 0)
                aggregate(NIG - 1, 1)

            @block.scalar
            def _(act):
                with act.Fori(0, NIG // 2) as it:
                    for p in range(2):
                        g = it * 2 + p
                        alone(act, s_gate, (s_z, g + 1))
                        nc.scalar.activation(soft[:, p, :], zp[p][:, :], ACT.Exp).then_inc(s_exp, 1)
                        alone(act, s_gate, (s_exp, g + 1))
                        nc.scalar.activation(soft[:, p, :], soft[:, p, :], ACT.Ln, bias=1.0).then_inc(s_ln, 1)

            @block.vector
            def _(dve):
                v = nc.vector
                dve.wait_ge(s_b, 1)
                dve.wait_ge(s_ld, 48)
                v.tensor_tensor(bias[:, :], bias[:, :], wp[:, 0:D], ALU.add).then_inc(s_bd, 1)
                dve.wait_ge(s_bd, 1)
                bias_b = bias[:, :].rearrange("p (a d) -> p a d", a=1).broadcast_to([P, IG, D])

                def softplus(g, p, steady=True):
                    dve.wait_ge(s_ln, g + 1)
                    if steady:
                        dve.wait_ge(s_w, g - 1)
                    v.scalar_tensor_tensor(hid[:, p, :], soft[:, p, :], SP_CAP, zp[p][:, :], ALU.min, ALU.max).then_inc(s_hid, 1)

                def one_hot(g, p, steady=True):
                    if steady:
                        alone(dve, s_gate, (s_agg, g - 1))
                    for j in range(IG):
                        i = g * IG + j
                        v.tensor_scalar(hot[:, p, j, :], c.iota_n[:, :], c.dst_rel[:, bass.ds(i, 1)], c.coef[:, bass.ds(i, 1)],
                                        ALU.is_equal, ALU.mult)

                def messages(g, it, p):
                    dve.wait_ge(s_w, g + 1)
                    v.tensor_tensor(msg[:, p, :, :], wp[:, :].rearrange("p (a d) -> p a d", a=IG), bias_b, ALU.add).then_inc(s_wb, 1)
                    dve.wait_ge(s_wb, g + 1)
                    dve.wait_ge(s_rows[p], (it + 1) * 64)
                    v.tensor_tensor(msg[:, p, :, :], msg[:, p, :, :], rows[:, p, :, :], ALU.mult).then_inc(s_msg, 1)

                def accumulate(g):
                    wins = [dve.value_load(c.w_row[0:1, bass.ds(g * IG + j, 1)], min_val=0, max_val=NW - 1) for j in range(IG)]
                    dve.wait_ge(s_agg, g + 1)
                    for j in range(IG):
                        to = c.agg[:, bass.ds(wins[j], 1), 0:D].rearrange("p a d -> p (a d)")
                        alone(dve, s_gate, (s_acc, g * IG + j))
                        v.tensor_tensor(to, to, ap[:, j * D:(j + 1) * D], ALU.add).then_inc(s_acc, 1)
                softplus(0, 0, False)
                one_hot(0, 0, False)
                softplus(1, 1, False)
                one_hot(1, 1, False)
                messages(0, 0, 0)
                with dve.Fori(0, NIG // 2 - 1) as it:
                    for q in (0, 1):
                        softplus(it * 2 + q + 2, q)
                        messages(it * 2 + q + 1, it + q, (q + 1) % 2)
                        accumulate(it * 2 + q)
                        one_hot(it * 2 + q + 2, q)
                messages(NIG - 1, NIG // 2 - 1, 1)
                accumulate(NIG - 2)
                accumulate(NIG - 1)


def nodes_first(c, A):
    nc = c.nc
    with ExitStack() as s:
        w2 = c.sb("u_w2", [P, KC, D], F32, s)
        w3 = c.sb("u_w3", [P, KC, D], F32, s)
        b2 = c.sb("u_b2", [P, KC], F32, s)
        b3 = c.sb("u_b3", [P, D], F32, s)
        ag = c.sb("u_agg", [P, GT, D], F32, s)
        aT = c.sb("u_aggT", [P, KC * GN], F32, s)
        z = c.sb("u_z", [P, KC, 2, HALF], F32, s)
        soft = c.sb("u_soft", [P, KC, 2, HALF], F32, s)
        hid = c.sb("u_hid", [P, KC * GN], F32, s)
        to = c.ps("u_to", [P, 3 * 512], F32, s)
        zp = c.ps("u_zp", [P, KC, 2, 512], F32, s)
        names = ("loaded", "agg", "transposed", "aggT", "z", "zbias", "exp", "ln", "max", "hid", "rows", "sum", "x", "dgate", "agate", "pgate")
        s_ld, s_ag, s_t, s_aT, s_z, s_zb, s_e, s_ln, s_mx, s_hid, s_r, s_s, s_x, s_dg, s_agt, s_pg = (c.sem("u_" + n) for n in names)
        with nc.Block() as block:
            @block.sync
            def _(sp):
                sp.dma_start(w2[:, :, :], A["g_w2T"].rearrange("(k p) n -> p k n", p=P)).then_inc(s_ld, 16)
                sp.dma_start(w3[:, :, :], A["g_w3T"].rearrange("(k p) n -> p k n", p=P)).then_inc(s_ld, 16)
                sp.dma_start(b2[:, :], A["g_b2"]).then_inc(s_ld, 16)
                sp.dma_start(b3[:, :], bcast_rows(A["g_b3"], P)).then_inc(s_ld, 16)

            @block.gpsimd
            def _(pool):
                with pool.Fori(0, NG) as g:
                    alone(pool, s_pg, (s_t, g))
                    nc.gpsimd.tensor_copy(ag[:, :, :], c.agg[:, bass.ds(g * GT, GT), 0:D]).then_inc(s_ag, 1)

            @block.tensor
            def _(pe):
                pe.wait_ge(s_ld, 64)
                with pe.Fori(0, NG) as g:
                    pe.wait_ge(s_ag, g + 1)
                    pe.wait_ge(s_s, g)
                    transpose_group(nc, to, lambda j, k: ag[:, j, k * P:(k + 1) * P], c.ident).then_inc(s_t, 1)
                    pe.wait_ge(s_aT, g + 1)
                    for m in range(KC):
                        for h in range(2):
                            for k in range(KC):
                                last = nc.tensor.matmul(zp[:, m, h, 0:HALF], w2[:, k, m * P:(m + 1) * P],
                                                        aT[:, k * GN + h * HALF:k * GN + (h + 1) * HALF], start=(k == 0), stop=(k == KC - 1))
                    last.then_inc(s_z, 1)
                    pe.wait_ge(s_hid, g + 1)
                    for j in range(GT):
                        for k in range(KC):
                            last = nc.tensor.matmul(to[:, j * D:(j + 1) * D], hid[:, k * GN + j * P:k * GN + (j + 1) * P], w3[:, k, :],
                                                    start=(k == 0), stop=(k == KC - 1))
                    last.then_inc(s_r, 1)

            @block.scalar
            def _(act):
                with act.Fori(0, NG) as g:
                    alone(act, s_agt, (s_t, g + 1), (s_z, g))
                    nc.scalar.copy(aT[:, :], to[:, 0:KC * GN]).then_inc(s_aT, 1)
                    alone(act, s_agt, (s_zb, g + 1), (s_mx, g))
                    nc.scalar.activation(soft[:, :, :, :], z[:, :, :, :], ACT.Exp).then_inc(s_e, 1)
                    alone(act, s_agt, (s_e, g + 1))
                    nc.scalar.activation(soft[:, :, :, :], soft[:, :, :, :], ACT.Ln, bias=1.0).then_inc(s_ln, 1)

            @block.vector
            def _(dve):
                v = nc.vector
                dve.wait_ge(s_ld, 64)
                b3_b = b3[:, :].rearrange("p (a d) -> p a d", a=1).broadcast_to([P, GT, D])
                with dve.Fori(0, NG) as g:
                    dve.wait_ge(s_z, g + 1)
                    for m in range(KC):
                        last = v.tensor_scalar(z[:, m], zp[:, m, :, 0:HALF], b2[:, m:m + 1], None, ALU.add)
                    last.then_inc(s_zb, 1)
                    alone(dve, s_dg, (s_ln, g + 1), (s_zb, g + 1), (s_r, g))
                    v.scalar_tensor_tensor(z[:, :, :, :], soft[:, :, :, :], SP_CAP, z[:, :, :, :], ALU.min, ALU.max).then_inc(s_mx, 1)
                    dve.wait_ge(s_mx, g + 1)
                    v.tensor_scalar(hid[:, :], z[:, :, :, :].rearrange("p m h n -> p (m h n)"), -LN2, None, ALU.add).then_inc(s_hid, 1)
                    xg = c.x[:, bass.ds(g * GT, GT), :]
                    v.tensor_tensor(xg, xg, b3_b, ALU.add).then_inc(s_x, 1)
                    alone(dve, s_dg, (s_r, g + 1), (s_x, g + 1))
                    v.tensor_tensor(xg, xg, to[:, 0:GT * D].rearrange("p (t d) -> p t d", t=GT), ALU.add).then_inc(s_s, 1)


def experts(c, A, routed):
    nc = c.nc
    name = "m_" if routed else "f_"
    NB = NEXP if routed else HF // D
    gelu = ACT.Gelu if routed else ACT.Gelu_apprx_tanh
    with ExitStack() as s:
        w1 = c.sb(name + "w1", [P, NB, KC, D], F32, s)
        w2 = c.sb(name + "w2", [P, NB, KC, D], F32, s)
        b1 = c.sb(name + "b1", [P, NB * KC], F32, s)
        acc = c.sb(name + "acc", [P, GT, D], F32, s)
        tok = c.sb(name + "tok", [P, GT, D], F32, s)
        xT = c.sb(name + "xT", [P, KC * GN], F32, s)
        hid = c.sb(name + "hid", [P, 2, KC * GN], F32, s)
        comb = c.sb(name + "comb", [P, GT, NEXP], F32, s)
        hp = c.ps(name + "hp", [P, KC, 2, 512], F32, s)
        yp = c.ps(name + "yp", [P, 3 * 512], F32, s)
        sems = lambda *ns: (c.sem(name + n) for n in ns)
        s_ld, s_cst, s_d, s_t, s_xT, s_h, s_hid, s_y, s_acc, s_x, s_dg, s_ag = sems(
            "loaded", "const", "chain", "transposed", "xT", "h", "hid", "y", "acc", "x", "dgate", "agate")
        if routed:
            nrm = Norm(c, "n1", s)
            s_tok = nrm.s_xn
            b2 = c.sb(name + "b2", [NEXP, D], F32, s)
            rw = c.sb(name + "rw", [P, KC, NEXP], F32, s)
            lower = c.sb(name + "lower", [P, NEXP, NEXP], F32, s)
            lg = c.sb(name + "lg", [P, GT, NEXP], F32, s)
            pr = c.sb(name + "pr", [P, GT, NEXP], F32, s)
            top = c.sb(name + "top", [P, GT], F32, s)
            gt = c.sb(name + "gt", [P, GT, NEXP, NEXP], F32, s)
            eq = c.sb(name + "eq", [P, GT, NEXP, NEXP], F32, s)
            combT = c.sb(name + "combT", [NEXP, GN], F32, s)
            lp = c.ps(name + "lp", [P, GT * NEXP], F32, s)
            s_lg, s_sub, s_exp, s_comb, s_cT, s_ct, s_b2 = sems("logits", "sub", "exp", "comb", "combT", "combt", "b2")
        else:
            s_tok = c.sem(name + "tok")
            b2 = c.sb(name + "b2", [P, D], F32, s)
        n_ld = 3 + NB * 2 * 1 + (1 if routed else 0)
        rounds = NB + (1 if routed else 0)
        with nc.Block() as block:
            @block.sync
            def _(sp):
                if routed:
                    for e in range(NB):
                        sp.dma_start(w1[:, e], A["m_w1"][e].rearrange("(k p) n -> p k n", p=P)).then_inc(s_ld, 16)
                        sp.dma_start(w2[:, e], A["m_w2"][e].rearrange("(k p) n -> p k n", p=P)).then_inc(s_ld, 16)
                    sp.dma_start(b2[:, :], A["m_b2"]).then_inc(s_ld, 16)
                    sp.dma_start(rw[:, :, :], A["r_wT"].rearrange("(k p) n -> p k n", p=P)).then_inc(s_ld, 16)
                    sp.dma_start(b1[:, :], A["m_b1"]).then_inc(s_ld, 16)
                    sp.wait_ge(s_ld, 16 * (2 * NB + 3))
                else:
                    for e in range(NB):
                        sp.dma_start(w1[:, e], A["f_w1"][:, e * D:(e + 1) * D].rearrange("(k p) n -> p k n", p=P)).then_inc(s_ld, 16)
                        sp.dma_start(w2[:, e], A["f_w2"][e * D:(e + 1) * D, :].rearrange("(k p) n -> p k n", p=P)).then_inc(s_ld, 16)
                    sp.dma_start(b2[:, :], bcast_rows(A["f_b2"], P)).then_inc(s_ld, 16)
                    sp.dma_start(b1[:, :], A["f_b1"]).then_inc(s_ld, 16)
                    sp.wait_ge(s_ld, 16 * (2 * NB + 2))

            loaded = 16 * (2 * NB + (3 if routed else 2))

            @block.gpsimd
            def _(pool):
                if routed:
                    pool.iota(lower[:, :, :], pattern=[[-1, NEXP], [1, NEXP]], base=0, channel_multiplier=0,
                              allow_small_or_imprecise_dtypes=True).then_inc(s_cst, 1)

            @block.tensor
            def _(pe):
                pe.wait_ge(s_ld, loaded)
                with pe.Fori(0, NG) as g:
                    pe.wait_ge(s_tok, g + 1)
                    pe.wait_ge(s_acc, g * rounds)
                    transpose_group(nc, yp, lambda j, k: tok[:, j, k * P:(k + 1) * P], c.ident).then_inc(s_t, 1)
                    pe.wait_ge(s_xT, g + 1)

                    def up(e):
                        pe.wait_ge(s_hid, g * NB + e)
                        for m in range(KC):
                            for h in range(2):
                                for k in range(KC):
                                    last = nc.tensor.matmul(hp[:, m, h, 0:HALF], w1[:, e, k, m * P:(m + 1) * P],
                                                            xT[:, k * GN + h * HALF:k * GN + (h + 1) * HALF], start=(k == 0), stop=(k == KC - 1))
                        last.then_inc(s_h, 1)

                    def down(e):
                        pe.wait_ge(s_hid, g * NB + e + 1)
                        pe.wait_ge(s_acc, g * rounds + rounds - NB + e)
                        for j in range(GT):
                            for k in range(KC):
                                last = nc.tensor.matmul(yp[:, j * D:(j + 1) * D], hid[:, e % 2, k * GN + j * P:k * GN + (j + 1) * P], w2[:, e, k, :],
                                                        start=(k == 0), stop=(k == KC - 1))
                        last.then_inc(s_y, 1)
                    if routed:
                        pe.wait_ge(s_sub, g)
                        for j in range(GT):
                            for k in range(KC):
                                last = nc.tensor.matmul(lp[:, j * NEXP:(j + 1) * NEXP], xT[:, k * GN + j * P:k * GN + (j + 1) * P], rw[:, k, :],
                                                        start=(k == 0), stop=(k == KC - 1))
                        last.then_inc(s_lg, 1)
                    up(0)
                    if routed:
                        pe.wait_ge(s_comb, g + 1)
                        for j in range(GT):
                            last = nc.tensor.transpose(yp[0:NEXP, j * P:(j + 1) * P], comb[:, j, :], c.ident[:, :])
                        last.then_inc(s_ct, 1)
                        pe.wait_ge(s_cT, g + 1)
                        for j in range(GT):
                            last = nc.tensor.matmul(yp[:, j * D:(j + 1) * D], combT[:, j * P:(j + 1) * P], b2[:, :], start=True, stop=True)
                        last.then_inc(s_b2, 1)
                    for e in range(1, NB):
                        up(e)
                        down(e - 1)
                    down(NB - 1)

            @block.scalar
            def _(act):
                a = nc.scalar
                if routed:
                    nrm.root(act)
                act.wait_ge(s_ld, loaded)
                with act.Fori(0, NG) as g:
                    alone(act, s_ag, (s_t, g + 1), (s_h, g * NB))
                    a.copy(xT[:, :], yp[:, 0:KC * GN]).then_inc(s_xT, 1)
                    if routed:
                        alone(act, s_ag, (s_sub, g + 1))
                        a.activation(lg[:, :, :], lg[:, :, :], ACT.Exp).then_inc(s_exp, 1)

                    def gelus(e):
                        if e >= 2:
                            alone(act, s_ag, (s_h, g * NB + e + 1), (s_y, g * NB + e - 1))
                        else:
                            alone(act, s_ag, (s_h, g * NB + e + 1), (s_y, g * NB))
                        for m in range(KC):
                            last = a.activation(hid[:, e % 2, m * GN:(m + 1) * GN].rearrange("p (h n) -> p h n", h=2), hp[:, m, :, 0:HALF], gelu,
                                                bias=b1[:, e * KC + m:e * KC + m + 1])
                        last.then_inc(s_hid, 1)
                    gelus(0)
                    if routed:
                        alone(act, s_ag, (s_ct, g + 1))
                        a.copy(combT[:, :], yp[0:NEXP, 0:GN]).then_inc(s_cT, 1)
                    for e in range(1, NB):
                        gelus(e)

            @block.vector
            def _(dve):
                v = nc.vector
                if routed:
                    dve.wait_ge(s_cst, 1)
                    v.tensor_scalar(lower[:, :, :], lower[:, :, :], 0.0, None, ALU.is_lt).then_inc(s_cst, 1)
                    nrm.moments(dve)
                    dve.wait_ge(nrm.s_rstd, 1)
                    dve.wait_ge(s_cst, 2)
                dve.wait_ge(s_ld, loaded)
                STEPS = 14 if routed else 2
                with dve.Fori(0, NG) as g:
                    count = [0]

                    def link(ins):
                        count[0] += 1
                        ins.then_inc(s_d, 1)
                        alone(dve, s_dg, (s_d, g * STEPS + count[0]))
                    xg = c.x[:, bass.ds(g * GT, GT), :]
                    if routed:
                        nrm.apply(dve, g, lambda j: tok[:, j, :], (s_t, g))
                    else:
                        alone(dve, s_dg, (s_t, g))
                        v.tensor_copy(tok[:, :, :], c.tok[:, bass.ds(g * GT, GT), :]).then_inc(s_tok, 1)
                    alone(dve, s_dg, (s_tok, g + 1))
                    link(v.tensor_tensor(acc[:, :, :], xg, tok[:, :, :], ALU.add))
                    if routed:
                        wide = lambda t: t.rearrange("p (t a) -> p t a", a=1).broadcast_to([P, GT, NEXP])
                        dve.wait_ge(s_lg, g + 1)
                        link(v.tensor_copy(pr[:, :, :], lp[:, :].rearrange("p (t e) -> p t e", t=GT)))
                        link(v.tensor_reduce(top[:, :], pr[:, :, :], AX.X, ALU.max))
                        v.tensor_tensor(lg[:, :, :], pr[:, :, :], wide(top[:, :]), ALU.subtract).then_inc(s_sub, 1)
                        alone(dve, s_dg, (s_exp, g + 1))
                        link(v.tensor_reduce(top[:, :], lg[:, :, :], AX.X, ALU.add))
                        link(v.reciprocal(top[:, :], top[:, :]))
                        link(v.tensor_tensor(pr[:, :, :], lg[:, :, :], wide(top[:, :]), ALU.mult))
                        other = pr[:, :, :].rearrange("p t (a f) -> p t a f", a=1).broadcast_to([P, GT, NEXP, NEXP])
                        own = pr[:, :, :].rearrange("p t (e a) -> p t e a", a=1).broadcast_to([P, GT, NEXP, NEXP])
                        low = lower[:, :, :].rearrange("p (a e) f -> p a e f", a=1).broadcast_to([P, GT, NEXP, NEXP])
                        v.tensor_tensor(gt[:, :, :, :], other, own, ALU.is_gt)
                        link(v.tensor_tensor(eq[:, :, :, :], other, own, ALU.is_equal))
                        link(v.tensor_tensor(eq[:, :, :, :], eq[:, :, :, :], low, ALU.mult))
                        link(v.tensor_tensor(gt[:, :, :, :], gt[:, :, :, :], eq[:, :, :, :], ALU.add))
                        link(v.tensor_reduce(comb[:, :, :], gt[:, :, :, :], AX.X, ALU.add))
                        link(v.scalar_tensor_tensor(comb[:, :, :], comb[:, :, :], TOPK - 0.5, pr[:, :, :], ALU.is_lt, ALU.mult))
                        link(v.tensor_reduce(top[:, :], comb[:, :, :], AX.X, ALU.add))
                        link(v.tensor_scalar(top[:, :], top[:, :], 1e-12, None, ALU.max))
                        link(v.reciprocal(top[:, :], top[:, :]))
                        v.tensor_tensor(comb[:, :, :], comb[:, :, :], wide(top[:, :]), ALU.mult).then_inc(s_comb, 1)
                        alone(dve, s_dg, (s_comb, g + 1), (s_b2, g + 1))
                        v.tensor_tensor(acc[:, :, :], acc[:, :, :], yp[:, 0:GT * D].rearrange("p (t d) -> p t d", t=GT), ALU.add).then_inc(s_acc, 1)
                        gate = lambda e, j: comb[:, j, e:e + 1]
                    else:
                        gate = lambda e, j: c.gate[:, bass.ds(g * GT + j, 1)]
                        for j in range(GT):
                            last = v.scalar_tensor_tensor(acc[:, j, :], b2[:, :], gate(0, j), acc[:, j, :], ALU.mult, ALU.add)
                        link(last)
                    for e in range(NB):
                        alone(dve, s_dg, (s_y, g * NB + e + 1), (s_acc, g * rounds + rounds - NB + e))
                        for j in range(GT):
                            to = acc[:, j, :] if e < NB - 1 else window(c.x, g * GT + j)
                            last = v.scalar_tensor_tensor(to, yp[:, j * D:(j + 1) * D], gate(e, j), acc[:, j, :], ALU.mult, ALU.add)
                        last.then_inc(s_acc, 1)
                    STEPS_SEEN = count[0]
                    assert STEPS_SEEN == STEPS, STEPS_SEEN


def project_qkv(c, A):
    nc = c.nc
    with ExitStack() as s:
        nrm = Norm(c, "n2", s)
        w = c.sb("q_w", [P, KC, 3 * D], F32, s)
        b = c.sb("q_b", [P, 3 * D], F32, s)
        xn = c.sb("q_xn", [P, GT, D], F32, s)
        xT = c.sb("q_xT", [P, KC * GN], F32, s)
        kv = c.sb("q_kv", [P, 2, GT, D], F32, s)
        banks = [c.ps(f"q_p{n}", [P, 3 * 512], F32, s) for n in range(2)]
        names = ("loaded", "transposed", "xT", "rows", "sum", "tok", "dgate", "agate", "pgate")
        s_ld, s_t, s_xT, s_r, s_s, s_tok, s_dg, s_ag, s_pg = (c.sem("q_" + n) for n in names)
        s_kv = [c.sem("q_kout"), c.sem("q_vout")]
        with nc.Block() as block:
            @block.sync
            def _(sp):
                sp.dma_start(w[:, :, :], A["W_qkv"].rearrange("(k p) n -> p k n", p=P)).then_inc(s_ld, 16)
                sp.dma_start(b[:, :], bcast_rows(A["b_qkv"], P)).then_inc(s_ld, 16)
                for g in range(NG):
                    for n, table in enumerate((c.k_dram, c.v_dram)):
                        sp.wait_ge(s_s, 3 * g + 2 + n)
                        sp.dma_start(table.rearrange("(t p) d -> p t d", p=P)[:, g * GT:(g + 1) * GT, :], kv[:, n, :, :]).then_inc(s_kv[n], 16)
                for n in range(2):
                    sp.wait_ge(s_kv[n], 16 * NG)

            @block.tensor
            def _(pe):
                pe.wait_ge(s_ld, 32)
                with pe.Fori(0, NG) as g:
                    pe.wait_ge(nrm.s_xn, g + 1)
                    pe.wait_ge(s_s, 3 * g)
                    transpose_group(nc, banks[0], lambda j, k: xn[:, j, k * P:(k + 1) * P], c.ident).then_inc(s_t, 1)
                    pe.wait_ge(s_xT, g + 1)
                    for n in range(3):
                        if n == 2:
                            pe.wait_ge(s_s, 3 * g + 1)
                        for j in range(GT):
                            for k in range(KC):
                                last = nc.tensor.matmul(banks[(n + 1) % 2][:, j * D:(j + 1) * D], xT[:, k * GN + j * P:k * GN + (j + 1) * P],
                                                        w[:, k, n * D:(n + 1) * D], start=(k == 0), stop=(k == KC - 1))
                        last.then_inc(s_r, 1)

            @block.scalar
            def _(act):
                nrm.root(act)
                with act.Fori(0, NG) as g:
                    alone(act, s_ag, (s_t, g + 1), (s_r, 3 * g))
                    nc.scalar.copy(xT[:, :], banks[0][:, 0:KC * GN]).then_inc(s_xT, 1)

            @block.gpsimd
            def _(pool):
                with pool.Fori(0, NG) as g:
                    alone(pool, s_pg, (nrm.s_xn, g + 1))
                    nc.gpsimd.tensor_copy(c.tok[:, bass.ds(g * GT, GT), :], xn[:, :, :]).then_inc(s_tok, 1)

            @block.vector
            def _(dve):
                v = nc.vector
                nrm.moments(dve)
                dve.wait_ge(nrm.s_rstd, 1)
                dve.wait_ge(s_ld, 32)
                with dve.Fori(0, NG) as g:
                    nrm.apply(dve, g, lambda j: xn[:, j, :], (s_t, g), (s_tok, g))
                    for n in range(3):
                        to = c.q[:, bass.ds(g * GT, GT), :] if n == 0 else kv[:, n - 1, :, :]
                        bias = b[:, n * D:(n + 1) * D].rearrange("p (a d) -> p a d", a=1).broadcast_to([P, GT, D])
                        waits = [(s_r, 3 * g + n + 1)] + ([(s_kv[n - 1], 16 * g)] if n else [])
                        alone(dve, s_dg, *waits)
                        v.tensor_tensor(to, banks[(n + 1) % 2][:, 0:GT * D].rearrange("p (t d) -> p t d", t=GT), bias, ALU.add).then_inc(s_s, 1)


def edge_scores(c, A):
    nc = c.nc
    with ExitStack() as s:
        drow = c.sb("s_drow", [P, 2, IG * P], I32, s)
        spread = c.sb("s_spread", [P, 2, IG, P], F32, s)
        idx = c.sb("s_idx", [P, 2, IG], I32, s)
        rows = c.sb("s_rows", [P, 2, IG, D], F32, s)
        prod = c.sb("s_prod", [P, 2, IG, D], F32, s)
        qp = [c.ps(f"s_q{p}", [P, IG * D], F32, s) for p in range(2)]
        s_dr = [c.sem(f"s_drow{p}") for p in range(2)]
        s_rows = [c.sem(f"s_rows{p}") for p in range(2)]
        names = ("spread", "q", "prod", "score", "idx", "dgate", "pgate")
        s_sp, s_q, s_pr, s_sc, s_idx, s_dg, s_pg = (c.sem("s_" + n) for n in names)
        with nc.Block() as block:
            @block.sync
            def _(sp):
                def load(g, p, steady=True):
                    tiles = [sp.value_load(c.t_row[0:1, bass.ds(g * IG + j, 1)], min_val=0, max_val=NT - 1) for j in range(IG)]
                    if steady:
                        sp.wait_ge(s_sp, g - 1)
                    for j in range(IG):
                        sp.dma_start(drow[:, p, j * P:(j + 1) * P], bcast_rows(A["dst_row"][0:1, bass.ds(tiles[j] * P, P)], P)).then_inc(s_dr[p], 16)
                load(0, 0, False)
                load(1, 1, False)
                with sp.Fori(0, NIG // 2 - 1) as it:
                    for p in (0, 1):
                        load(it * 2 + 2 + p, p)

            @block.gpsimd
            def _(pool):
                def gather(it, p):
                    g = it * 2 + p
                    if not isinstance(it, int):
                        alone(pool, s_pg, (s_pr, g - 1), (s_rows[p], it * 64))
                    nc.gpsimd.tensor_copy(idx[:, p, :], c.src_i[:, bass.ds(g * IG, IG)]).then_inc(s_idx, 1)
                    alone(pool, s_pg, (s_idx, g + 1))
                    for j in range(IG):
                        nc.gpsimd.indirect_dma_start(out=rows[:, p, j, :], out_offset=None, in_=c.k_dram,
                                                     in_offset=bass.IndirectOffsetOnAxis(ap=idx[:, p, j:j + 1], axis=0)).then_inc(s_rows[p], 16)
                gather(0, 0)
                gather(0, 1)
                with pool.Fori(1, NIG // 2) as it:
                    for p in range(2):
                        gather(it, p)

            @block.tensor
            def _(pe):
                def spread_q(g, p, steady=True):
                    wins = [pe.value_load(c.w_row[0:1, bass.ds(g * IG + j, 1)], min_val=0, max_val=NW - 1) for j in range(IG)]
                    pe.wait_ge(s_sp, g + 1)
                    if steady:
                        pe.wait_ge(s_pr, g - 1)
                    for j in range(IG):
                        last = nc.tensor.matmul(qp[p][:, j * D:(j + 1) * D], spread[:, p, j, :], window(c.q, wins[j]), start=True, stop=True)
                    last.then_inc(s_q, 1)
                spread_q(0, 0, False)
                spread_q(1, 1, False)
                with pe.Fori(0, NIG // 2 - 1) as it:
                    for p in (0, 1):
                        spread_q(it * 2 + 2 + p, p)

            @block.vector
            def _(dve):
                v = nc.vector

                def one_hot(g, it, p, steady=True):
                    waits = [(s_dr[p], (it + 1) * 64)] + ([(s_q, g - 1)] if steady else [])
                    alone(dve, s_dg, *waits)
                    for j in range(IG):
                        last = v.tensor_scalar(spread[:, p, j, :], drow[:, p, j * P:(j + 1) * P], c.node_id[:, bass.ds(g * IG + j, 1)], None, ALU.is_equal)
                    last.then_inc(s_sp, 1)

                def scores(g, it, p):
                    dve.wait_ge(s_q, g + 1)
                    dve.wait_ge(s_rows[p], (it + 1) * 64)
                    v.tensor_tensor(prod[:, p, :, :], qp[p][:, :].rearrange("p (a d) -> p a d", a=IG), rows[:, p, :, :], ALU.mult).then_inc(s_pr, 1)
                    alone(dve, s_dg, (s_pr, g + 1))
                    v.tensor_reduce(c.score[:, bass.ds(g * IG, IG), :].rearrange("p a h -> p (a h)"),
                                    prod[:, p, :, :].rearrange("p a (h d) -> p (a h) d", h=H), AX.X, ALU.add).then_inc(s_sc, 1)
                one_hot(0, 0, 0, False)
                one_hot(1, 0, 1, False)
                with dve.Fori(0, NIG // 2 - 1) as it:
                    for p in (0, 1):
                        scores(it * 2 + p, it, p)
                        one_hot(it * 2 + 2 + p, it + 1, p)
                scores(NIG - 2, NIG // 2 - 1, 0)
                scores(NIG - 1, NIG // 2 - 1, 1)


def segment_exp(c, A):
    nc = c.nc
    NEG = -1.0e30
    with ExitStack() as s:
        sT = c.sb("x_sT", [P, CE], F32, s)
        idT = c.sb("x_idT", [P, CE], F32, s)
        new = c.sb("x_new", [P, CE + 1], F32, s)
        run = c.sb("x_run", [P, CE], F32, s)
        up = c.sb("x_up", [P, P], F32, s)
        down = c.sb("x_down", [P, P], F32, s)
        one = c.sb("x_one", [1, 1], F32, s)
        col = c.sb("x_col", [P, 16], F32, s)
        row = c.sb("x_row", [1, 3, P], F32, s)
        carry = c.sb("x_carry", [P, 2], F32, s)
        tp = [c.ps(f"x_tp{n}", [P, 512], F32, s) for n in range(4)]
        sp_ = c.ps("x_small", [P, 512], F32, s)
        s_cst, s_ord, s_d, s_t, s_ev, s_pe, s_v, s_ex = (c.sem("x_" + n) for n in ("const", "ordered", "chain", "transposed", "evacuated", "pe", "dve", "exp"))
        blocks = [(r, min(4, CI - r)) for r in range(0, CI, 4)]
        ids_by_chunk = c.seg_id[:, :].rearrange("p (c r) -> p r c", c=CH)
        score_by_chunk = c.score[:, :, :].rearrange("p (c r) h -> p r c h", c=CH)
        ex_by_chunk = c.ex[:, :, :].rearrange("p (c r) h -> p r c h", c=CH)
        NBK = len(blocks)
        with nc.Block() as block:
            @block.gpsimd
            def _(pool):
                nc.gpsimd.memset(up[:, :], 0.0).then_inc(s_cst, 1)
                nc.gpsimd.memset(down[:, :], 0.0).then_inc(s_cst, 1)
                pool.wait_ge(s_cst, 2)
                nc.gpsimd.memset(one[:, :], 1.0).then_inc(s_cst, 1)
                pool.wait_ge(s_cst, 3)
                pool.affine_select(out=up[:, :], in_=up[:, :], compare_op=ALU.not_equal, fill=1.0, base=H,
                                   pattern=[[-1, P]], channel_multiplier=1).then_inc(s_cst, 1)
                pool.affine_select(out=down[:, :], in_=down[:, :], compare_op=ALU.not_equal, fill=1.0, base=-H,
                                   pattern=[[-1, P]], channel_multiplier=1).then_inc(s_cst, 1)

            @block.tensor
            def _(pe):
                t = nc.tensor
                pe.wait_ge(s_cst, 5)
                pe.wait_ge(s_ord, 2)
                n = 0
                for what in range(2):
                    for r0, k in blocks:
                        if n >= 4:
                            pe.wait_ge(s_ev, n - 3)
                        for r in range(k):
                            at = (r0 + r) * P
                            last = t.transpose(tp[n % 4][:, r * P:(r + 1) * P], (run, new)[what][:, at:at + P], c.ident[:, :])
                        last.then_inc(s_t, 1)
                        n += 1
                pe.wait_ge(s_v, 1)
                t.matmul(sp_[:, 0:1], up[:, :], col[:, 0:1], start=True, stop=True).then_inc(s_pe, 1)
                t.matmul(sp_[:, 1:2], down[:, :], col[:, 1:2], start=True, stop=True).then_inc(s_pe, 1)
                pe.wait_ge(s_v, 2)
                t.matmul(sp_[:, 2:3], down[:, :], new[:, 0:1], start=True, stop=True).then_inc(s_pe, 1)
                for way in range(2):
                    pe.wait_ge(s_v, 3 + 2 * way)
                    t.matmul(sp_[0:1, 128:256], col[:, 8 + 2 * way:9 + 2 * way], c.ident[:, :], start=True, stop=True)
                    t.matmul(sp_[0:1, 256:384], col[:, 9 + 2 * way:10 + 2 * way], c.ident[:, :], start=True, stop=True).then_inc(s_pe, 1)
                    pe.wait_ge(s_v, 4 + 2 * way)
                    t.matmul(sp_[:, 4:5], row[:, 2, :], one[:, :], start=True, stop=True).then_inc(s_pe, 1)
                pe.wait_ge(s_ex, 1)
                for r0, k in blocks:
                    pe.wait_ge(s_ev, n - 3)
                    for r in range(k):
                        last = t.transpose(tp[n % 4][:, r * P:(r + 1) * P], sT[:, (r0 + r) * P:(r0 + r + 1) * P], c.ident[:, :])
                    last.then_inc(s_t, 1)
                    n += 1

            @block.scalar
            def _(act):
                act.wait_ge(s_v, 7)
                nc.scalar.activation(sT[:, :], run[:, :], ACT.Exp, scale=SCALE).then_inc(s_ex, 1)

            @block.vector
            def _(dve):
                v = nc.vector
                link = Chain(dve, s_d)
                order = lambda t: t[:, 0:CE].rearrange("p (r c h) -> p r c h", c=CH, h=H)
                v.tensor_copy(order(run), score_by_chunk).then_inc(s_ord, 1)
                v.tensor_copy(order(new), ids_by_chunk.rearrange("p r (c a) -> p r c a", a=1).broadcast_to([P, CI, CH, H])).then_inc(s_ord, 1)
                n = 0
                for to in (sT, idT):
                    for r0, k in blocks:
                        dve.wait_ge(s_t, n + 1)
                        v.tensor_copy(to[:, r0 * P:(r0 + k) * P], tp[n % 4][:, 0:k * P]).then_inc(s_ev, 1)
                        n += 1
                dve.wait_ge(s_ev, n)
                first, last = idT[:, 0:1], idT[:, CE - 1:CE]
                v.tensor_copy(col[:, 0:1], last)
                v.tensor_copy(col[:, 1:2], first).then_inc(s_v, 1)
                v.tensor_tensor(new[:, 1:CE], idT[:, 1:CE], idT[:, 0:CE - 1], ALU.not_equal)
                dve.wait_ge(s_pe, 2)
                link(v.tensor_tensor(new[:, 0:1], first, sp_[:, 0:1], ALU.not_equal))
                link(v.tensor_scalar(new[:, 0:CE], new[:, 0:CE], NEG, None, ALU.mult))
                link(v.tensor_tensor(col[:, 2:3], first, last, ALU.not_equal))
                v.tensor_tensor(col[:, 3:4], last, sp_[:, 1:2], ALU.not_equal).then_inc(s_v, 1)
                dve.wait_ge(s_v, 2)
                link(v.tensor_scalar(col[:, 2:4], col[:, 2:4], NEG, None, ALU.mult))
                link(v.tensor_tensor(col[:, 8:9], col[:, 2:3], new[:, 0:1], ALU.add))
                link(v.tensor_tensor(col[:, 10:11], col[:, 2:3], col[:, 3:4], ALU.add))
                dve.wait_ge(s_pe, 3)
                link(v.tensor_copy(new[:, CE:CE + 1], sp_[:, 2:3]))

                def carried(way, end):
                    v.tensor_copy(col[:, 9 + 2 * way:10 + 2 * way], end).then_inc(s_v, 1)
                    dve.wait_ge(s_pe, 4 + 2 * way)
                    link(v.tensor_copy(row[:, 0:2, :], sp_[0:1, 128:384].rearrange("p (a n) -> p a n", a=2)))
                    link(v.memset(row[:, 2, :], NEG))
                    by_head = row[:, :, :].rearrange("p a (c h) -> p a h c", h=H)
                    for h in range(H):
                        if way == 0:
                            last = v.tensor_tensor_scan(by_head[:, 2, h, 1:CH], by_head[:, 0, h, 0:CH - 1], by_head[:, 1, h, 0:CH - 1], NEG, ALU.add, ALU.max)
                        else:
                            last = v.tensor_tensor_scan(by_head[:, 2, h, CH - 2::-1], by_head[:, 0, h, CH - 1:0:-1], by_head[:, 1, h, CH - 1:0:-1], NEG, ALU.add, ALU.max)
                    last.then_inc(s_v, 1)
                    dve.wait_ge(s_pe, 5 + 2 * way)
                    link(v.tensor_copy(carry[:, way:way + 1], sp_[:, 4:5]))
                link(v.tensor_tensor_scan(run[:, :], new[:, 0:CE], sT[:, :], NEG, ALU.add, ALU.max))
                carried(0, run[:, CE - 1:CE])
                link(v.tensor_tensor_scan(run[:, :], new[:, 0:CE], sT[:, :], carry[:, 0:1], ALU.add, ALU.max))
                back = lambda t, lo, hi: t[:, lo:hi][:, ::-1]
                link(v.tensor_tensor_scan(back(idT, 0, CE), back(new, 1, CE + 1), back(run, 0, CE), NEG, ALU.add, ALU.max))
                carried(1, idT[:, 0:1])
                link(v.tensor_tensor_scan(back(idT, 0, CE), back(new, 1, CE + 1), back(run, 0, CE), carry[:, 1:2], ALU.add, ALU.max))
                v.tensor_tensor(run[:, :], sT[:, :], idT[:, :], ALU.subtract).then_inc(s_v, 1)
                for r0, k in blocks:
                    dve.wait_ge(s_t, n + 1)
                    v.tensor_copy(ex_by_chunk[:, r0:r0 + k], tp[n % 4][:, 0:k * P].rearrange("p (r c h) -> p r c h", r=k, h=H)).then_inc(s_ev, 1)
                    n += 1


def edge_messages(c, A):
    nc = c.nc
    DM = D + H
    with ExitStack() as s:
        idx = c.sb("a_idx", [P, 2, IG], I32, s)
        rows = c.sb("a_rows", [P, 2, IG, D], F32, s)
        msg = c.sb("a_msg", [P, 2, IG, DM], F32, s)
        hot = c.sb("a_hot", [P, 2, IG, P], F32, s)
        ap = [c.ps(f"a_agg{p}", [P, IG, 512], F32, s) for p in range(2)]
        s_rows = [c.sem(f"a_rows{p}") for p in range(2)]
        names = ("idx", "zero", "ex", "msg", "agg", "acc", "dgate", "pgate", "agate")
        s_idx, s_zero, s_ex, s_msg, s_agg, s_acc, s_dg, s_pg, s_ag = (c.sem("a_" + n) for n in names)
        with nc.Block() as block:
            @block.gpsimd
            def _(pool):
                nc.gpsimd.memset(c.agg[:, :, :], 0.0).then_inc(s_zero, 1)
                pool.wait_ge(s_zero, 1)

                def gather(it, p):
                    g = it * 2 + p
                    if not isinstance(it, int):
                        alone(pool, s_pg, (s_msg, g - 1), (s_rows[p], it * 64))
                    nc.gpsimd.tensor_copy(idx[:, p, :], c.src_i[:, bass.ds(g * IG, IG)]).then_inc(s_idx, 1)
                    alone(pool, s_pg, (s_idx, g + 1))
                    for j in range(IG):
                        nc.gpsimd.indirect_dma_start(out=rows[:, p, j, :], out_offset=None, in_=c.v_dram,
                                                     in_offset=bass.IndirectOffsetOnAxis(ap=idx[:, p, j:j + 1], axis=0)).then_inc(s_rows[p], 16)
                gather(0, 0)
                gather(0, 1)
                with pool.Fori(1, NIG // 2) as it:
                    for p in range(2):
                        gather(it, p)

            @block.tensor
            def _(pe):
                def aggregate(g, p, steady=True):
                    pe.wait_ge(s_msg, g + 1)
                    if steady:
                        pe.wait_ge(s_acc, (g - 1) * IG)
                    for j in range(IG):
                        last = nc.tensor.matmul(ap[p][:, j, 0:DM], hot[:, p, j, :], msg[:, p, j, :], start=True, stop=True)
                    last.then_inc(s_agg, 1)
                aggregate(0, 0, False)
                aggregate(1, 1, False)
                with pe.Fori(0, NIG // 2 - 1) as it:
                    for p in (0, 1):
                        aggregate(it * 2 + 2 + p, p)

            @block.scalar
            def _(act):
                def denominators(g, p, steady=True):
                    if steady:
                        alone(act, s_ag, (s_agg, g - 1))
                    nc.scalar.copy(msg[:, p, :, D:DM], c.ex[:, bass.ds(g * IG, IG), :]).then_inc(s_ex, 1)
                denominators(0, 0, False)
                denominators(1, 1, False)
                with act.Fori(0, NIG // 2 - 1) as it:
                    for p in (0, 1):
                        denominators(it * 2 + 2 + p, p)

            @block.vector
            def _(dve):
                v = nc.vector

                def messages(g, it, p, steady=True):
                    waits = [(s_rows[p], (it + 1) * 64), (s_ex, g + 1)] + ([(s_agg, g - 1)] if steady else [])
                    alone(dve, s_dg, *waits)
                    for j in range(IG):
                        v.tensor_scalar(hot[:, p, j, :], c.iota_n[:, :], c.dst_rel[:, bass.ds(g * IG + j, 1)], None, ALU.is_equal)
                    ex = c.ex[:, bass.ds(g * IG, IG), :].rearrange("p t (h a) -> p (t h) a", a=1).broadcast_to([P, IG * H, DH])
                    for j in range(1):
                        v.tensor_tensor(msg[:, p, :, 0:D].rearrange("p t (h d) -> p t h d", h=H), rows[:, p, :, :].rearrange("p t (h d) -> p t h d", h=H),
                                        c.ex[:, bass.ds(g * IG, IG), :].rearrange("p t (h a) -> p t h a", a=1).broadcast_to([P, IG, H, DH]), ALU.mult).then_inc(s_msg, 1)

                def accumulate(g, p):
                    wins = [dve.value_load(c.w_row[0:1, bass.ds(g * IG + j, 1)], min_val=0, max_val=NW - 1) for j in range(IG)]
                    alone(dve, s_dg, (s_agg, g + 1))
                    for j in range(IG):
                        to = window(c.agg, wins[j])
                        alone(dve, s_dg, (s_acc, g * IG + j))
                        v.tensor_tensor(to, to, ap[p][:, j, 0:DM], ALU.add).then_inc(s_acc, 1)
                dve.wait_ge(s_zero, 1)
                messages(0, 0, 0, False)
                messages(1, 0, 1, False)
                with dve.Fori(0, NIG // 2 - 1) as it:
                    for p in (0, 1):
                        accumulate(it * 2 + p, p)
                        messages(it * 2 + 2 + p, it + 1, p)
                accumulate(NIG - 2, 0)
                accumulate(NIG - 1, 1)


def attention_out(c, A):
    nc = c.nc
    with ExitStack() as s:
        w = c.sb("o_w", [P, KC, D], F32, s)
        b = c.sb("o_b", [P, D], F32, s)
        rden = c.sb("o_rden", [P, NW, H], F32, s)
        hc = c.sb("o_hc", [P, GT, D], F32, s)
        xT = c.sb("o_xT", [P, KC * GN], F32, s)
        tp = c.ps("o_tp", [P, 3 * 512], F32, s)
        op = c.ps("o_op", [P, 3 * 512], F32, s)
        names = ("loaded", "chain", "scaled", "hc", "transposed", "xT", "rows", "bias", "x", "dgate", "agate")
        s_ld, s_d, s_sc, s_hc, s_t, s_xT, s_r, s_b, s_x, s_dg, s_ag = (c.sem("o_" + n) for n in names)
        with nc.Block() as block:
            @block.sync
            def _(sp):
                sp.dma_start(w[:, :, :], A["W_out"].rearrange("(k p) n -> p k n", p=P)).then_inc(s_ld, 16)
                sp.dma_start(b[:, :], bcast_rows(A["b_out"], P)).then_inc(s_ld, 16)

            @block.tensor
            def _(pe):
                pe.wait_ge(s_ld, 32)
                with pe.Fori(0, NG) as g:
                    pe.wait_ge(s_hc, g + 1)
                    pe.wait_ge(s_xT, g)
                    transpose_group(nc, tp, lambda j, k: hc[:, j, k * P:(k + 1) * P], c.ident).then_inc(s_t, 1)
                    pe.wait_ge(s_xT, g + 1)
                    pe.wait_ge(s_x, g)
                    for j in range(GT):
                        for k in range(KC):
                            last = nc.tensor.matmul(op[:, j * D:(j + 1) * D], xT[:, k * GN + j * P:k * GN + (j + 1) * P], w[:, k, :], start=(k == 0), stop=(k == KC - 1))
                    last.then_inc(s_r, 1)

            @block.scalar
            def _(act):
                with act.Fori(0, NG) as g:
                    alone(act, s_ag, (s_t, g + 1), (s_r, g))
                    nc.scalar.copy(xT[:, :], tp[:, 0:KC * GN]).then_inc(s_xT, 1)

            @block.vector
            def _(dve):
                v = nc.vector
                link = Chain(dve, s_d)
                link(v.tensor_scalar(rden[:, :, :], c.agg[:, :, D:D + H], 1e-30, None, ALU.max))
                link(v.reciprocal(rden[:, :, :], rden[:, :, :]))
                dve.wait_ge(s_ld, 32)
                bias = b[:, :].rearrange("p (a d) -> p a d", a=1).broadcast_to([P, GT, D])
                with dve.Fori(0, NG) as g:
                    alone(dve, s_dg, (s_t, g))
                    for j in range(GT):
                        t = g * GT + j
                        last = v.tensor_tensor(hc[:, j, :].rearrange("p (d h) -> p d h", h=H),
                                               c.agg[:, bass.ds(t, 1), 0:D].rearrange("p a (h d) -> p (a d) h", h=H),
                                               rden[:, bass.ds(t, 1), :].broadcast_to([P, DH, H]), ALU.mult)
                    last.then_inc(s_sc, 1)
                    alone(dve, s_dg, (s_sc, g + 1))
                    v.tensor_tensor(hc[:, :, :], hc[:, :, :], c.tok[:, bass.ds(g * GT, GT), :], ALU.add).then_inc(s_hc, 1)
                    xg = c.x[:, bass.ds(g * GT, GT), :]
                    v.tensor_tensor(xg, xg, bias, ALU.add).then_inc(s_b, 1)
                    alone(dve, s_dg, (s_r, g + 1), (s_b, g + 1))
                    v.tensor_tensor(xg, xg, op[:, 0:GT * D].rearrange("p (t d) -> p t d", t=GT), ALU.add).then_inc(s_x, 1)


def select_tokens(c, A):
    nc = c.nc
    with ExitStack() as s:
        nrm = Norm(c, "n3", s)
        wr = c.sb("t_wr", [P, KC], F32, s)
        wrb = c.sb("t_wrb", [P, KC, P], F32, s)
        br = c.sb("t_br", [P, 1], F32, s)
        xn = c.sb("t_xn", [P, GT, D], F32, s)
        xT = c.sb("t_xT", [P, KC * GN], F32, s)
        wrow = c.sb("t_wrow", [P, NP], F32, s)
        r1 = c.sb("t_r1", [P, NP], F32, s)
        r2 = c.sb("t_r2", [P, NP], F32, s)
        r3 = c.sb("t_r3", [P, NP], F32, s)
        wcol = c.sb("t_wcol", [P, NW], F32, s)
        above = c.sb("t_above", [P, NW], F32, s)
        col = c.sb("t_col", [P, 8], F32, s)
        onesr = c.sb("t_onesr", [1, P], F32, s)
        cut = c.sb("t_cut", [1, 1], F32, s)
        tp = c.ps("t_tp", [P, 3 * 512], F32, s)
        wp = c.ps("t_wp", [P, 2, 512], F32, s)
        mp = c.ps("t_mp", [P, 512], F32, s)
        names = ("loaded", "cst", "chain", "tok", "transposed", "xT", "w", "wrow", "cand", "cutT", "cut", "cutb", "count", "dgate", "agate", "pgate")
        s_ld, s_cst, s_d, s_tok, s_t, s_xT, s_w, s_wr, s_cand, s_cT, s_cut, s_cb, s_n, s_dg, s_ag, s_pg = (c.sem("t_" + n) for n in names)
        with nc.Block() as block:
            @block.sync
            def _(sp):
                sp.dma_start(wr[:, :], A["wr"]).then_inc(s_ld, 16)
                sp.dma_start(br[:, :], bcast_rows(A["br"], P)).then_inc(s_ld, 16)

            @block.gpsimd
            def _(pool):
                nc.gpsimd.memset(onesr[:, :], 1.0).then_inc(s_cst, 1)
                with pool.Fori(0, NG) as g:
                    alone(pool, s_pg, (nrm.s_xn, g + 1))
                    nc.gpsimd.tensor_copy(c.tok[:, bass.ds(g * GT, GT), :], xn[:, :, :]).then_inc(s_tok, 1)

            @block.tensor
            def _(pe):
                with pe.Fori(0, NG) as g:
                    pe.wait_ge(nrm.s_xn, g + 1)
                    pe.wait_ge(s_xT, g)
                    transpose_group(nc, tp, lambda j, k: xn[:, j, k * P:(k + 1) * P], c.ident).then_inc(s_t, 1)
                    pe.wait_ge(s_xT, g + 1)
                    pe.wait_ge(s_wr, g)
                    for h in range(2):
                        for k in range(KC):
                            last = nc.tensor.matmul(wp[:, h, 0:HALF], wrb[:, k, :], xT[:, k * GN + h * HALF:k * GN + (h + 1) * HALF], start=(k == 0), stop=(k == KC - 1))
                    last.then_inc(s_w, 1)
                pe.wait_ge(s_cand, 1)
                pe.wait_ge(s_cst, 1)
                nc.tensor.transpose(mp[0:1, 0:P], col[:, 0:1], c.ident[:, :]).then_inc(s_cT, 1)
                pe.wait_ge(s_cut, 1)
                nc.tensor.matmul(mp[:, 256:257], onesr[:, :], cut[:, :], start=True, stop=True).then_inc(s_cb, 1)

            @block.scalar
            def _(act):
                nrm.root(act)
                with act.Fori(0, NG) as g:
                    alone(act, s_ag, (s_t, g + 1), (s_w, g))
                    nc.scalar.copy(xT[:, :], tp[:, 0:KC * GN]).then_inc(s_xT, 1)

            @block.vector
            def _(dve):
                v = nc.vector
                link = Chain(dve, s_d)
                dve.wait_ge(s_ld, 32)
                link(v.tensor_copy(wrb[:, :, :], wr[:, :].rearrange("p (k a) -> p k a", a=1).broadcast_to([P, KC, P])))
                nrm.moments(dve)
                dve.wait_ge(nrm.s_rstd, 1)
                with dve.Fori(0, NG) as g:
                    nrm.apply(dve, g, lambda j: xn[:, j, :], (s_t, g), (s_tok, g))
                    alone(dve, s_dg, (s_w, g + 1))
                    v.tensor_scalar(wrow[:, bass.ds(g * GN, GN)].rearrange("p (h n) -> p h n", h=2), wp[:, :, 0:HALF], br[:, 0:1], None, ALU.add).then_inc(s_wr, 1)
                dve.wait_ge(s_wr, NG)
                link(v.memset(wrow[:, N:NP], -BIG / 3))
                by_win = lambda t: t[:, :].rearrange("p (t n) -> p t n", n=P)
                diag = c.ident[:, :].rearrange("p (a n) -> p a n", a=1).broadcast_to([P, NW, P])
                link(v.tensor_tensor(by_win(r1), by_win(wrow), diag, ALU.mult))
                link(v.tensor_reduce(wcol[:, :], by_win(r1), AX.X, ALU.add))
                with dve.Fori(0, NW) as t:
                    alone(dve, s_dg, (s_n, t))
                    v.tensor_scalar(r1[:, :], wrow[:, :], wcol[:, bass.ds(t, 1)], 0.0, ALU.is_gt, ALU.add, accum_out=above[:, bass.ds(t, 1)]).then_inc(s_n, 1)
                dve.wait_ge(s_n, NW)
                link(v.tensor_scalar(above[:, :], above[:, :], KEEP - 0.5, BIG, ALU.is_gt, ALU.mult))
                link(v.tensor_tensor(above[:, :], above[:, :], wcol[:, :], ALU.add))
                v.tensor_reduce(col[:, 0:1], above[:, :], AX.X, ALU.min).then_inc(s_cand, 1)
                dve.wait_ge(s_cT, 1)
                v.tensor_reduce(cut[:, :], mp[0:1, 0:P], AX.X, ALU.min).then_inc(s_cut, 1)
                dve.wait_ge(s_cb, 1)
                link(v.tensor_copy(col[:, 1:2], mp[:, 256:257]))
                link(v.tensor_scalar(r1[:, :], wrow[:, :], col[:, 1:2], 0.0, ALU.is_gt, ALU.add, accum_out=col[:, 2:3]))
                link(v.tensor_scalar(col[:, 3:4], col[:, 2:3], -1.0, KEEP + 0.5, ALU.mult, ALU.add))
                link(v.tensor_scalar(r2[:, :], wrow[:, :], col[:, 1:2], None, ALU.is_equal))
                link(v.tensor_tensor_scan(r3[:, :], r2[:, :], r2[:, :], 0.0, ALU.add, ALU.bypass))
                link(v.scalar_tensor_tensor(r2[:, :], r3[:, :], col[:, 3:4], r2[:, :], ALU.is_lt, ALU.mult))
                link(v.tensor_tensor(r1[:, :], r1[:, :], r2[:, :], ALU.add))
                link(v.tensor_tensor(r1[:, :], r1[:, :], wrow[:, :], ALU.mult))
                link(v.tensor_tensor(by_win(r1), by_win(r1), diag, ALU.mult))
                link(v.tensor_reduce(c.gate[:, :], by_win(r1), AX.X, ALU.add))


def store(c, A):
    nc = c.nc
    s_out = c.sem("stored")
    with nc.Block() as block:
        @block.sync
        def _(sp):
            sp.dma_start(c.out.rearrange("(t p) d -> p t d", p=P), c.x[:, :, :]).then_inc(s_out, 16)
            sp.wait_ge(s_out, 16)


def build_program(nc, A, out, upto=99):
    c = Core(nc)
    n = [0]

    def phase(f, *args):
        n[0] += 1
        if n[0] <= upto:
            f(c, A, *args)
    with c.keep:
        c.out = out
        c.h_dram = nc.dram_tensor("h_table", (NP, D), F32, kind="Internal").ap()
        c.k_dram = nc.dram_tensor("k_table", (NP, D), F32, kind="Internal").ap()
        c.v_dram = nc.dram_tensor("v_table", (NP, D), F32, kind="Internal").ap()
        c.x = c.sb("x", [P, NW, D])
        c.agg = c.sb("agg", [P, NW, D + H])
        c.tok = c.sb("tok", [P, NW, D])
        c.gate = c.sb("gate", [P, NW])
        phase(prepare)
        phase(source_features)
        phase(edges_first)
        phase(nodes_first)
        phase(experts, True)
        with ExitStack() as attention:
            c.score = c.sb("score", [P, NI, H], F32, attention)
            c.ex = c.sb("ex", [P, NI, H], F32, attention)
            with ExitStack() as queries:
                c.q = c.sb("q", [P, NW, D], F32, queries)
                phase(project_qkv)
                phase(edge_scores)
            phase(segment_exp)
            phase(edge_messages)
            phase(attention_out)
        phase(select_tokens)
        phase(experts, False)
        phase(store)
    return c


def layouts(inputs):
    f = lambda n: np.ascontiguousarray(np.asarray(inputs[n]))
    pad_e = lambda a, v: np.concatenate([a, np.full((EP - E,) + a.shape[1:], v, a.dtype)])
    A = {}
    A["x"] = np.concatenate([f("x"), np.zeros((NP - N, D), np.float32)])
    A["src"] = pad_e(f("src"), 0).reshape(NT, P)
    A["dst"] = pad_e(f("dst"), N).reshape(NT, P)
    A["dst_row"] = A["dst"].reshape(1, EP)
    A["edge_weight"] = pad_e(f("edge_weight"), 0).reshape(NT, P)
    A["eaT"] = np.ascontiguousarray(pad_e(f("edge_attr_64"), 0).T)
    A["g_fw1T"] = np.concatenate([f("L0_gnn_fw1").T, f("L0_gnn_fb1")[None]])
    A["g_fw2T"] = np.ascontiguousarray(f("L0_gnn_fw2").T)
    A["g_fb2"] = f("L0_gnn_fb2")
    A["g_w1T"] = np.ascontiguousarray(f("L0_gnn_w1").T)
    A["g_w2T"] = np.ascontiguousarray(f("L0_gnn_w2").T)
    A["g_b2"] = np.ascontiguousarray(f("L0_gnn_b2").reshape(KC, P).T)
    A["g_w3T"] = np.ascontiguousarray(f("L0_gnn_w3").T)
    A["g_b3"] = f("L0_gnn_b3")
    A["r_wT"] = np.ascontiguousarray(f("L0_ffn_router_w").T)
    A["m_w1"] = f("L0_ffn_w1")
    A["m_b1"] = np.ascontiguousarray(f("L0_ffn_b1").reshape(NEXP, KC, P).transpose(2, 0, 1).reshape(P, NEXP * KC))
    A["m_w2"] = f("L0_ffn_w2")
    A["m_b2"] = f("L0_ffn_b2")
    A["W_qkv"] = f("L1_gnn_W_qkv")
    A["b_qkv"] = f("L1_gnn_b_qkv")
    A["W_out"] = f("L1_gnn_W_out")
    A["b_out"] = f("L1_gnn_b_out")
    A["wr"] = np.ascontiguousarray(f("L1_ffn_wr").reshape(KC, P).T)
    A["br"] = f("L1_ffn_br")
    A["f_w1"] = f("L1_ffn_w1")
    A["f_b1"] = np.ascontiguousarray(f("L1_ffn_b1").reshape(HF // P, P).T)
    A["f_w2"] = f("L1_ffn_w2")
    A["f_b2"] = f("L1_ffn_b2")
    return A


def kernel(**inputs):
    import concourse.bacc as bacc
    from concourse.bass_utils import run_bass_kernel_spmd

    nc = bacc.Bacc("TRN2", target_bir_lowering=False, num_devices=1)
    arrays = {f"in_{k}": v for k, v in layouts(inputs).items()}
    A = {k[3:]: nc.dram_tensor(k, v.shape, mybir.dt.from_np(v.dtype), kind="ExternalInput").ap() for k, v in arrays.items()}
    out = nc.dram_tensor("out", (NP, D), F32, kind="ExternalOutput").ap()
    build_program(nc, A, out)
    r = run_bass_kernel_spmd(nc, [arrays], core_ids=[0])
    return r.results[0]["out"][:N]
```

```python
from contextlib import ExitStack

import numpy as np
import concourse.bass as bass
from concourse import mybir

F32 = mybir.dt.float32
F32R = mybir.dt.float32r
I32 = mybir.dt.int32
ALU = mybir.AluOpType
ACT = mybir.ActivationFunctionType
AX = mybir.AxisListType

P = 128
N, D, E = 3125, 256, 50000
KC = D // P
NW = -(-N // P)
NP = NW * P
GT = 5
NG = NW // GT
GN = GT * P
HALF = GN // 2
CT = 2
TE = CT * P
NT = -(-(E + 1) // TE)
EP = NT * TE
NI = NT + NW - 1
NC = NI * CT
RT, RC = 98, 2
GA = 64
IG = 4
JG = IG // CT
NIG = NC // IG
H, DH = 8, 32
SCALE = DH ** -0.5
CH = 16
CI = -(-NC // CH)
NCP = CI * CH
CE = CI * P
BIG = 3.0e38
LN2 = float(np.log(np.float32(2.0)))
EPS = 1e-5
NEXP = 8
TOPK = 2
HF = 4 * D
KEEP = N // 2 - 1
SP_CAP = 80.0
assert NW % GT == 0 and RT * RC == NT and NI % JG == 0 and RT <= P


class Core:

    def __init__(self, nc):
        self.nc = nc
        self.keep = ExitStack()
        self.gates = {}
        self.phase_sems = []

    def sb(self, name, shape, dt=F32, scope=None):
        return (scope or self.keep).enter_context(self.nc.sbuf_tensor(name, shape, dt))

    def ps(self, name, shape, dt=F32, scope=None):
        return (scope or self.keep).enter_context(self.nc.psum_tensor(name, shape, dt))

    def sem(self, name):
        kind = name.rsplit("_", 1)[-1]
        if not kind.endswith("gate"):
            self.phase_sems.append(self.nc.alloc_semaphore(name=name))
            return self.phase_sems[-1]
        if kind not in self.gates:
            self.gates[kind] = self.keep.enter_context(self.nc.semaphore(kind))
        return self.gates[kind]

    def recycle(self):
        self.nc.clear_and_free_semaphores(self.phase_sems)
        self.phase_sems = []
        self.nc.all_engine_barrier()


class Chain:

    def __init__(self, eng, sem):
        self.eng, self.sem, self.n = eng, sem, 0

    def __call__(self, ins):
        self.n += 1
        ins.then_inc(self.sem, 1)
        self.eng.wait_ge(self.sem, self.n)


def alone(eng, gate, *waits):
    for sem, value in waits:
        eng.wait_ge(sem, value)
    eng.sem_inc(gate, 1)


def bcast_rows(ap, parts):
    n = ap.shape[-1]
    return ap.rearrange("(a n) -> a n", a=1).broadcast_to([parts, n]) if len(ap.shape) == 1 else ap.broadcast_to([parts, n])


def prepare(c, A):
    nc = c.nc
    c.ident = c.sb("ident", [P, P])
    c.iota_n = c.sb("iota_n", [P, P])
    c.src_i = c.sb("src_i", [P, NCP], I32)
    c.dst_rel = c.sb("dst_rel", [P, NCP])
    c.coef = c.sb("coef", [P, NCP])
    c.node_id = c.sb("node_id", [P, NCP])
    c.seg_id = c.sb("seg_id", [P, NCP])
    c.t_row = c.sb("t_row", [1, NI], I32)
    c.w_row = c.sb("w_row", [1, NI], I32)
    with ExitStack() as s:
        rows_i = c.sb("rows_i", [RT, 2, RC, TE], I32, s)
        rows_f = c.sb("rows_f", [RT, 3, RC, TE], F32, s)
        whi = c.sb("whi", [RT, RC], I32, s)
        key = c.sb("key", [RT, RC], F32, s)
        tcol = c.sb("tcol", [RT, RC], F32, s)
        iota_i = c.sb("iota_i", [P, NI], F32, s)
        part = c.sb("part", [P, 1], F32, s)
        after = c.sb("after", [RT, RC, NI], F32, s)
        pick = c.sb("pick", [RT, RC, NI], F32, s)
        ones = c.sb("prep_ones", [RT, P], F32, s)
        t_all = c.sb("t_all", [P, NI], F32, s)
        w_all = c.sb("w_all", [P, NI], F32, s)
        w128 = c.sb("w128", [P, NI], F32, s)
        cols = c.sb("prep_cols", [P, 3, NC], F32, s)
        tmp = c.sb("prep_tmp", [P, NC], F32, s)
        tmp2 = c.sb("prep_tmp2", [P, NC], F32, s)
        period = c.sb("period", [P, NC], F32, s)
        whole = c.sb("whole", [P, NC], I32, s)
        sine = c.sb("sine", [P, NC], F32, s)
        p_t = c.ps("prep_t", [P, 512], F32, s)
        p_c = c.ps("prep_c", [P, 3, 512], F32, s)
        s_in, s_io = c.sem("prep_loaded"), c.sem("prep_iotas")
        s_d, s_a = c.sem("prep_chain"), c.sem("prep_after")
        s_t, s_pick, s_c = c.sem("prep_tiles"), c.sem("prep_picked"), c.sem("prep_columns")
        s_m, s_sin = c.sem("prep_phase"), c.sem("prep_sine")
        with nc.Block() as block:
            @block.sync
            def _(sp):
                sp.dma_start(rows_i[:, 0], A["src"].rearrange("(c p) e -> p c e", p=RT)).then_inc(s_in, 16)
                sp.dma_start(rows_i[:, 1], A["dst"].rearrange("(c p) e -> p c e", p=RT)).then_inc(s_in, 16)
                sp.dma_start(rows_f[:, 2], A["edge_weight"].rearrange("(c p) e -> p c e", p=RT)).then_inc(s_in, 16)

            @block.gpsimd
            def _(pool):
                pool.memset(c.ident[:, :], 0.0).then_inc(s_io, 1)
                pool.iota(iota_i[:, :], pattern=[[1, NI]], base=0, channel_multiplier=0, allow_small_or_imprecise_dtypes=True).then_inc(s_io, 1)
                pool.iota(c.iota_n[:, :], pattern=[[1, P]], base=0, channel_multiplier=0, allow_small_or_imprecise_dtypes=True).then_inc(s_io, 1)
                pool.iota(tcol[:, :], pattern=[[RT, RC]], base=0, channel_multiplier=1, allow_small_or_imprecise_dtypes=True).then_inc(s_io, 1)
                pool.iota(part[:, :], pattern=[[1, 1]], base=0, channel_multiplier=1, allow_small_or_imprecise_dtypes=True).then_inc(s_io, 1)
                pool.memset(ones[:, :], 1.0).then_inc(s_io, 1)
                pool.wait_ge(s_io, 6)
                pool.affine_select(out=c.ident[:, :], in_=c.ident[:, :], compare_op=ALU.not_equal, fill=1.0,
                                   base=0, pattern=[[-1, P]], channel_multiplier=1).then_inc(s_io, 1)

            @block.vector
            def _(dve):
                link = Chain(dve, s_d)
                v = nc.vector
                dve.wait_ge(s_in, 48)
                dve.wait_ge(s_io, 7)
                link(v.tensor_scalar(whi[:, :], rows_i[:, 1, :, TE - 1], 7, None, ALU.logical_shift_right))
                link(v.tensor_copy(rows_f[:, 0:2], rows_i[:, :]))
                link(v.tensor_tensor(key[:, :], whi[:, :], tcol[:, :], ALU.add))
                for k in range(RC):
                    v.tensor_scalar(after[:, k, :], iota_i[0:RT, :], key[:, k:k + 1], None, ALU.is_gt).then_inc(s_a, 1)
                dve.wait_ge(s_t, 1)
                link(v.tensor_copy(t_all[:, :], p_t[:, 0:NI]))
                link(v.tensor_tensor(w_all[:, :], iota_i[:, :], t_all[:, :], ALU.subtract))
                link(v.tensor_scalar(w_all[:, :], w_all[:, :], 0.0, float(NW - 1), ALU.max, ALU.min))
                v.tensor_copy(c.t_row[:, :], t_all[0:1, :]).then_inc(s_pick, 1)
                v.tensor_copy(c.w_row[:, :], w_all[0:1, :]).then_inc(s_pick, 1)
                for k in range(RC):
                    v.tensor_scalar(pick[:, k, :], t_all[0:RT, :], tcol[:, k:k + 1], None, ALU.is_equal).then_inc(s_pick, 1)
                link(v.tensor_scalar(w128[:, :], w_all[:, :], float(P), None, ALU.mult))
                by_item = lambda t: t.rearrange("p (i s) -> p i s", s=CT)
                w128_c = w128[:, :].rearrange("p (i a) -> p i a", a=1).broadcast_to([P, NI, CT])
                link(v.tensor_scalar(by_item(c.node_id[:, 0:NC]), w128_c, part[:, 0:1], None, ALU.add))
                link(v.memset(c.seg_id[:, NC:NCP], 0.0))
                dve.wait_ge(s_c, 3)
                link(v.tensor_copy(cols[:, :, :], p_c[:, :, 0:NC]))
                link(v.tensor_scalar(period[:, :], cols[:, 2, :], 0.5, None, ALU.mult))
                link(v.tensor_copy(whole[:, :], period[:, :]))
                v.tensor_tensor(period[:, :], period[:, :], whole[:, :], ALU.subtract).then_inc(s_m, 1)
                link(v.tensor_copy(c.src_i[:, 0:NC], cols[:, 0, :]))
                link(v.tensor_tensor(by_item(c.dst_rel[:, 0:NC]), by_item(cols[:, 1, :]), w128_c, ALU.subtract))
                link(v.tensor_scalar(tmp[:, :], c.dst_rel[:, 0:NC], 0.0, None, ALU.is_ge))
                link(v.tensor_scalar(tmp2[:, :], c.dst_rel[:, 0:NC], float(P), None, ALU.is_lt))
                link(v.tensor_tensor(tmp[:, :], tmp[:, :], tmp2[:, :], ALU.mult))
                link(v.tensor_scalar(tmp2[:, :], cols[:, 1, :], 1.0, None, ALU.add))
                link(v.tensor_tensor(c.seg_id[:, 0:NC], tmp[:, :], tmp2[:, :], ALU.mult))
                dve.wait_ge(s_sin, 1)
                link(v.tensor_tensor(tmp[:, :], sine[:, :], sine[:, :], ALU.mult))
                link(v.tensor_scalar(c.coef[:, 0:NC], tmp[:, :], -0.5, 0.5, ALU.mult, ALU.add))

            @block.scalar
            def _(act):
                act.wait_ge(s_m, 1)
                nc.scalar.activation(sine[:, :], period[:, :], ACT.Sin, scale=float(np.pi)).then_inc(s_sin, 1)

            @block.tensor
            def _(pe):
                pe.wait_ge(s_io, 7)
                for k in range(RC):
                    pe.wait_ge(s_a, k + 1)
                    last = nc.tensor.matmul(p_t[:, 0:NI], ones[:, :], after[:, k, :], start=(k == 0), stop=(k == RC - 1))
                last.then_inc(s_t, 1)
                pe.wait_ge(s_pick, 2 + RC)
                for a in range(3):
                    for h in range(CT):
                        for k in range(RC):
                            last = nc.tensor.matmul(p_c[:, a, h:NC:CT], rows_f[:, a, k, h * P:(h + 1) * P], pick[:, k, :], start=(k == 0), stop=(k == RC - 1))
                    last.then_inc(s_c, 1)


class Norm:

    def __init__(self, c, name, scope):
        self.c = c
        self.stat = c.sb(f"{name}_stat", [P, NW, 6], F32, scope)
        self.mv = c.sb(f"{name}_mv", [P, NW, 2], F32, scope)
        self.var = c.sb(f"{name}_var", [P, NW], F32, scope)
        self.rstd = c.sb(f"{name}_rstd", [P, NW], F32, scope)
        self.s_stat, self.s_inv, self.s_rstd = c.sem(f"{name}_stats"), c.sem(f"{name}_inv"), c.sem(f"{name}_rstd")
        self.s_gate, self.s_xn = c.sem(f"{name}_gate"), c.sem(f"{name}_normed")

    def moments(self, dve):
        v = self.c.nc.vector
        with dve.Fori(0, NW) as t:
            v.bn_stats(self.stat[:, bass.ds(t, 1), :].rearrange("p a d -> p (a d)"), window(self.c.x, t)).then_inc(self.s_stat, 1)
        dve.wait_ge(self.s_stat, NW)
        for t in range(NW):
            last = v.bn_aggr(self.mv[:, t, :], self.stat[:, t, :])
        last.then_inc(self.s_stat, 1)
        dve.wait_ge(self.s_stat, NW + 1)
        v.tensor_scalar(self.var[:, :], self.mv[:, :, 1], EPS, None, ALU.add).then_inc(self.s_stat, 1)
        dve.wait_ge(self.s_stat, NW + 2)
        v.reciprocal(self.var[:, :], self.var[:, :]).then_inc(self.s_inv, 1)

    def root(self, act):
        act.wait_ge(self.s_inv, 1)
        self.c.nc.scalar.activation(self.rstd[:, :], self.var[:, :], ACT.Sqrt).then_inc(self.s_rstd, 1)

    def apply(self, dve, g, out, *after):
        alone(dve, self.s_gate, *after)
        for j in range(GT):
            last = self.c.nc.vector.tensor_scalar(
                out(j), window(self.c.x, g * GT + j), self.mv[:, bass.ds(g * GT + j, 1), 0:1].rearrange("p a b -> p (a b)"),
                self.rstd[:, bass.ds(g * GT + j, 1)], ALU.subtract, ALU.mult)
        last.then_inc(self.s_xn, 1)


def window(t, n):
    return t[:, bass.ds(n, 1), :].rearrange("p a d -> p (a d)")


def transpose_group(nc, tp, src, ident):
    for k in range(KC):
        for j in range(GT):
            at = (k * GT + j) * P
            last = nc.tensor.transpose(tp[:, at:at + P], src(j, k), ident[:, :])
    return last


def source_features(c, A):
    nc = c.nc
    with ExitStack() as s:
        nrm = Norm(c, "n0", s)
        xn = c.sb("n0_xn", [P, GT, D], F32, s)
        xT = c.sb("n0_xT", [P, KC * GN], F32, s)
        w = c.sb("n0_w", [P, KC, D], F32, s)
        ho = c.sb("n0_h", [P, GT, D], F32, s)
        tp = c.ps("n0_tp", [P, 3 * 512], F32, s)
        hp = c.ps("n0_hp", [P, 3 * 512], F32, s)
        s_x = [c.sem(f"n0_x{g}") for g in range(NG)]
        s_w, s_t, s_xT, s_h, s_ho, s_st = (c.sem("n0_" + n) for n in ("weights", "transposed", "xT", "h", "hout", "stored"))
        s_gate = c.sem("n0_agate")
        with nc.Block() as block:
            @block.sync
            def _(sp):
                sp.dma_start(w[:, :, :], A["g_w1T"].rearrange("(k p) n -> p k n", p=P)).then_inc(s_w, 16)
                for g in range(NG):
                    sp.dma_start(c.x[:, g * GT:(g + 1) * GT, :], A["x"].rearrange("(t p) d -> p t d", p=P)[:, g * GT:(g + 1) * GT, :]).then_inc(s_x[g], 16)
                for g in range(NG):
                    sp.wait_ge(s_ho, g + 1)
                    sp.dma_start(c.h_dram.rearrange("(t p) d -> p t d", p=P)[:, g * GT:(g + 1) * GT, :], ho[:, :, :]).then_inc(s_st, 16)
                sp.wait_ge(s_st, 16 * NG)

            @block.vector
            def _(dve):
                for g in range(NG):
                    dve.wait_ge(s_x[g], 16)
                nrm.moments(dve)
                dve.wait_ge(nrm.s_rstd, 1)
                with dve.Fori(0, NG) as g:
                    nrm.apply(dve, g, lambda j: xn[:, j, :], (s_t, g))

            @block.tensor
            def _(pe):
                pe.wait_ge(s_w, 16)
                with pe.Fori(0, NG) as g:
                    alone(pe, s_gate, (nrm.s_xn, g + 1), (s_xT, g))
                    transpose_group(nc, tp, lambda j, k: xn[:, j, k * P:(k + 1) * P], c.ident).then_inc(s_t, 1)
                    alone(pe, s_gate, (s_xT, g + 1), (s_ho, g))
                    for j in range(GT):
                        for k in range(KC):
                            last = nc.tensor.matmul(hp[:, j * D:(j + 1) * D], xT[:, k * GN + j * P:k * GN + (j + 1) * P], w[:, k, :],
                                                    start=(k == 0), stop=(k == KC - 1))
                    last.then_inc(s_h, 1)

            @block.scalar
            def _(act):
                nrm.root(act)
                with act.Fori(0, NG) as g:
                    alone(act, s_gate, (s_t, g + 1), (s_h, g))
                    nc.scalar.copy(xT[:, :], tp[:, 0:KC * GN]).then_inc(s_xT, 1)
                    alone(act, s_gate, (s_h, g + 1), (s_st, 16 * g))
                    nc.scalar.copy(ho[:, :, :].rearrange("p t d -> p (t d)"), hp[:, 0:GT * D]).then_inc(s_ho, 1)


class Group:

    def __init__(self, it, q):
        self.n = it * 4 + q
        self.slot, self.turn = q % 2, it * 2 + q // 2
        self.slot4, self.turn4 = q % 4, it + q // 4


def real(g):
    return not isinstance(g.n, int) or 0 <= g.n < NIG


def need(eng, gate, *waits, own=False):
    waits = [(s, n) for s, n in waits if not isinstance(n, int) or n > 0]
    for s, n in waits:
        eng.wait_ge(s, n)
    if waits and not own:
        eng.sem_inc(gate, 1)


def gather(c, pool, g, idx, rows, table, s_rows, s_idx, s_used):
    need(pool, c.sem("poolgate"), (s_idx, g.n + 1), (s_used, g.n - 3))
    for j in range(IG):
        c.nc.gpsimd.indirect_dma_start(out=rows[:, g.slot4, j, :], out_offset=None, in_=table,
                                       in_offset=bass.IndirectOffsetOnAxis(ap=idx[:, g.slot4, j:j + 1], axis=0)).then_inc(s_rows[g.slot4], 16)


def source_index(c, act, g, idx, s_rows, s_idx):
    need(act, c.sem("actgate"), (s_rows[g.slot4], g.turn4 * 64))
    c.nc.scalar.copy(idx[:, g.slot4, :], c.src_i[:, bass.ds(g.n * IG, IG)]).then_inc(s_idx, 1)


def item_values(eng, g, row, most):
    return [eng.value_load(row[0:1, bass.ds(g.n * JG + j, 1)], min_val=0, max_val=most) for j in range(JG)]


def rounds(eng, step, before, after):
    first, end = 1, (NIG - before) // 4
    for r in range(-before, 4 * first):
        step(lambda ahead: Group(0, r + ahead))
    with eng.Fori(first, end) as it:
        for q in range(4):
            step(lambda ahead: Group(it, q + ahead))
    for r in range(4 * end, NIG + after + 1):
        step(lambda ahead: Group(0, r + ahead))


def edges_first(c, A):
    nc = c.nc
    W2 = IG * P
    with ExitStack() as s:
        fw1 = c.sb("e1_fw1", [P, D], F32, s)
        fb1 = c.sb("e1_fb1", [P, D], F32, s)
        w1a = c.sb("e1_w1a", [P, D], F32R, s)
        w1b = c.sb("e1_w1b", [P, D], F32R, s)
        fw2 = c.sb("e1_fw2", [P, KC, D], F32, s)
        w2h = c.sb("e1_w2h", [P, KC, D], F32R, s)
        w2l = c.sb("e1_w2l", [P, KC, D], F32R, s)
        bias = c.sb("e1_bias", [P, D], F32, s)
        b2hl = c.sb("e1_b2hl", [GA, D], F32R, s)
        share = c.sb("e1_share", [GA, P], F32R, s)
        mln2 = c.sb("e1_mln2", [P, P], F32, s)
        ea = c.sb("e1_ea", [GA, 2, W2], F32, s)
        eaa = c.sb("e1_eaa", [P, 2, W2], F32R, s)
        eab = c.sb("e1_eab", [P, 2, W2], F32R, s)
        soft = c.sb("e1_soft", [P, 2, KC * W2], F32, s)
        hid = c.sb("e1_hid", [P, 2, KC * W2], F32, s)
        hidh = c.sb("e1_hidh", [P, 2, KC * W2], F32R, s)
        hidl = c.sb("e1_hidl", [P, 2, KC * W2], F32R, s)
        idx = c.sb("e1_idx", [P, 4, IG], I32, s)
        rows = c.sb("e1_rows", [P, 4, IG, D], F32, s)
        msg = c.sb("e1_msg", [P, 2, IG, D], F32, s)
        hot = c.sb("e1_hot", [P, 2, IG, P], F32, s)
        zp = [c.ps(f"e1_z{p}", [P, KC * W2], F32, s) for p in range(2)]
        wp = c.ps("e1_w", [P, IG * D], F32, s)
        ap = [c.ps(f"e1_agg{p}", [P, JG * D], F32, s) for p in range(2)]
        s_ld, s_b, s_split, s_cst = (c.sem("e1_" + n) for n in ("loaded", "biassum", "weightsplit", "constants"))
        s_ea = [c.sem(f"e1_ea{p}") for p in range(2)]
        s_rows = [c.sem(f"e1_rows{p}") for p in range(4)]
        s_idx, s_ag, s_pg, s_dg = c.sem("e1_idx"), c.sem("e1_agate"), c.sem("e1_pgate"), c.sem("e1_dgate")
        s_eh, s_el, s_z, s_exp, s_ln, s_hid, s_hh, s_hl = (c.sem("e1_" + n) for n in ("eahigh", "ealow", "z", "exp", "ln", "hid", "hidhigh", "hidlow"))
        s_w, s_msg, s_agg, s_acc = (c.sem("e1_" + n) for n in ("w", "msg", "agg", "acc"))
        with nc.Block() as block:
            @block.sync
            def _(sp):
                sp.dma_start(fw1[0:GA, :], A["g_fw1T"][0:GA]).then_inc(s_ld, 16)
                sp.dma_start(fw1[GA:P, :], A["g_fw1T"][0:GA]).then_inc(s_ld, 16)
                sp.dma_start(fb1[GA:P, :], A["g_fw1T"][GA:GA + 1].broadcast_to([GA, D])).then_inc(s_ld, 16)
                sp.dma_start(fw2[:, :, :], A["g_fw2T"].rearrange("(k p) n -> p k n", p=P)).then_inc(s_ld, 16)
                sp.dma_start(bias[:, :], bcast_rows(A["g_fb2"], P)).then_inc(s_ld, 16)

                def load(at):
                    g = at(7)
                    if not real(g):
                        return
                    tiles = item_values(sp, g, c.t_row, NT - 1)
                    need(sp, None, (s_el, g.n - 1), own=True)
                    for j in range(JG):
                        sp.dma_start(ea[:, g.slot, j * TE:(j + 1) * TE], A["eaT"][:, bass.ds(tiles[j] * TE, TE)]).then_inc(s_ea[g.slot], 16)
                rounds(sp, load, 7, 0)

            @block.gpsimd
            def _(pool):
                link = Chain(pool, s_cst)
                link(nc.gpsimd.memset(mln2[:, :], -LN2))
                link(nc.gpsimd.memset(share[:, :].bitcast(F32), 1.0 / 32))
                link(nc.gpsimd.memset(eab[GA:P, :, :].bitcast(F32), 1.0 / 32))
                link(nc.gpsimd.memset(c.agg[:, :, 0:D], 0.0))

                def step(at):
                    g = at(3)
                    if real(g):
                        gather(c, pool, g, idx, rows, c.h_dram, s_rows, s_idx, s_msg)
                    g = at(6)
                    if real(g):
                        need(pool, s_pg, (s_eh, g.n + 1), (s_el, g.n))
                        nc.gpsimd.tensor_tensor(eaa[GA:P, g.slot, :], ea[:, g.slot, :], eaa[0:GA, g.slot, :].bitcast(F32), ALU.subtract).then_inc(s_el, 1)
                rounds(pool, step, 6, 0)

            @block.tensor
            def _(pe):
                mm = nc.tensor.matmul
                pe.wait_ge(s_ld, 80)
                pe.wait_ge(s_cst, 4)
                for k in range(KC):
                    last = mm(wp[:, 0:D], mln2[:, :], fw2[:, k, :], start=(k == 0), stop=(k == KC - 1))
                last.then_inc(s_b, 1)
                pe.wait_ge(s_split, 6)

                def step(at):
                    g = at(4)
                    if real(g):
                        need(pe, None, (s_el, g.n + 1), (s_hid, g.n - 1), own=True)
                        for m in range(KC):
                            z, cols = zp[g.slot][:, m * W2:(m + 1) * W2], slice(m * P, (m + 1) * P)
                            mm(z, w1a[:, cols], eaa[:, g.slot, :], start=True, stop=False)
                            last = mm(z, w1b[:, cols], eab[:, g.slot, :], start=False, stop=True)
                        last.then_inc(s_z, 1)
                    g = at(1)
                    if real(g):
                        need(pe, None, (s_hl, g.n + 1), (s_msg, g.n), own=True)
                        for j in range(IG):
                            w = wp[:, j * D:(j + 1) * D]
                            mm(w, share[:, :], b2hl[:, :], start=True, stop=False)
                            for k in range(KC):
                                cols = slice((k * IG + j) * P, (k * IG + j + 1) * P)
                                mm(w, hidh[:, g.slot, cols], w2h[:, k, :], start=False, stop=False)
                                mm(w, hidh[:, g.slot, cols], w2l[:, k, :], start=False, stop=False)
                                last = mm(w, hidl[:, g.slot, cols], w2h[:, k, :], start=False, stop=(k == KC - 1))
                        last.then_inc(s_w, 1)
                    g = at(0)
                    if real(g):
                        need(pe, None, (s_msg, g.n + 1), (s_acc, (g.n - 1) * JG), own=True)
                        for j in range(IG):
                            h, half = divmod(j, CT)
                            last = mm(ap[g.slot][:, h * D:(h + 1) * D], hot[:, g.slot, j, :], msg[:, g.slot, j, :], start=(half == 0), stop=(half == CT - 1))
                        last.then_inc(s_agg, 1)
                rounds(pe, step, 4, 0)

            @block.scalar
            def _(act):
                act.preload_act_table_set("natural_log_exp_and_others")
                act.wait_ge(s_cst, 4)

                def step(at):
                    g = at(4)
                    if real(g):
                        need(act, s_ag, (s_z, g.n + 1))
                        nc.scalar.activation(soft[:, g.slot, :], zp[g.slot][:, :], ACT.Exp).then_inc(s_exp, 1)
                        need(act, s_ag, (s_exp, g.n + 1))
                        nc.scalar.activation(soft[:, g.slot, :], soft[:, g.slot, :], ACT.Ln, bias=1.0).then_inc(s_ln, 1)
                    g = at(6)
                    if real(g):
                        need(act, s_ag, (s_ea[g.slot], (g.turn + 1) * 16 * JG), (s_z, g.n - 1))
                        nc.scalar.copy(eab[0:GA, g.slot, :], ea[:, g.slot, :])
                        nc.scalar.copy(eaa[0:GA, g.slot, :], ea[:, g.slot, :]).then_inc(s_eh, 1)
                    g = at(4)
                    if real(g):
                        source_index(c, act, g, idx, s_rows, s_idx)
                    g = at(3)
                    if real(g):
                        need(act, s_ag, (s_hid, g.n + 1), (s_w, g.n - 1))
                        nc.scalar.copy(hidh[:, g.slot, :], hid[:, g.slot, :]).then_inc(s_hh, 1)
                rounds(act, step, 6, 0)

            @block.vector
            def _(dve):
                v = nc.vector
                high, low = lambda to, x: v.tensor_copy(to, x), lambda to, x, h: v.tensor_tensor(to, x, h.bitcast(F32), ALU.subtract)
                link = Chain(dve, s_split)
                dve.wait_ge(s_ld, 80)
                dve.wait_ge(s_b, 1)
                v.tensor_tensor(bias[:, :], bias[:, :], wp[:, 0:D], ALU.add)
                high(w1a[:, :], fw1[:, :])
                high(w1b[GA:P, :], fb1[GA:P, :])
                link(high(w2h[:, :, :], fw2[:, :, :]))
                link(high(b2hl[:, :], bias[0:GA, :]))
                link(low(w1b[0:GA, :], fw1[0:GA, :], w1a[0:GA, :]))
                link(low(w1b[96:P, :], fb1[96:P, :], w1b[96:P, :]))
                link(low(w2l[:, :, :], fw2[:, :, :], w2h[:, :, :]))
                link(low(b2hl[32:GA, :], bias[32:GA, :], b2hl[32:GA, :]))

                def one_hot(g):
                    if real(g):
                        need(dve, s_dg, (s_agg, g.n - 1))
                        for j in range(IG):
                            i = g.n * IG + j
                            v.tensor_scalar(hot[:, g.slot, j, :], c.iota_n[:, :], c.dst_rel[:, bass.ds(i, 1)], c.coef[:, bass.ds(i, 1)],
                                            ALU.is_equal, ALU.mult)

                def step(at):
                    g = at(-1)
                    if real(g):
                        wins = item_values(dve, g, c.w_row, NW - 1)
                    for j in range(JG):
                        if real(g):
                            to = c.agg[:, bass.ds(wins[j], 1), 0:D].rearrange("p a d -> p (a d)")
                            need(dve, s_dg, (s_agg, g.n + 1), (s_acc, g.n * JG + j))
                            v.tensor_tensor(to, to, ap[g.slot][:, j * D:(j + 1) * D], ALU.add).then_inc(s_acc, 1)
                        if j == 0:
                            one_hot(at(1))
                    h = at(3)
                    if real(h):
                        need(dve, s_dg, (s_ln, h.n + 1), (s_hl, h.n - 1))
                        v.scalar_tensor_tensor(hid[:, h.slot, :], soft[:, h.slot, :], SP_CAP, zp[h.slot][:, :], ALU.min, ALU.max).then_inc(s_hid, 1)
                    g, h = at(1), at(2)
                    if real(h):
                        need(dve, s_dg, (s_hh, h.n + 1))
                        low(hidl[:, h.slot, :], hid[:, h.slot, :], hidh[:, h.slot, :]).then_inc(s_hl, 1)
                    if real(g):
                        need(dve, s_dg, (s_w, g.n + 1), (s_rows[g.slot4], (g.turn4 + 1) * 64))
                        v.tensor_tensor(msg[:, g.slot, :, :], wp[:, :].rearrange("p (a d) -> p a d", a=IG), rows[:, g.slot4, :, :], ALU.mult).then_inc(s_msg, 1)
                rounds(dve, step, 3, 1)


def nodes_first(c, A):
    nc = c.nc
    with ExitStack() as s:
        w2 = c.sb("u_w2", [P, KC, D], F32, s)
        w3 = c.sb("u_w3", [P, KC, D], F32, s)
        b2 = c.sb("u_b2", [P, KC], F32, s)
        b3 = c.sb("u_b3", [P, D], F32, s)
        ag = c.sb("u_agg", [P, GT, D], F32, s)
        aT = c.sb("u_aggT", [P, KC * GN], F32, s)
        z = c.sb("u_z", [P, KC, 2, HALF], F32, s)
        soft = c.sb("u_soft", [P, KC, 2, HALF], F32, s)
        hid = c.sb("u_hid", [P, KC * GN], F32, s)
        to = c.ps("u_to", [P, 3 * 512], F32, s)
        zp = c.ps("u_zp", [P, KC, 2, 512], F32, s)
        names = ("loaded", "agg", "transposed", "aggT", "z", "zbias", "exp", "ln", "max", "hid", "rows", "sum", "x", "dgate", "agate", "pgate")
        s_ld, s_ag, s_t, s_aT, s_z, s_zb, s_e, s_ln, s_mx, s_hid, s_r, s_s, s_x, s_dg, s_agt, s_pg = (c.sem("u_" + n) for n in names)
        with nc.Block() as block:
            @block.sync
            def _(sp):
                sp.dma_start(w2[:, :, :], A["g_w2T"].rearrange("(k p) n -> p k n", p=P)).then_inc(s_ld, 16)
                sp.dma_start(w3[:, :, :], A["g_w3T"].rearrange("(k p) n -> p k n", p=P)).then_inc(s_ld, 16)
                sp.dma_start(b2[:, :], A["g_b2"]).then_inc(s_ld, 16)
                sp.dma_start(b3[:, :], bcast_rows(A["g_b3"], P)).then_inc(s_ld, 16)

            @block.gpsimd
            def _(pool):
                with pool.Fori(0, NG) as g:
                    alone(pool, s_pg, (s_t, g))
                    nc.gpsimd.tensor_copy(ag[:, :, :], c.agg[:, bass.ds(g * GT, GT), 0:D]).then_inc(s_ag, 1)

            @block.tensor
            def _(pe):
                pe.wait_ge(s_ld, 64)
                with pe.Fori(0, NG) as g:
                    pe.wait_ge(s_ag, g + 1)
                    pe.wait_ge(s_s, g)
                    transpose_group(nc, to, lambda j, k: ag[:, j, k * P:(k + 1) * P], c.ident).then_inc(s_t, 1)
                    pe.wait_ge(s_aT, g + 1)
                    for m in range(KC):
                        for h in range(2):
                            for k in range(KC):
                                last = nc.tensor.matmul(zp[:, m, h, 0:HALF], w2[:, k, m * P:(m + 1) * P],
                                                        aT[:, k * GN + h * HALF:k * GN + (h + 1) * HALF], start=(k == 0), stop=(k == KC - 1))
                    last.then_inc(s_z, 1)
                    pe.wait_ge(s_hid, g + 1)
                    for j in range(GT):
                        for k in range(KC):
                            last = nc.tensor.matmul(to[:, j * D:(j + 1) * D], hid[:, k * GN + j * P:k * GN + (j + 1) * P], w3[:, k, :],
                                                    start=(k == 0), stop=(k == KC - 1))
                    last.then_inc(s_r, 1)

            @block.scalar
            def _(act):
                with act.Fori(0, NG) as g:
                    alone(act, s_agt, (s_t, g + 1), (s_z, g))
                    nc.scalar.copy(aT[:, :], to[:, 0:KC * GN]).then_inc(s_aT, 1)
                    alone(act, s_agt, (s_zb, g + 1), (s_mx, g))
                    nc.scalar.activation(soft[:, :, :, :], z[:, :, :, :], ACT.Exp).then_inc(s_e, 1)
                    alone(act, s_agt, (s_e, g + 1))
                    nc.scalar.activation(soft[:, :, :, :], soft[:, :, :, :], ACT.Ln, bias=1.0).then_inc(s_ln, 1)

            @block.vector
            def _(dve):
                v = nc.vector
                dve.wait_ge(s_ld, 64)
                b3_b = b3[:, :].rearrange("p (a d) -> p a d", a=1).broadcast_to([P, GT, D])
                with dve.Fori(0, NG) as g:
                    dve.wait_ge(s_z, g + 1)
                    for m in range(KC):
                        last = v.tensor_scalar(z[:, m], zp[:, m, :, 0:HALF], b2[:, m:m + 1], None, ALU.add)
                    last.then_inc(s_zb, 1)
                    alone(dve, s_dg, (s_ln, g + 1), (s_zb, g + 1), (s_r, g))
                    v.scalar_tensor_tensor(z[:, :, :, :], soft[:, :, :, :], SP_CAP, z[:, :, :, :], ALU.min, ALU.max).then_inc(s_mx, 1)
                    dve.wait_ge(s_mx, g + 1)
                    v.tensor_scalar(hid[:, :], z[:, :, :, :].rearrange("p m h n -> p (m h n)"), -LN2, None, ALU.add).then_inc(s_hid, 1)
                    xg = c.x[:, bass.ds(g * GT, GT), :]
                    v.tensor_tensor(xg, xg, b3_b, ALU.add).then_inc(s_x, 1)
                    alone(dve, s_dg, (s_r, g + 1), (s_x, g + 1))
                    v.tensor_tensor(xg, xg, to[:, 0:GT * D].rearrange("p (t d) -> p t d", t=GT), ALU.add).then_inc(s_s, 1)


def experts(c, A, routed):
    nc = c.nc
    name = "m_" if routed else "f_"
    NB = NEXP if routed else HF // D
    gelu = ACT.Gelu if routed else ACT.Gelu_apprx_tanh
    with ExitStack() as s:
        w1 = c.sb(name + "w1", [P, NB, KC, D], F32, s)
        w2 = c.sb(name + "w2", [P, NB, KC, D], F32, s)
        b1 = c.sb(name + "b1", [P, NB * KC], F32, s)
        acc = c.sb(name + "acc", [P, GT, D], F32, s)
        tok = c.sb(name + "tok", [P, GT, D], F32, s)
        xT = c.sb(name + "xT", [P, KC * GN], F32, s)
        hid = c.sb(name + "hid", [P, 2, KC * GN], F32, s)
        comb = c.sb(name + "comb", [P, GT, NEXP], F32, s)
        hp = c.ps(name + "hp", [P, KC, 2, 512], F32, s)
        yp = c.ps(name + "yp", [P, 3 * 512], F32, s)
        sems = lambda *ns: (c.sem(name + n) for n in ns)
        s_ld, s_cst, s_d, s_t, s_xT, s_h, s_hid, s_y, s_acc, s_x, s_dg, s_ag = sems(
            "loaded", "const", "chain", "transposed", "xT", "h", "hid", "y", "acc", "x", "dgate", "agate")
        if routed:
            nrm = Norm(c, "n1", s)
            s_tok = nrm.s_xn
            b2 = c.sb(name + "b2", [NEXP, D], F32, s)
            rw = c.sb(name + "rw", [P, KC, NEXP], F32, s)
            lower = c.sb(name + "lower", [P, NEXP, NEXP], F32, s)
            lg = c.sb(name + "lg", [P, GT, NEXP], F32, s)
            pr = c.sb(name + "pr", [P, GT, NEXP], F32, s)
            top = c.sb(name + "top", [P, GT], F32, s)
            gt = c.sb(name + "gt", [P, GT, NEXP, NEXP], F32, s)
            eq = c.sb(name + "eq", [P, GT, NEXP, NEXP], F32, s)
            combT = c.sb(name + "combT", [NEXP, GN], F32, s)
            lp = c.ps(name + "lp", [P, GT * NEXP], F32, s)
            s_lg, s_sub, s_exp, s_comb, s_cT, s_ct, s_b2 = sems("logits", "sub", "exp", "comb", "combT", "combt", "b2")
        else:
            s_tok = c.sem(name + "tok")
            b2 = c.sb(name + "b2", [P, D], F32, s)
        n_ld = 3 + NB * 2 * 1 + (1 if routed else 0)
        rounds = NB + (1 if routed else 0)
        with nc.Block() as block:
            @block.sync
            def _(sp):
                if routed:
                    for e in range(NB):
                        sp.dma_start(w1[:, e], A["m_w1"][e].rearrange("(k p) n -> p k n", p=P)).then_inc(s_ld, 16)
                        sp.dma_start(w2[:, e], A["m_w2"][e].rearrange("(k p) n -> p k n", p=P)).then_inc(s_ld, 16)
                    sp.dma_start(b2[:, :], A["m_b2"]).then_inc(s_ld, 16)
                    sp.dma_start(rw[:, :, :], A["r_wT"].rearrange("(k p) n -> p k n", p=P)).then_inc(s_ld, 16)
                    sp.dma_start(b1[:, :], A["m_b1"]).then_inc(s_ld, 16)
                    sp.wait_ge(s_ld, 16 * (2 * NB + 3))
                else:
                    for e in range(NB):
                        sp.dma_start(w1[:, e], A["f_w1"][:, e * D:(e + 1) * D].rearrange("(k p) n -> p k n", p=P)).then_inc(s_ld, 16)
                        sp.dma_start(w2[:, e], A["f_w2"][e * D:(e + 1) * D, :].rearrange("(k p) n -> p k n", p=P)).then_inc(s_ld, 16)
                    sp.dma_start(b2[:, :], bcast_rows(A["f_b2"], P)).then_inc(s_ld, 16)
                    sp.dma_start(b1[:, :], A["f_b1"]).then_inc(s_ld, 16)
                    sp.wait_ge(s_ld, 16 * (2 * NB + 2))

            loaded = 16 * (2 * NB + (3 if routed else 2))

            @block.gpsimd
            def _(pool):
                if routed:
                    pool.iota(lower[:, :, :], pattern=[[-1, NEXP], [1, NEXP]], base=0, channel_multiplier=0,
                              allow_small_or_imprecise_dtypes=True).then_inc(s_cst, 1)

            @block.tensor
            def _(pe):
                pe.wait_ge(s_ld, loaded)
                with pe.Fori(0, NG) as g:
                    pe.wait_ge(s_tok, g + 1)
                    pe.wait_ge(s_acc, g * rounds)
                    transpose_group(nc, yp, lambda j, k: tok[:, j, k * P:(k + 1) * P], c.ident).then_inc(s_t, 1)
                    pe.wait_ge(s_xT, g + 1)

                    def up(e):
                        pe.wait_ge(s_hid, g * NB + e)
                        for m in range(KC):
                            for h in range(2):
                                for k in range(KC):
                                    last = nc.tensor.matmul(hp[:, m, h, 0:HALF], w1[:, e, k, m * P:(m + 1) * P],
                                                            xT[:, k * GN + h * HALF:k * GN + (h + 1) * HALF], start=(k == 0), stop=(k == KC - 1))
                        last.then_inc(s_h, 1)

                    def down(e):
                        pe.wait_ge(s_hid, g * NB + e + 1)
                        pe.wait_ge(s_acc, g * rounds + rounds - NB + e)
                        for j in range(GT):
                            for k in range(KC):
                                last = nc.tensor.matmul(yp[:, j * D:(j + 1) * D], hid[:, e % 2, k * GN + j * P:k * GN + (j + 1) * P], w2[:, e, k, :],
                                                        start=(k == 0), stop=(k == KC - 1))
                        last.then_inc(s_y, 1)
                    if routed:
                        pe.wait_ge(s_sub, g)
                        for j in range(GT):
                            for k in range(KC):
                                last = nc.tensor.matmul(lp[:, j * NEXP:(j + 1) * NEXP], xT[:, k * GN + j * P:k * GN + (j + 1) * P], rw[:, k, :],
                                                        start=(k == 0), stop=(k == KC - 1))
                        last.then_inc(s_lg, 1)
                    up(0)
                    if routed:
                        pe.wait_ge(s_comb, g + 1)
                        for j in range(GT):
                            last = nc.tensor.transpose(yp[0:NEXP, j * P:(j + 1) * P], comb[:, j, :], c.ident[:, :])
                        last.then_inc(s_ct, 1)
                        pe.wait_ge(s_cT, g + 1)
                        for j in range(GT):
                            last = nc.tensor.matmul(yp[:, j * D:(j + 1) * D], combT[:, j * P:(j + 1) * P], b2[:, :], start=True, stop=True)
                        last.then_inc(s_b2, 1)
                    for e in range(1, NB):
                        up(e)
                        down(e - 1)
                    down(NB - 1)

            @block.scalar
            def _(act):
                a = nc.scalar
                if routed:
                    nrm.root(act)
                act.wait_ge(s_ld, loaded)
                with act.Fori(0, NG) as g:
                    alone(act, s_ag, (s_t, g + 1), (s_h, g * NB))
                    a.copy(xT[:, :], yp[:, 0:KC * GN]).then_inc(s_xT, 1)
                    if routed:
                        alone(act, s_ag, (s_sub, g + 1))
                        a.activation(lg[:, :, :], lg[:, :, :], ACT.Exp).then_inc(s_exp, 1)

                    def gelus(e):
                        if e >= 2:
                            alone(act, s_ag, (s_h, g * NB + e + 1), (s_y, g * NB + e - 1))
                        else:
                            alone(act, s_ag, (s_h, g * NB + e + 1), (s_y, g * NB))
                        for m in range(KC):
                            last = a.activation(hid[:, e % 2, m * GN:(m + 1) * GN].rearrange("p (h n) -> p h n", h=2), hp[:, m, :, 0:HALF], gelu,
                                                bias=b1[:, e * KC + m:e * KC + m + 1])
                        last.then_inc(s_hid, 1)
                    gelus(0)
                    if routed:
                        alone(act, s_ag, (s_ct, g + 1))
                        a.copy(combT[:, :], yp[0:NEXP, 0:GN]).then_inc(s_cT, 1)
                    for e in range(1, NB):
                        gelus(e)

            @block.vector
            def _(dve):
                v = nc.vector
                if routed:
                    dve.wait_ge(s_cst, 1)
                    v.tensor_scalar(lower[:, :, :], lower[:, :, :], 0.0, None, ALU.is_lt).then_inc(s_cst, 1)
                    nrm.moments(dve)
                    dve.wait_ge(nrm.s_rstd, 1)
                    dve.wait_ge(s_cst, 2)
                dve.wait_ge(s_ld, loaded)
                STEPS = 14 if routed else 2
                with dve.Fori(0, NG) as g:
                    count = [0]

                    def link(ins):
                        count[0] += 1
                        ins.then_inc(s_d, 1)
                        alone(dve, s_dg, (s_d, g * STEPS + count[0]))
                    xg = c.x[:, bass.ds(g * GT, GT), :]
                    if routed:
                        nrm.apply(dve, g, lambda j: tok[:, j, :], (s_t, g))
                    else:
                        alone(dve, s_dg, (s_t, g))
                        v.tensor_copy(tok[:, :, :], c.tok[:, bass.ds(g * GT, GT), :]).then_inc(s_tok, 1)
                    alone(dve, s_dg, (s_tok, g + 1))
                    link(v.tensor_tensor(acc[:, :, :], xg, tok[:, :, :], ALU.add))
                    if routed:
                        wide = lambda t: t.rearrange("p (t a) -> p t a", a=1).broadcast_to([P, GT, NEXP])
                        dve.wait_ge(s_lg, g + 1)
                        link(v.tensor_copy(pr[:, :, :], lp[:, :].rearrange("p (t e) -> p t e", t=GT)))
                        link(v.tensor_reduce(top[:, :], pr[:, :, :], AX.X, ALU.max))
                        v.tensor_tensor(lg[:, :, :], pr[:, :, :], wide(top[:, :]), ALU.subtract).then_inc(s_sub, 1)
                        alone(dve, s_dg, (s_exp, g + 1))
                        link(v.tensor_reduce(top[:, :], lg[:, :, :], AX.X, ALU.add))
                        link(v.reciprocal(top[:, :], top[:, :]))
                        link(v.tensor_tensor(pr[:, :, :], lg[:, :, :], wide(top[:, :]), ALU.mult))
                        other = pr[:, :, :].rearrange("p t (a f) -> p t a f", a=1).broadcast_to([P, GT, NEXP, NEXP])
                        own = pr[:, :, :].rearrange("p t (e a) -> p t e a", a=1).broadcast_to([P, GT, NEXP, NEXP])
                        low = lower[:, :, :].rearrange("p (a e) f -> p a e f", a=1).broadcast_to([P, GT, NEXP, NEXP])
                        v.tensor_tensor(gt[:, :, :, :], other, own, ALU.is_gt)
                        link(v.tensor_tensor(eq[:, :, :, :], other, own, ALU.is_equal))
                        link(v.tensor_tensor(eq[:, :, :, :], eq[:, :, :, :], low, ALU.mult))
                        link(v.tensor_tensor(gt[:, :, :, :], gt[:, :, :, :], eq[:, :, :, :], ALU.add))
                        link(v.tensor_reduce(comb[:, :, :], gt[:, :, :, :], AX.X, ALU.add))
                        link(v.scalar_tensor_tensor(comb[:, :, :], comb[:, :, :], TOPK - 0.5, pr[:, :, :], ALU.is_lt, ALU.mult))
                        link(v.tensor_reduce(top[:, :], comb[:, :, :], AX.X, ALU.add))
                        link(v.tensor_scalar(top[:, :], top[:, :], 1e-12, None, ALU.max))
                        link(v.reciprocal(top[:, :], top[:, :]))
                        v.tensor_tensor(comb[:, :, :], comb[:, :, :], wide(top[:, :]), ALU.mult).then_inc(s_comb, 1)
                        alone(dve, s_dg, (s_comb, g + 1), (s_b2, g + 1))
                        v.tensor_tensor(acc[:, :, :], acc[:, :, :], yp[:, 0:GT * D].rearrange("p (t d) -> p t d", t=GT), ALU.add).then_inc(s_acc, 1)
                        gate = lambda e, j: comb[:, j, e:e + 1]
                    else:
                        gate = lambda e, j: c.gate[:, bass.ds(g * GT + j, 1)]
                        for j in range(GT):
                            last = v.scalar_tensor_tensor(acc[:, j, :], b2[:, :], gate(0, j), acc[:, j, :], ALU.mult, ALU.add)
                        link(last)
                    for e in range(NB):
                        alone(dve, s_dg, (s_y, g * NB + e + 1), (s_acc, g * rounds + rounds - NB + e))
                        for j in range(GT):
                            to = acc[:, j, :] if e < NB - 1 else window(c.x, g * GT + j)
                            last = v.scalar_tensor_tensor(to, yp[:, j * D:(j + 1) * D], gate(e, j), acc[:, j, :], ALU.mult, ALU.add)
                        last.then_inc(s_acc, 1)
                    STEPS_SEEN = count[0]
                    assert STEPS_SEEN == STEPS, STEPS_SEEN


def project_qkv(c, A):
    nc = c.nc
    with ExitStack() as s:
        nrm = Norm(c, "n2", s)
        w = c.sb("q_w", [P, KC, 3 * D], F32, s)
        b = c.sb("q_b", [P, 3 * D], F32, s)
        xn = c.sb("q_xn", [P, GT, D], F32, s)
        xT = c.sb("q_xT", [P, KC * GN], F32, s)
        kv = c.sb("q_kv", [P, 2, GT, D], F32, s)
        banks = [c.ps(f"q_p{n}", [P, 3 * 512], F32, s) for n in range(2)]
        names = ("loaded", "transposed", "xT", "rows", "sum", "tok", "dgate", "agate", "pgate")
        s_ld, s_t, s_xT, s_r, s_s, s_tok, s_dg, s_ag, s_pg = (c.sem("q_" + n) for n in names)
        s_kv = [c.sem("q_kout"), c.sem("q_vout")]
        with nc.Block() as block:
            @block.sync
            def _(sp):
                sp.dma_start(w[:, :, :], A["W_qkv"].rearrange("(k p) n -> p k n", p=P)).then_inc(s_ld, 16)
                sp.dma_start(b[:, :], bcast_rows(A["b_qkv"], P)).then_inc(s_ld, 16)
                for g in range(NG):
                    for n, table in enumerate((c.k_dram, c.v_dram)):
                        sp.wait_ge(s_s, 3 * g + 2 + n)
                        sp.dma_start(table.rearrange("(t p) d -> p t d", p=P)[:, g * GT:(g + 1) * GT, :], kv[:, n, :, :]).then_inc(s_kv[n], 16)
                for n in range(2):
                    sp.wait_ge(s_kv[n], 16 * NG)

            @block.tensor
            def _(pe):
                pe.wait_ge(s_ld, 32)
                with pe.Fori(0, NG) as g:
                    pe.wait_ge(nrm.s_xn, g + 1)
                    pe.wait_ge(s_s, 3 * g)
                    transpose_group(nc, banks[0], lambda j, k: xn[:, j, k * P:(k + 1) * P], c.ident).then_inc(s_t, 1)
                    pe.wait_ge(s_xT, g + 1)
                    for n in range(3):
                        if n == 2:
                            pe.wait_ge(s_s, 3 * g + 1)
                        for j in range(GT):
                            for k in range(KC):
                                last = nc.tensor.matmul(banks[(n + 1) % 2][:, j * D:(j + 1) * D], xT[:, k * GN + j * P:k * GN + (j + 1) * P],
                                                        w[:, k, n * D:(n + 1) * D], start=(k == 0), stop=(k == KC - 1))
                        last.then_inc(s_r, 1)

            @block.scalar
            def _(act):
                nrm.root(act)
                with act.Fori(0, NG) as g:
                    alone(act, s_ag, (s_t, g + 1), (s_r, 3 * g))
                    nc.scalar.copy(xT[:, :], banks[0][:, 0:KC * GN]).then_inc(s_xT, 1)

            @block.gpsimd
            def _(pool):
                with pool.Fori(0, NG) as g:
                    alone(pool, s_pg, (nrm.s_xn, g + 1))
                    nc.gpsimd.tensor_copy(c.tok[:, bass.ds(g * GT, GT), :], xn[:, :, :]).then_inc(s_tok, 1)

            @block.vector
            def _(dve):
                v = nc.vector
                nrm.moments(dve)
                dve.wait_ge(nrm.s_rstd, 1)
                dve.wait_ge(s_ld, 32)
                with dve.Fori(0, NG) as g:
                    nrm.apply(dve, g, lambda j: xn[:, j, :], (s_t, g), (s_tok, g))
                    for n in range(3):
                        to = c.q[:, bass.ds(g * GT, GT), :] if n == 0 else kv[:, n - 1, :, :]
                        bias = b[:, n * D:(n + 1) * D].rearrange("p (a d) -> p a d", a=1).broadcast_to([P, GT, D])
                        waits = [(s_r, 3 * g + n + 1)] + ([(s_kv[n - 1], 16 * g)] if n else [])
                        alone(dve, s_dg, *waits)
                        v.tensor_tensor(to, banks[(n + 1) % 2][:, 0:GT * D].rearrange("p (t d) -> p t d", t=GT), bias, ALU.add).then_inc(s_s, 1)


def edge_scores(c, A):
    nc = c.nc
    with ExitStack() as s:
        drow = c.sb("s_drow", [P, 2, IG * P], I32, s)
        spread = c.sb("s_spread", [P, 2, IG, P], F32, s)
        idx = c.sb("s_idx", [P, 4, IG], I32, s)
        rows = c.sb("s_rows", [P, 4, IG, D], F32, s)
        prod = c.sb("s_prod", [P, 2, IG, D], F32, s)
        qp = [c.ps(f"s_q{p}", [P, IG * D], F32, s) for p in range(2)]
        s_dr = [c.sem(f"s_drow{p}") for p in range(2)]
        s_rows = [c.sem(f"s_rows{p}") for p in range(4)]
        names = ("spread", "q", "prod", "score", "idx", "dgate", "pad")
        s_sp, s_q, s_pr, s_sc, s_idx, s_dg, s_pad = (c.sem("s_" + n) for n in names)
        with nc.Block() as block:
            @block.sync
            def _(sp):
                def load(at):
                    g = at(3)
                    if real(g):
                        tiles = item_values(sp, g, c.t_row, NT - 1)
                        need(sp, None, (s_sp, g.n - 1), own=True)
                        for j in range(JG):
                            sp.dma_start(drow[:, g.slot, j * TE:(j + 1) * TE], bcast_rows(A["dst_row"][0:1, bass.ds(tiles[j] * TE, TE)], P)).then_inc(s_dr[g.slot], 16)
                rounds(sp, load, 3, 0)

            @block.gpsimd
            def _(pool):
                nc.gpsimd.memset(c.score[:, NC:NCP, :], 0.0).then_inc(s_pad, 1)

                def step(at):
                    g = at(3)
                    if real(g):
                        gather(c, pool, g, idx, rows, c.k_dram, s_rows, s_idx, s_pr)
                rounds(pool, step, 3, 0)
                pool.wait_ge(s_pad, 1)

            @block.scalar
            def _(act):
                def step(at):
                    g = at(4)
                    if real(g):
                        source_index(c, act, g, idx, s_rows, s_idx)
                rounds(act, step, 4, 0)

            @block.tensor
            def _(pe):
                def step(at):
                    g = at(1)
                    if real(g):
                        wins = item_values(pe, g, c.w_row, NW - 1)
                        need(pe, None, (s_sp, g.n + 1), (s_pr, g.n - 1), own=True)
                        for j in range(IG):
                            last = nc.tensor.matmul(qp[g.slot][:, j * D:(j + 1) * D], spread[:, g.slot, j, :], window(c.q, wins[j // CT]), start=True, stop=True)
                        last.then_inc(s_q, 1)
                rounds(pe, step, 1, 0)

            @block.vector
            def _(dve):
                v = nc.vector

                def step(at):
                    g = at(0)
                    if real(g):
                        need(dve, s_dg, (s_q, g.n + 1), (s_rows[g.slot4], (g.turn4 + 1) * 64), (s_sc, g.n - 1))
                        v.tensor_tensor(prod[:, g.slot, :, :], qp[g.slot][:, :].rearrange("p (a d) -> p a d", a=IG), rows[:, g.slot4, :, :], ALU.mult).then_inc(s_pr, 1)
                    h = at(2)
                    if real(h):
                        need(dve, s_dg, (s_dr[h.slot], (h.turn + 1) * 16 * JG), (s_q, h.n - 1))
                        for j in range(IG):
                            last = v.tensor_scalar(spread[:, h.slot, j, :], drow[:, h.slot, j * P:(j + 1) * P], c.node_id[:, bass.ds(h.n * IG + j, 1)], None, ALU.is_equal)
                        last.then_inc(s_sp, 1)
                    if real(g):
                        need(dve, s_dg, (s_pr, g.n + 1))
                        v.tensor_reduce(c.score[:, bass.ds(g.n * IG, IG), :].rearrange("p a h -> p (a h)"),
                                        prod[:, g.slot, :, :].rearrange("p a (h d) -> p (a h) d", h=H), AX.X, ALU.add).then_inc(s_sc, 1)
                rounds(dve, step, 2, 0)


def segment_exp(c, A):
    nc = c.nc
    NEG = -1.0e30
    with ExitStack() as s:
        sT = c.sb("x_sT", [P, CE], F32, s)
        idT = c.sb("x_idT", [P, CE], F32, s)
        new = c.sb("x_new", [P, CE + 1], F32, s)
        run = c.sb("x_run", [P, CE], F32, s)
        up = c.sb("x_up", [P, P], F32, s)
        down = c.sb("x_down", [P, P], F32, s)
        one = c.sb("x_one", [1, 1], F32, s)
        col = c.sb("x_col", [P, 16], F32, s)
        row = c.sb("x_row", [1, 3, P], F32, s)
        carry = c.sb("x_carry", [P, 2], F32, s)
        tp = [c.ps(f"x_tp{n}", [P, 512], F32, s) for n in range(4)]
        sp_ = c.ps("x_small", [P, 512], F32, s)
        s_cst, s_ord, s_d, s_t, s_ev, s_pe, s_v, s_ex = (c.sem("x_" + n) for n in ("const", "ordered", "chain", "transposed", "evacuated", "pe", "dve", "exp"))
        blocks = [(r, min(4, CI - r)) for r in range(0, CI, 4)]
        ids_by_chunk = c.seg_id[:, :].rearrange("p (c r) -> p r c", c=CH)
        score_by_chunk = c.score[:, :, :].rearrange("p (c r) h -> p r c h", c=CH)
        ex_by_chunk = c.ex[:, :, :].rearrange("p (c r) h -> p r c h", c=CH)
        NBK = len(blocks)
        with nc.Block() as block:
            @block.gpsimd
            def _(pool):
                nc.gpsimd.memset(up[:, :], 0.0).then_inc(s_cst, 1)
                nc.gpsimd.memset(down[:, :], 0.0).then_inc(s_cst, 1)
                pool.wait_ge(s_cst, 2)
                nc.gpsimd.memset(one[:, :], 1.0).then_inc(s_cst, 1)
                pool.wait_ge(s_cst, 3)
                pool.affine_select(out=up[:, :], in_=up[:, :], compare_op=ALU.not_equal, fill=1.0, base=H,
                                   pattern=[[-1, P]], channel_multiplier=1).then_inc(s_cst, 1)
                pool.affine_select(out=down[:, :], in_=down[:, :], compare_op=ALU.not_equal, fill=1.0, base=-H,
                                   pattern=[[-1, P]], channel_multiplier=1).then_inc(s_cst, 1)

            @block.tensor
            def _(pe):
                t = nc.tensor
                pe.wait_ge(s_cst, 5)
                pe.wait_ge(s_ord, 2)
                n = 0
                for what in range(2):
                    for r0, k in blocks:
                        if n >= 4:
                            pe.wait_ge(s_ev, n - 3)
                        for r in range(k):
                            at = (r0 + r) * P
                            last = t.transpose(tp[n % 4][:, r * P:(r + 1) * P], (run, new)[what][:, at:at + P], c.ident[:, :])
                        last.then_inc(s_t, 1)
                        n += 1
                pe.wait_ge(s_v, 1)
                t.matmul(sp_[:, 0:1], up[:, :], col[:, 0:1], start=True, stop=True).then_inc(s_pe, 1)
                t.matmul(sp_[:, 1:2], down[:, :], col[:, 1:2], start=True, stop=True).then_inc(s_pe, 1)
                pe.wait_ge(s_v, 2)
                t.matmul(sp_[:, 2:3], down[:, :], new[:, 0:1], start=True, stop=True).then_inc(s_pe, 1)
                for way in range(2):
                    pe.wait_ge(s_v, 3 + 2 * way)
                    t.matmul(sp_[0:1, 128:256], col[:, 8 + 2 * way:9 + 2 * way], c.ident[:, :], start=True, stop=True)
                    t.matmul(sp_[0:1, 256:384], col[:, 9 + 2 * way:10 + 2 * way], c.ident[:, :], start=True, stop=True).then_inc(s_pe, 1)
                    pe.wait_ge(s_v, 4 + 2 * way)
                    t.matmul(sp_[:, 4:5], row[:, 2, :], one[:, :], start=True, stop=True).then_inc(s_pe, 1)
                pe.wait_ge(s_ex, 1)
                for r0, k in blocks:
                    pe.wait_ge(s_ev, n - 3)
                    for r in range(k):
                        last = t.transpose(tp[n % 4][:, r * P:(r + 1) * P], sT[:, (r0 + r) * P:(r0 + r + 1) * P], c.ident[:, :])
                    last.then_inc(s_t, 1)
                    n += 1

            @block.scalar
            def _(act):
                act.wait_ge(s_v, 7)
                nc.scalar.activation(sT[:, :], run[:, :], ACT.Exp, scale=SCALE).then_inc(s_ex, 1)

            @block.vector
            def _(dve):
                v = nc.vector
                link = Chain(dve, s_d)
                order = lambda t: t[:, 0:CE].rearrange("p (r c h) -> p r c h", c=CH, h=H)
                v.tensor_copy(order(run), score_by_chunk).then_inc(s_ord, 1)
                v.tensor_copy(order(new), ids_by_chunk.rearrange("p r (c a) -> p r c a", a=1).broadcast_to([P, CI, CH, H])).then_inc(s_ord, 1)
                n = 0
                for to in (sT, idT):
                    for r0, k in blocks:
                        dve.wait_ge(s_t, n + 1)
                        v.tensor_copy(to[:, r0 * P:(r0 + k) * P], tp[n % 4][:, 0:k * P]).then_inc(s_ev, 1)
                        n += 1
                dve.wait_ge(s_ev, n)
                first, last = idT[:, 0:1], idT[:, CE - 1:CE]
                v.tensor_copy(col[:, 0:1], last)
                v.tensor_copy(col[:, 1:2], first).then_inc(s_v, 1)
                v.tensor_tensor(new[:, 1:CE], idT[:, 1:CE], idT[:, 0:CE - 1], ALU.not_equal)
                dve.wait_ge(s_pe, 2)
                link(v.tensor_tensor(new[:, 0:1], first, sp_[:, 0:1], ALU.not_equal))
                link(v.tensor_scalar(new[:, 0:CE], new[:, 0:CE], NEG, None, ALU.mult))
                link(v.tensor_tensor(col[:, 2:3], first, last, ALU.not_equal))
                v.tensor_tensor(col[:, 3:4], last, sp_[:, 1:2], ALU.not_equal).then_inc(s_v, 1)
                dve.wait_ge(s_v, 2)
                link(v.tensor_scalar(col[:, 2:4], col[:, 2:4], NEG, None, ALU.mult))
                link(v.tensor_tensor(col[:, 8:9], col[:, 2:3], new[:, 0:1], ALU.add))
                link(v.tensor_tensor(col[:, 10:11], col[:, 2:3], col[:, 3:4], ALU.add))
                dve.wait_ge(s_pe, 3)
                link(v.tensor_copy(new[:, CE:CE + 1], sp_[:, 2:3]))

                def carried(way, end):
                    v.tensor_copy(col[:, 9 + 2 * way:10 + 2 * way], end).then_inc(s_v, 1)
                    dve.wait_ge(s_pe, 4 + 2 * way)
                    link(v.tensor_copy(row[:, 0:2, :], sp_[0:1, 128:384].rearrange("p (a n) -> p a n", a=2)))
                    link(v.memset(row[:, 2, :], NEG))
                    by_head = row[:, :, :].rearrange("p a (c h) -> p a h c", h=H)
                    for h in range(H):
                        if way == 0:
                            last = v.tensor_tensor_scan(by_head[:, 2, h, 1:CH], by_head[:, 0, h, 0:CH - 1], by_head[:, 1, h, 0:CH - 1], NEG, ALU.add, ALU.max)
                        else:
                            last = v.tensor_tensor_scan(by_head[:, 2, h, CH - 2::-1], by_head[:, 0, h, CH - 1:0:-1], by_head[:, 1, h, CH - 1:0:-1], NEG, ALU.add, ALU.max)
                    last.then_inc(s_v, 1)
                    dve.wait_ge(s_pe, 5 + 2 * way)
                    link(v.tensor_copy(carry[:, way:way + 1], sp_[:, 4:5]))
                link(v.tensor_tensor_scan(run[:, :], new[:, 0:CE], sT[:, :], NEG, ALU.add, ALU.max))
                carried(0, run[:, CE - 1:CE])
                link(v.tensor_tensor_scan(run[:, :], new[:, 0:CE], sT[:, :], carry[:, 0:1], ALU.add, ALU.max))
                back = lambda t, lo, hi: t[:, lo:hi][:, ::-1]
                link(v.tensor_tensor_scan(back(idT, 0, CE), back(new, 1, CE + 1), back(run, 0, CE), NEG, ALU.add, ALU.max))
                carried(1, idT[:, 0:1])
                link(v.tensor_tensor_scan(back(idT, 0, CE), back(new, 1, CE + 1), back(run, 0, CE), carry[:, 1:2], ALU.add, ALU.max))
                v.tensor_tensor(run[:, :], sT[:, :], idT[:, :], ALU.subtract).then_inc(s_v, 1)
                for r0, k in blocks:
                    dve.wait_ge(s_t, n + 1)
                    v.tensor_copy(ex_by_chunk[:, r0:r0 + k], tp[n % 4][:, 0:k * P].rearrange("p (r c h) -> p r c h", r=k, h=H)).then_inc(s_ev, 1)
                    n += 1


def edge_messages(c, A):
    nc = c.nc
    DM = D + H
    with ExitStack() as s:
        idx = c.sb("a_idx", [P, 4, IG], I32, s)
        rows = c.sb("a_rows", [P, 4, IG, D], F32, s)
        msg = c.sb("a_msg", [P, 2, IG, DM], F32, s)
        hot = c.sb("a_hot", [P, 2, IG, P], F32, s)
        ap = [c.ps(f"a_agg{p}", [P, JG, 512], F32, s) for p in range(2)]
        s_rows = [c.sem(f"a_rows{p}") for p in range(4)]
        names = ("idx", "zero", "ex", "msg", "agg", "acc", "dgate", "agate")
        s_idx, s_zero, s_ex, s_msg, s_agg, s_acc, s_dg, s_ag = (c.sem("a_" + n) for n in names)
        with nc.Block() as block:
            @block.gpsimd
            def _(pool):
                nc.gpsimd.memset(c.agg[:, :, :], 0.0).then_inc(s_zero, 1)
                pool.wait_ge(s_zero, 1)

                def step(at):
                    g = at(3)
                    if real(g):
                        gather(c, pool, g, idx, rows, c.v_dram, s_rows, s_idx, s_msg)
                rounds(pool, step, 3, 0)

            @block.tensor
            def _(pe):
                def step(at):
                    g = at(0)
                    if real(g):
                        need(pe, None, (s_msg, g.n + 1), (s_acc, (g.n - 1) * JG), own=True)
                        for j in range(IG):
                            h, half = divmod(j, CT)
                            last = nc.tensor.matmul(ap[g.slot][:, h, 0:DM], hot[:, g.slot, j, :], msg[:, g.slot, j, :], start=(half == 0), stop=(half == CT - 1))
                        last.then_inc(s_agg, 1)
                rounds(pe, step, 0, 0)

            @block.scalar
            def _(act):
                def step(at):
                    g = at(4)
                    if real(g):
                        source_index(c, act, g, idx, s_rows, s_idx)
                    g = at(2)
                    if real(g):
                        need(act, s_ag, (s_agg, g.n - 1))
                        nc.scalar.copy(msg[:, g.slot, :, D:DM], c.ex[:, bass.ds(g.n * IG, IG), :]).then_inc(s_ex, 1)
                rounds(act, step, 4, 0)

            @block.vector
            def _(dve):
                v = nc.vector
                by_head = lambda t: t.rearrange("p t (h d) -> p t h d", h=H)

                def one_hot(g):
                    if real(g):
                        need(dve, s_dg, (s_agg, g.n - 1))
                        for j in range(IG):
                            v.tensor_scalar(hot[:, g.slot, j, :], c.iota_n[:, :], c.dst_rel[:, bass.ds(g.n * IG + j, 1)], None, ALU.is_equal)

                def step(at):
                    g = at(-1)
                    if real(g):
                        wins = item_values(dve, g, c.w_row, NW - 1)
                    for j in range(JG):
                        if real(g):
                            need(dve, s_dg, (s_agg, g.n + 1), (s_acc, g.n * JG + j))
                            to = window(c.agg, wins[j])
                            v.tensor_tensor(to, to, ap[g.slot][:, j, 0:DM], ALU.add).then_inc(s_acc, 1)
                        if j == 0:
                            one_hot(at(1))
                    g = at(1)
                    if real(g):
                        need(dve, s_dg, (s_rows[g.slot4], (g.turn4 + 1) * 64), (s_ex, g.n + 1))
                        ex = c.ex[:, bass.ds(g.n * IG, IG), :].rearrange("p t (h a) -> p t h a", a=1).broadcast_to([P, IG, H, DH])
                        v.tensor_tensor(by_head(msg[:, g.slot, :, 0:D]), by_head(rows[:, g.slot4, :, :]), ex, ALU.mult).then_inc(s_msg, 1)
                dve.wait_ge(s_zero, 1)
                rounds(dve, step, 1, 1)


def attention_out(c, A):
    nc = c.nc
    with ExitStack() as s:
        w = c.sb("o_w", [P, KC, D], F32, s)
        b = c.sb("o_b", [P, D], F32, s)
        rden = c.sb("o_rden", [P, NW, H], F32, s)
        hc = c.sb("o_hc", [P, GT, D], F32, s)
        xT = c.sb("o_xT", [P, KC * GN], F32, s)
        tp = c.ps("o_tp", [P, 3 * 512], F32, s)
        op = c.ps("o_op", [P, 3 * 512], F32, s)
        names = ("loaded", "chain", "scaled", "hc", "transposed", "xT", "rows", "bias", "x", "dgate", "agate")
        s_ld, s_d, s_sc, s_hc, s_t, s_xT, s_r, s_b, s_x, s_dg, s_ag = (c.sem("o_" + n) for n in names)
        with nc.Block() as block:
            @block.sync
            def _(sp):
                sp.dma_start(w[:, :, :], A["W_out"].rearrange("(k p) n -> p k n", p=P)).then_inc(s_ld, 16)
                sp.dma_start(b[:, :], bcast_rows(A["b_out"], P)).then_inc(s_ld, 16)

            @block.tensor
            def _(pe):
                pe.wait_ge(s_ld, 32)
                with pe.Fori(0, NG) as g:
                    pe.wait_ge(s_hc, g + 1)
                    pe.wait_ge(s_xT, g)
                    transpose_group(nc, tp, lambda j, k: hc[:, j, k * P:(k + 1) * P], c.ident).then_inc(s_t, 1)
                    pe.wait_ge(s_xT, g + 1)
                    pe.wait_ge(s_x, g)
                    for j in range(GT):
                        for k in range(KC):
                            last = nc.tensor.matmul(op[:, j * D:(j + 1) * D], xT[:, k * GN + j * P:k * GN + (j + 1) * P], w[:, k, :], start=(k == 0), stop=(k == KC - 1))
                    last.then_inc(s_r, 1)

            @block.scalar
            def _(act):
                with act.Fori(0, NG) as g:
                    alone(act, s_ag, (s_t, g + 1), (s_r, g))
                    nc.scalar.copy(xT[:, :], tp[:, 0:KC * GN]).then_inc(s_xT, 1)

            @block.vector
            def _(dve):
                v = nc.vector
                link = Chain(dve, s_d)
                link(v.tensor_scalar(rden[:, :, :], c.agg[:, :, D:D + H], 1e-30, None, ALU.max))
                link(v.reciprocal(rden[:, :, :], rden[:, :, :]))
                dve.wait_ge(s_ld, 32)
                bias = b[:, :].rearrange("p (a d) -> p a d", a=1).broadcast_to([P, GT, D])
                with dve.Fori(0, NG) as g:
                    alone(dve, s_dg, (s_t, g))
                    for j in range(GT):
                        t = g * GT + j
                        last = v.tensor_tensor(hc[:, j, :].rearrange("p (d h) -> p d h", h=H),
                                               c.agg[:, bass.ds(t, 1), 0:D].rearrange("p a (h d) -> p (a d) h", h=H),
                                               rden[:, bass.ds(t, 1), :].broadcast_to([P, DH, H]), ALU.mult)
                    last.then_inc(s_sc, 1)
                    alone(dve, s_dg, (s_sc, g + 1))
                    v.tensor_tensor(hc[:, :, :], hc[:, :, :], c.tok[:, bass.ds(g * GT, GT), :], ALU.add).then_inc(s_hc, 1)
                    xg = c.x[:, bass.ds(g * GT, GT), :]
                    v.tensor_tensor(xg, xg, bias, ALU.add).then_inc(s_b, 1)
                    alone(dve, s_dg, (s_r, g + 1), (s_b, g + 1))
                    v.tensor_tensor(xg, xg, op[:, 0:GT * D].rearrange("p (t d) -> p t d", t=GT), ALU.add).then_inc(s_x, 1)


def select_tokens(c, A):
    nc = c.nc
    with ExitStack() as s:
        nrm = Norm(c, "n3", s)
        wr = c.sb("t_wr", [P, KC], F32, s)
        wrb = c.sb("t_wrb", [P, KC, P], F32, s)
        br = c.sb("t_br", [P, 1], F32, s)
        xn = c.sb("t_xn", [P, GT, D], F32, s)
        xT = c.sb("t_xT", [P, KC * GN], F32, s)
        wrow = c.sb("t_wrow", [P, NP], F32, s)
        r1 = c.sb("t_r1", [P, NP], F32, s)
        r2 = c.sb("t_r2", [P, NP], F32, s)
        r3 = c.sb("t_r3", [P, NP], F32, s)
        wcol = c.sb("t_wcol", [P, NW], F32, s)
        above = c.sb("t_above", [P, NW], F32, s)
        col = c.sb("t_col", [P, 8], F32, s)
        onesr = c.sb("t_onesr", [1, P], F32, s)
        cut = c.sb("t_cut", [1, 1], F32, s)
        tp = c.ps("t_tp", [P, 3 * 512], F32, s)
        wp = c.ps("t_wp", [P, 2, 512], F32, s)
        mp = c.ps("t_mp", [P, 512], F32, s)
        names = ("loaded", "cst", "chain", "tok", "transposed", "xT", "w", "wrow", "cand", "cutT", "cut", "cutb", "count", "dgate", "agate", "pgate")
        s_ld, s_cst, s_d, s_tok, s_t, s_xT, s_w, s_wr, s_cand, s_cT, s_cut, s_cb, s_n, s_dg, s_ag, s_pg = (c.sem("t_" + n) for n in names)
        with nc.Block() as block:
            @block.sync
            def _(sp):
                sp.dma_start(wr[:, :], A["wr"]).then_inc(s_ld, 16)
                sp.dma_start(br[:, :], bcast_rows(A["br"], P)).then_inc(s_ld, 16)

            @block.gpsimd
            def _(pool):
                nc.gpsimd.memset(onesr[:, :], 1.0).then_inc(s_cst, 1)
                with pool.Fori(0, NG) as g:
                    alone(pool, s_pg, (nrm.s_xn, g + 1))
                    nc.gpsimd.tensor_copy(c.tok[:, bass.ds(g * GT, GT), :], xn[:, :, :]).then_inc(s_tok, 1)

            @block.tensor
            def _(pe):
                with pe.Fori(0, NG) as g:
                    pe.wait_ge(nrm.s_xn, g + 1)
                    pe.wait_ge(s_xT, g)
                    transpose_group(nc, tp, lambda j, k: xn[:, j, k * P:(k + 1) * P], c.ident).then_inc(s_t, 1)
                    pe.wait_ge(s_xT, g + 1)
                    pe.wait_ge(s_wr, g)
                    for h in range(2):
                        for k in range(KC):
                            last = nc.tensor.matmul(wp[:, h, 0:HALF], wrb[:, k, :], xT[:, k * GN + h * HALF:k * GN + (h + 1) * HALF], start=(k == 0), stop=(k == KC - 1))
                    last.then_inc(s_w, 1)
                pe.wait_ge(s_cand, 1)
                pe.wait_ge(s_cst, 1)
                nc.tensor.transpose(mp[0:1, 0:P], col[:, 0:1], c.ident[:, :]).then_inc(s_cT, 1)
                pe.wait_ge(s_cut, 1)
                nc.tensor.matmul(mp[:, 256:257], onesr[:, :], cut[:, :], start=True, stop=True).then_inc(s_cb, 1)

            @block.scalar
            def _(act):
                nrm.root(act)
                with act.Fori(0, NG) as g:
                    alone(act, s_ag, (s_t, g + 1), (s_w, g))
                    nc.scalar.copy(xT[:, :], tp[:, 0:KC * GN]).then_inc(s_xT, 1)

            @block.vector
            def _(dve):
                v = nc.vector
                link = Chain(dve, s_d)
                dve.wait_ge(s_ld, 32)
                link(v.tensor_copy(wrb[:, :, :], wr[:, :].rearrange("p (k a) -> p k a", a=1).broadcast_to([P, KC, P])))
                nrm.moments(dve)
                dve.wait_ge(nrm.s_rstd, 1)
                with dve.Fori(0, NG) as g:
                    nrm.apply(dve, g, lambda j: xn[:, j, :], (s_t, g), (s_tok, g))
                    alone(dve, s_dg, (s_w, g + 1))
                    v.tensor_scalar(wrow[:, bass.ds(g * GN, GN)].rearrange("p (h n) -> p h n", h=2), wp[:, :, 0:HALF], br[:, 0:1], None, ALU.add).then_inc(s_wr, 1)
                dve.wait_ge(s_wr, NG)
                link(v.memset(wrow[:, N:NP], -BIG / 3))
                by_win = lambda t: t[:, :].rearrange("p (t n) -> p t n", n=P)
                diag = c.ident[:, :].rearrange("p (a n) -> p a n", a=1).broadcast_to([P, NW, P])
                link(v.tensor_tensor(by_win(r1), by_win(wrow), diag, ALU.mult))
                link(v.tensor_reduce(wcol[:, :], by_win(r1), AX.X, ALU.add))
                with dve.Fori(0, NW) as t:
                    alone(dve, s_dg, (s_n, t))
                    v.tensor_scalar(r1[:, :], wrow[:, :], wcol[:, bass.ds(t, 1)], 0.0, ALU.is_gt, ALU.add, accum_out=above[:, bass.ds(t, 1)]).then_inc(s_n, 1)
                dve.wait_ge(s_n, NW)
                link(v.tensor_scalar(above[:, :], above[:, :], KEEP - 0.5, BIG, ALU.is_gt, ALU.mult))
                link(v.tensor_tensor(above[:, :], above[:, :], wcol[:, :], ALU.add))
                v.tensor_reduce(col[:, 0:1], above[:, :], AX.X, ALU.min).then_inc(s_cand, 1)
                dve.wait_ge(s_cT, 1)
                v.tensor_reduce(cut[:, :], mp[0:1, 0:P], AX.X, ALU.min).then_inc(s_cut, 1)
                dve.wait_ge(s_cb, 1)
                link(v.tensor_copy(col[:, 1:2], mp[:, 256:257]))
                link(v.tensor_scalar(r1[:, :], wrow[:, :], col[:, 1:2], 0.0, ALU.is_gt, ALU.add, accum_out=col[:, 2:3]))
                link(v.tensor_scalar(col[:, 3:4], col[:, 2:3], -1.0, KEEP + 0.5, ALU.mult, ALU.add))
                link(v.tensor_scalar(r2[:, :], wrow[:, :], col[:, 1:2], None, ALU.is_equal))
                link(v.tensor_tensor_scan(r3[:, :], r2[:, :], r2[:, :], 0.0, ALU.add, ALU.bypass))
                link(v.scalar_tensor_tensor(r2[:, :], r3[:, :], col[:, 3:4], r2[:, :], ALU.is_lt, ALU.mult))
                link(v.tensor_tensor(r1[:, :], r1[:, :], r2[:, :], ALU.add))
                link(v.tensor_tensor(r1[:, :], r1[:, :], wrow[:, :], ALU.mult))
                link(v.tensor_tensor(by_win(r1), by_win(r1), diag, ALU.mult))
                link(v.tensor_reduce(c.gate[:, :], by_win(r1), AX.X, ALU.add))


def store(c, A):
    nc = c.nc
    s_out = c.sem("stored")
    with nc.Block() as block:
        @block.sync
        def _(sp):
            sp.dma_start(c.out.rearrange("(t p) d -> p t d", p=P), c.x[:, :, :]).then_inc(s_out, 16)
            sp.wait_ge(s_out, 16)


def build_program(nc, A, out, upto=99):
    c = Core(nc)
    n = [0]

    def phase(f, *args):
        n[0] += 1
        if n[0] <= upto:
            f(c, A, *args)
    with c.keep:
        c.out = out
        c.h_dram = nc.dram_tensor("h_table", (NP, D), F32, kind="Internal").ap()
        c.k_dram = nc.dram_tensor("k_table", (NP, D), F32, kind="Internal").ap()
        c.v_dram = nc.dram_tensor("v_table", (NP, D), F32, kind="Internal").ap()
        c.x = c.sb("x", [P, NW, D])
        c.agg = c.sb("agg", [P, NW, D + H])
        c.tok = c.sb("tok", [P, NW, D])
        c.gate = c.sb("gate", [P, NW])
        phase(prepare)
        phase(source_features)
        phase(edges_first)
        phase(nodes_first)
        phase(experts, True)
        c.recycle()
        with ExitStack() as attention:
            c.score = c.sb("score", [P, NCP, H], F32, attention)
            c.ex = c.sb("ex", [P, NCP, H], F32, attention)
            with ExitStack() as queries:
                c.q = c.sb("q", [P, NW, D], F32, queries)
                phase(project_qkv)
                phase(edge_scores)
            phase(segment_exp)
            phase(edge_messages)
            phase(attention_out)
        phase(select_tokens)
        phase(experts, False)
        phase(store)
    return c


def layouts(inputs):
    f = lambda n: np.ascontiguousarray(np.asarray(inputs[n]))
    pad_e = lambda a, v: np.concatenate([a, np.full((EP - E,) + a.shape[1:], v, a.dtype)])
    A = {}
    A["x"] = np.concatenate([f("x"), np.zeros((NP - N, D), np.float32)])
    A["src"] = pad_e(f("src"), 0).reshape(NT, TE)
    A["dst"] = pad_e(f("dst"), N).reshape(NT, TE)
    A["dst_row"] = A["dst"].reshape(1, EP)
    A["edge_weight"] = pad_e(f("edge_weight"), 0).reshape(NT, TE)
    A["eaT"] = np.ascontiguousarray(pad_e(f("edge_attr_64"), 0).T)
    A["g_fw1T"] = np.concatenate([f("L0_gnn_fw1").T, f("L0_gnn_fb1")[None]])
    A["g_fw2T"] = np.ascontiguousarray(f("L0_gnn_fw2").T)
    A["g_fb2"] = f("L0_gnn_fb2")
    A["g_w1T"] = np.ascontiguousarray(f("L0_gnn_w1").T)
    A["g_w2T"] = np.ascontiguousarray(f("L0_gnn_w2").T)
    A["g_b2"] = np.ascontiguousarray(f("L0_gnn_b2").reshape(KC, P).T)
    A["g_w3T"] = np.ascontiguousarray(f("L0_gnn_w3").T)
    A["g_b3"] = f("L0_gnn_b3")
    A["r_wT"] = np.ascontiguousarray(f("L0_ffn_router_w").T)
    A["m_w1"] = f("L0_ffn_w1")
    A["m_b1"] = np.ascontiguousarray(f("L0_ffn_b1").reshape(NEXP, KC, P).transpose(2, 0, 1).reshape(P, NEXP * KC))
    A["m_w2"] = f("L0_ffn_w2")
    A["m_b2"] = f("L0_ffn_b2")
    A["W_qkv"] = f("L1_gnn_W_qkv")
    A["b_qkv"] = f("L1_gnn_b_qkv")
    A["W_out"] = f("L1_gnn_W_out")
    A["b_out"] = f("L1_gnn_b_out")
    A["wr"] = np.ascontiguousarray(f("L1_ffn_wr").reshape(KC, P).T)
    A["br"] = f("L1_ffn_br")
    A["f_w1"] = f("L1_ffn_w1")
    A["f_b1"] = np.ascontiguousarray(f("L1_ffn_b1").reshape(HF // P, P).T)
    A["f_w2"] = f("L1_ffn_w2")
    A["f_b2"] = f("L1_ffn_b2")
    return A


def kernel(**inputs):
    import concourse.bacc as bacc
    from concourse.bass_utils import run_bass_kernel_spmd

    nc = bacc.Bacc("TRN2", target_bir_lowering=False, num_devices=1)
    arrays = {f"in_{k}": v for k, v in layouts(inputs).items()}
    A = {k[3:]: nc.dram_tensor(k, v.shape, mybir.dt.from_np(v.dtype), kind="ExternalInput").ap() for k, v in arrays.items()}
    out = nc.dram_tensor("out", (NP, D), F32, kind="ExternalOutput").ap()
    build_program(nc, A, out)
    r = run_bass_kernel_spmd(nc, [arrays], core_ids=[0])
    return r.results[0]["out"][:N]
```

```python
from contextlib import ExitStack

import numpy as np
import concourse.bass as bass
from concourse import mybir

F32 = mybir.dt.float32
F32R = mybir.dt.float32r
I32 = mybir.dt.int32
ALU = mybir.AluOpType
ACT = mybir.ActivationFunctionType
AX = mybir.AxisListType

P = 128
N, D, E = 3125, 256, 50000
KC = D // P
NW = -(-N // P)
NP = NW * P
GT = 5
NG = NW // GT
GN = GT * P
HALF = GN // 2
CT = 2
TE = CT * P
NT = -(-(E + 1) // TE)
EP = NT * TE
NI = NT + NW - 1
NC = NI * CT
RT, RC = 98, 2
GA = 64
IG = 4
JG = IG // CT
NIG = NC // IG
H, DH = 8, 32
SCALE = DH ** -0.5
CH = 16
CI = -(-NC // CH)
NCP = CI * CH
CE = CI * P
BIG = 3.0e38
LN2 = float(np.log(np.float32(2.0)))
EPS = 1e-5
NEXP = 8
TOPK = 2
HF = 4 * D
KEEP = N // 2 - 1
SP_CAP = 80.0
assert NW % GT == 0 and RT * RC == NT and NI % JG == 0 and RT <= P


class Core:

    def __init__(self, nc):
        self.nc = nc
        self.keep = ExitStack()
        self.gates = {}
        self.phase_sems = []

    def sb(self, name, shape, dt=F32, scope=None):
        return (scope or self.keep).enter_context(self.nc.sbuf_tensor(name, shape, dt))

    def ps(self, name, shape, dt=F32, scope=None):
        return (scope or self.keep).enter_context(self.nc.psum_tensor(name, shape, dt))

    def sem(self, name):
        kind = name.rsplit("_", 1)[-1]
        if not kind.endswith("gate"):
            self.phase_sems.append(self.nc.alloc_semaphore(name=name))
            return self.phase_sems[-1]
        if kind not in self.gates:
            self.gates[kind] = self.keep.enter_context(self.nc.semaphore(kind))
        return self.gates[kind]

    def recycle(self):
        self.nc.clear_and_free_semaphores(self.phase_sems)
        self.phase_sems = []
        self.nc.all_engine_barrier()


class Chain:

    def __init__(self, eng, sem):
        self.eng, self.sem, self.n = eng, sem, 0

    def __call__(self, ins):
        self.n += 1
        ins.then_inc(self.sem, 1)
        self.eng.wait_ge(self.sem, self.n)


def alone(eng, gate, *waits):
    for sem, value in waits:
        eng.wait_ge(sem, value)
    eng.sem_inc(gate, 1)


def bcast_rows(ap, parts):
    n = ap.shape[-1]
    return ap.rearrange("(a n) -> a n", a=1).broadcast_to([parts, n]) if len(ap.shape) == 1 else ap.broadcast_to([parts, n])


def prepare(c, A):
    nc = c.nc
    c.norm = Norm(c)
    c.norm.begin("n0")
    c.ident = c.sb("ident", [P, P])
    c.iota_n = c.sb("iota_n", [P, P])
    c.src_i = c.sb("src_i", [P, NCP], I32)
    c.dst_rel = c.sb("dst_rel", [P, NCP])
    c.coef = c.sb("coef", [P, NCP])
    c.node_id = c.sb("node_id", [P, NCP])
    c.seg_id = c.sb("seg_id", [P, NCP])
    c.t_row = c.sb("t_row", [1, NI], I32)
    c.w_row = c.sb("w_row", [1, NI], I32)
    with ExitStack() as s:
        rows_i = c.sb("rows_i", [RT, 2, RC, TE], I32, s)
        rows_f = c.sb("rows_f", [RT, 3, RC, TE], F32, s)
        whi = c.sb("whi", [RT, RC], I32, s)
        key = c.sb("key", [RT, RC], F32, s)
        tcol = c.sb("tcol", [RT, RC], F32, s)
        iota_i = c.sb("iota_i", [P, NI], F32, s)
        part = c.sb("part", [P, 1], F32, s)
        after = c.sb("after", [RT, RC, NI], F32, s)
        pick = c.sb("pick", [RT, RC, NI], F32, s)
        ones = c.sb("prep_ones", [RT, P], F32, s)
        t_all = c.sb("t_all", [P, NI], F32, s)
        w_all = c.sb("w_all", [P, NI], F32, s)
        w128 = c.sb("w128", [P, NI], F32, s)
        cols = c.sb("prep_cols", [P, 3, NC], F32, s)
        tmp = c.sb("prep_tmp", [P, NC], F32, s)
        tmp2 = c.sb("prep_tmp2", [P, NC], F32, s)
        period = c.sb("period", [P, NC], F32, s)
        whole = c.sb("whole", [P, NC], I32, s)
        sine = c.sb("sine", [P, NC], F32, s)
        p_t = c.ps("prep_t", [P, 512], F32, s)
        p_c = c.ps("prep_c", [P, 3, 512], F32, s)
        s_in, s_io = c.sem("prep_loaded"), c.sem("prep_iotas")
        s_d, s_a = c.sem("prep_chain"), c.sem("prep_after")
        s_t, s_pick, s_c = c.sem("prep_tiles"), c.sem("prep_picked"), c.sem("prep_columns")
        s_m, s_sin, s_x = c.sem("prep_phase"), c.sem("prep_sine"), c.sem("prep_x")
        with nc.Block() as block:
            @block.sync
            def _(sp):
                sp.dma_start(rows_i[:, 0], A["src"].rearrange("(c p) e -> p c e", p=RT)).then_inc(s_in, 16)
                sp.dma_start(rows_i[:, 1], A["dst"].rearrange("(c p) e -> p c e", p=RT)).then_inc(s_in, 16)
                sp.dma_start(rows_f[:, 2], A["edge_weight"].rearrange("(c p) e -> p c e", p=RT)).then_inc(s_in, 16)
                sp.dma_start(c.x[:, :, :], A["x"].rearrange("(t p) d -> p t d", p=P)).then_inc(s_x, 16)

            @block.gpsimd
            def _(pool):
                pool.memset(c.ident[:, :], 0.0).then_inc(s_io, 1)
                pool.iota(iota_i[:, :], pattern=[[1, NI]], base=0, channel_multiplier=0, allow_small_or_imprecise_dtypes=True).then_inc(s_io, 1)
                pool.iota(c.iota_n[:, :], pattern=[[1, P]], base=0, channel_multiplier=0, allow_small_or_imprecise_dtypes=True).then_inc(s_io, 1)
                pool.iota(tcol[:, :], pattern=[[RT, RC]], base=0, channel_multiplier=1, allow_small_or_imprecise_dtypes=True).then_inc(s_io, 1)
                pool.iota(part[:, :], pattern=[[1, 1]], base=0, channel_multiplier=1, allow_small_or_imprecise_dtypes=True).then_inc(s_io, 1)
                pool.memset(ones[:, :], 1.0).then_inc(s_io, 1)
                pool.wait_ge(s_io, 6)
                pool.affine_select(out=c.ident[:, :], in_=c.ident[:, :], compare_op=ALU.not_equal, fill=1.0,
                                   base=0, pattern=[[-1, P]], channel_multiplier=1).then_inc(s_io, 1)

            @block.vector
            def _(dve):
                link = Chain(dve, s_d)
                v = nc.vector
                dve.wait_ge(s_in, 48)
                dve.wait_ge(s_io, 7)
                link(v.tensor_scalar(whi[:, :], rows_i[:, 1, :, TE - 1], 7, None, ALU.logical_shift_right))
                link(v.tensor_copy(rows_f[:, 0:2], rows_i[:, :]))
                link(v.tensor_tensor(key[:, :], whi[:, :], tcol[:, :], ALU.add))
                for k in range(RC):
                    v.tensor_scalar(after[:, k, :], iota_i[0:RT, :], key[:, k:k + 1], None, ALU.is_gt).then_inc(s_a, 1)
                dve.wait_ge(s_t, 1)
                link(v.tensor_copy(t_all[:, :], p_t[:, 0:NI]))
                link(v.tensor_tensor(w_all[:, :], iota_i[:, :], t_all[:, :], ALU.subtract))
                link(v.tensor_scalar(w_all[:, :], w_all[:, :], 0.0, float(NW - 1), ALU.max, ALU.min))
                v.tensor_copy(c.t_row[:, :], t_all[0:1, :]).then_inc(s_pick, 1)
                v.tensor_copy(c.w_row[:, :], w_all[0:1, :]).then_inc(s_pick, 1)
                for k in range(RC):
                    v.tensor_scalar(pick[:, k, :], t_all[0:RT, :], tcol[:, k:k + 1], None, ALU.is_equal).then_inc(s_pick, 1)
                link(v.tensor_scalar(w128[:, :], w_all[:, :], float(P), None, ALU.mult))
                by_item = lambda t: t.rearrange("p (i s) -> p i s", s=CT)
                w128_c = w128[:, :].rearrange("p (i a) -> p i a", a=1).broadcast_to([P, NI, CT])
                link(v.tensor_scalar(by_item(c.node_id[:, 0:NC]), w128_c, part[:, 0:1], None, ALU.add))
                link(v.memset(c.seg_id[:, NC:NCP], 0.0))
                dve.wait_ge(s_x, 16)
                for t in range(NW):
                    c.norm.observe(t)
                c.norm.finish(dve)
                dve.wait_ge(s_c, 3)
                link(v.tensor_copy(cols[:, :, :], p_c[:, :, 0:NC]))
                link(v.tensor_scalar(period[:, :], cols[:, 2, :], 0.5, None, ALU.mult))
                link(v.tensor_copy(whole[:, :], period[:, :]))
                v.tensor_tensor(period[:, :], period[:, :], whole[:, :], ALU.subtract).then_inc(s_m, 1)
                link(v.tensor_copy(c.src_i[:, 0:NC], cols[:, 0, :]))
                link(v.tensor_tensor(by_item(c.dst_rel[:, 0:NC]), by_item(cols[:, 1, :]), w128_c, ALU.subtract))
                link(v.tensor_scalar(tmp[:, :], c.dst_rel[:, 0:NC], 0.0, None, ALU.is_ge))
                link(v.tensor_scalar(tmp2[:, :], c.dst_rel[:, 0:NC], float(P), None, ALU.is_lt))
                link(v.tensor_tensor(tmp[:, :], tmp[:, :], tmp2[:, :], ALU.mult))
                link(v.tensor_scalar(tmp2[:, :], cols[:, 1, :], 1.0, None, ALU.add))
                link(v.tensor_tensor(c.seg_id[:, 0:NC], tmp[:, :], tmp2[:, :], ALU.mult))
                dve.wait_ge(s_sin, 1)
                link(v.tensor_tensor(tmp[:, :], sine[:, :], sine[:, :], ALU.mult))
                link(v.tensor_scalar(c.coef[:, 0:NC], tmp[:, :], -0.5, 0.5, ALU.mult, ALU.add))

            @block.scalar
            def _(act):
                c.norm.root(act)
                act.wait_ge(s_m, 1)
                nc.scalar.activation(sine[:, :], period[:, :], ACT.Sin, scale=float(np.pi)).then_inc(s_sin, 1)

            @block.tensor
            def _(pe):
                pe.wait_ge(s_io, 7)
                for k in range(RC):
                    pe.wait_ge(s_a, k + 1)
                    last = nc.tensor.matmul(p_t[:, 0:NI], ones[:, :], after[:, k, :], start=(k == 0), stop=(k == RC - 1))
                last.then_inc(s_t, 1)
                pe.wait_ge(s_pick, 2 + RC)
                for a in range(3):
                    for h in range(CT):
                        for k in range(RC):
                            last = nc.tensor.matmul(p_c[:, a, h:NC:CT], rows_f[:, a, k, h * P:(h + 1) * P], pick[:, k, :], start=(k == 0), stop=(k == RC - 1))
                    last.then_inc(s_c, 1)


class Group:
    COUNT, UNROLL = NIG, 4

    def __init__(self, it, q):
        self.n = it * 4 + q
        self.slot, self.turn = q % 2, it * 2 + q // 2
        self.slot4, self.turn4 = q % 4, it + q // 4


class Window:
    COUNT, UNROLL = NW, GT

    def __init__(self, it, q):
        self.n = it * GT + q
        self.slot, self.turn = q % GT, it + q // GT
        self.bank = self.slot % 2
        self.back = (1, 3, 2, 2, 2)[self.slot]
        self.free = self.n - self.back + 1


def real(g):
    return not isinstance(g.n, int) or 0 <= g.n < g.COUNT


def need(eng, gate, *waits, own=False):
    waits = [(s, n) for s, n in waits if not isinstance(n, int) or n > 0]
    for s, n in waits:
        eng.wait_ge(s, n)
    if waits and not own:
        eng.sem_inc(gate, 1)


def rounds(eng, step, before, after, kind=Group):
    size = kind.UNROLL
    end = (kind.COUNT - before) // size
    for r in range(-before, size):
        step(lambda ahead: kind(0, r + ahead))
    with eng.Fori(1, end) as it:
        for q in range(size):
            step(lambda ahead: kind(it, q + ahead))
    for r in range(size * end, kind.COUNT + after + 1):
        step(lambda ahead: kind(0, r + ahead))


def gather(c, pool, g, idx, rows, table, s_rows, s_idx, s_used):
    need(pool, c.sem("poolgate"), (s_idx, g.n + 1), (s_used, g.n - 3))
    for j in range(IG):
        c.nc.gpsimd.indirect_dma_start(out=rows[:, g.slot4, j, :], out_offset=None, in_=table,
                                       in_offset=bass.IndirectOffsetOnAxis(ap=idx[:, g.slot4, j:j + 1], axis=0)).then_inc(s_rows[g.slot4], 16)


def source_index(c, act, g, idx, s_rows, s_idx):
    need(act, c.sem("actgate"), (s_rows[g.slot4], g.turn4 * 64))
    c.nc.scalar.copy(idx[:, g.slot4, :], c.src_i[:, bass.ds(g.n * IG, IG)]).then_inc(s_idx, 1)


def item_values(eng, g, row, most):
    return [eng.value_load(row[0:1, bass.ds(g.n * JG + j, 1)], min_val=0, max_val=most) for j in range(JG)]


def window(t, n):
    return t[:, bass.ds(n, 1), :].rearrange("p a d -> p (a d)")


class Norm:

    def __init__(self, c):
        self.c = c
        self.stat = c.sb("norm_stat", [P, NW, 6])
        self.mv = c.sb("norm_mv", [P, NW, 2])
        self.var = c.sb("norm_var", [P, NW])
        self.rstd = c.sb("norm_rstd", [P, NW])

    def begin(self, name):
        self.s_stat, self.s_inv, self.s_rstd = (self.c.sem(f"{name}_{n}") for n in ("stats", "inv", "rstd"))

    def observe(self, n):
        self.c.nc.vector.bn_stats(window(self.stat, n), window(self.c.x, n)).then_inc(self.s_stat, 1)

    def finish(self, dve):
        v = self.c.nc.vector
        dve.wait_ge(self.s_stat, NW)
        for t in range(NW):
            last = v.bn_aggr(self.mv[:, t, :], self.stat[:, t, :])
        last.then_inc(self.s_stat, 1)
        dve.wait_ge(self.s_stat, NW + 1)
        v.tensor_scalar(self.var[:, :], self.mv[:, :, 1], EPS, None, ALU.add).then_inc(self.s_stat, 1)
        dve.wait_ge(self.s_stat, NW + 2)
        v.reciprocal(self.var[:, :], self.var[:, :]).then_inc(self.s_inv, 1)

    def root(self, act):
        act.wait_ge(self.s_inv, 1)
        self.c.nc.scalar.activation(self.rstd[:, :], self.var[:, :], ACT.Sqrt).then_inc(self.s_rstd, 1)

    def one(self, n, out):
        return self.c.nc.vector.tensor_scalar(out, window(self.c.x, n), window(self.mv[:, :, 0:1], n),
                                              self.rstd[:, bass.ds(n, 1)], ALU.subtract, ALU.mult)


def transpose_window(nc, to, src, ident):
    for k in range(KC):
        last = nc.tensor.transpose(to[:, k, :], src[:, k * P:(k + 1) * P], ident[:, :])
    return last


def source_features(c, A):
    nc = c.nc
    with ExitStack() as s:
        xn = c.sb("n0_xn", [P, GT, D], F32, s)
        xT = c.sb("n0_xT", [P, GT, KC, P], F32, s)
        w = c.sb("n0_w", [P, KC, D], F32, s)
        ho = c.sb("n0_h", [P, NW, D], F32, s)
        tp = [c.ps(f"n0_tp{b}", [P, 4, P], F32, s) for b in range(2)]
        hp = [c.ps(f"n0_hp{b}", [P, 512], F32, s) for b in range(2)]
        s_w, s_t, s_xT, s_h, s_ho, s_st = (c.sem("n0_" + n) for n in ("weights", "transposed", "xT", "h", "hout", "stored"))
        s_xn, s_ag, s_dg = c.sem("n0_normed"), c.sem("n0_agate"), c.sem("n0_dgate")
        with nc.Block() as block:
            @block.sync
            def _(sp):
                sp.dma_start(w[:, :, :], A["g_w1T"].rearrange("(k p) n -> p k n", p=P)).then_inc(s_w, 16)
                for g in range(NG):
                    sp.wait_ge(s_ho, (g + 1) * GT)
                    sp.dma_start(c.h_dram.rearrange("(t p) d -> p t d", p=P)[:, g * GT:(g + 1) * GT, :], ho[:, g * GT:(g + 1) * GT, :]).then_inc(s_st, 16)
                sp.wait_ge(s_st, 16 * NG)

            @block.vector
            def _(dve):
                def step(at):
                    t = at(2)
                    if real(t):
                        need(dve, s_dg, (s_t, t.n - GT + 1))
                        c.norm.one(t.n, xn[:, t.slot, :]).then_inc(s_xn, 1)
                rounds(dve, step, 2, 0, Window)

            @block.tensor
            def _(pe):
                pe.wait_ge(s_w, 16)

                def step(at):
                    t = at(1)
                    if real(t):
                        need(pe, None, (s_xn, t.n + 1), (s_xT, t.free), own=True)
                        transpose_window(nc, tp[t.bank], xn[:, t.slot, :], c.ident).then_inc(s_t, 1)
                    t = at(0)
                    if real(t):
                        need(pe, None, (s_xT, t.n + 1), (s_ho, t.free), own=True)
                        for k in range(KC):
                            last = nc.tensor.matmul(hp[t.bank][:, 0:D], xT[:, t.slot, k, :], w[:, k, :], start=(k == 0), stop=(k == KC - 1))
                        last.then_inc(s_h, 1)
                rounds(pe, step, 1, 0, Window)

            @block.scalar
            def _(act):
                def step(at):
                    t = at(1)
                    if real(t):
                        need(act, s_ag, (s_t, t.n + 1), (s_h, t.n - GT + 1))
                        nc.scalar.copy(xT[:, t.slot, :, :], tp[t.bank][:, 0:KC, :]).then_inc(s_xT, 1)
                    t = at(0)
                    if real(t):
                        need(act, s_ag, (s_h, t.n + 1))
                        nc.scalar.copy(window(ho, t.n), hp[t.bank][:, 0:D]).then_inc(s_ho, 1)
                rounds(act, step, 1, 0, Window)


def edges_first(c, A):
    nc = c.nc
    W2 = IG * P
    with ExitStack() as s:
        fw1 = c.sb("e1_fw1", [P, D], F32, s)
        fb1 = c.sb("e1_fb1", [P, D], F32, s)
        w1a = c.sb("e1_w1a", [P, D], F32R, s)
        w1b = c.sb("e1_w1b", [P, D], F32R, s)
        fw2 = c.sb("e1_fw2", [P, KC, D], F32, s)
        w2h = c.sb("e1_w2h", [P, KC, D], F32R, s)
        w2l = c.sb("e1_w2l", [P, KC, D], F32R, s)
        bias = c.sb("e1_bias", [P, D], F32, s)
        b2hl = c.sb("e1_b2hl", [GA, D], F32R, s)
        share = c.sb("e1_share", [GA, P], F32R, s)
        mln2 = c.sb("e1_mln2", [P, P], F32, s)
        ea = c.sb("e1_ea", [GA, 2, W2], F32, s)
        eaa = c.sb("e1_eaa", [P, 2, W2], F32R, s)
        eab = c.sb("e1_eab", [P, 2, W2], F32R, s)
        soft = c.sb("e1_soft", [P, 2, KC * W2], F32, s)
        hid = c.sb("e1_hid", [P, 2, KC * W2], F32, s)
        hidh = c.sb("e1_hidh", [P, 2, KC * W2], F32R, s)
        hidl = c.sb("e1_hidl", [P, 2, KC * W2], F32R, s)
        idx = c.sb("e1_idx", [P, 4, IG], I32, s)
        rows = c.sb("e1_rows", [P, 4, IG, D], F32, s)
        msg = c.sb("e1_msg", [P, 2, IG, D], F32, s)
        hot = c.sb("e1_hot", [P, 2, IG, P], F32, s)
        zp = [c.ps(f"e1_z{p}", [P, KC * W2], F32, s) for p in range(2)]
        wp = c.ps("e1_w", [P, IG * D], F32, s)
        ap = [c.ps(f"e1_agg{p}", [P, JG * D], F32, s) for p in range(2)]
        s_ld, s_b, s_split, s_cst, s_zero = (c.sem("e1_" + n) for n in ("loaded", "biassum", "weightsplit", "constants", "zeroed"))
        s_ea = [c.sem(f"e1_ea{p}") for p in range(2)]
        s_rows = [c.sem(f"e1_rows{p}") for p in range(4)]
        s_idx, s_ag, s_pg, s_dg = c.sem("e1_idx"), c.sem("e1_agate"), c.sem("e1_pgate"), c.sem("e1_dgate")
        s_eh, s_el, s_z, s_exp, s_ln, s_hid, s_hh, s_hl = (c.sem("e1_" + n) for n in ("eahigh", "ealow", "z", "exp", "ln", "hid", "hidhigh", "hidlow"))
        s_w, s_msg, s_agg, s_acc = (c.sem("e1_" + n) for n in ("w", "msg", "agg", "acc"))
        with nc.Block() as block:
            @block.sync
            def _(sp):
                sp.dma_start(fw1[0:GA, :], A["g_fw1T"][0:GA]).then_inc(s_ld, 16)
                sp.dma_start(fw1[GA:P, :], A["g_fw1T"][0:GA]).then_inc(s_ld, 16)
                sp.dma_start(fb1[GA:P, :], A["g_fw1T"][GA:GA + 1].broadcast_to([GA, D])).then_inc(s_ld, 16)
                sp.dma_start(fw2[:, :, :], A["g_fw2T"].rearrange("(k p) n -> p k n", p=P)).then_inc(s_ld, 16)
                sp.dma_start(bias[:, :], bcast_rows(A["g_fb2"], P)).then_inc(s_ld, 16)

                def load(at):
                    g = at(7)
                    if not real(g):
                        return
                    tiles = item_values(sp, g, c.t_row, NT - 1)
                    need(sp, None, (s_el, g.n - 1), own=True)
                    for j in range(JG):
                        sp.dma_start(ea[:, g.slot, j * TE:(j + 1) * TE], A["eaT"][:, bass.ds(tiles[j] * TE, TE)]).then_inc(s_ea[g.slot], 16)
                rounds(sp, load, 7, 0)

            @block.gpsimd
            def _(pool):
                link = Chain(pool, s_cst)
                link(nc.gpsimd.memset(mln2[:, :], -LN2))
                link(nc.gpsimd.memset(share[:, :].bitcast(F32), 1.0 / 32))
                link(nc.gpsimd.memset(eab[GA:P, :, :].bitcast(F32), 1.0 / 32))

                def step(at):
                    g = at(3)
                    if real(g):
                        gather(c, pool, g, idx, rows, c.h_dram, s_rows, s_idx, s_msg)
                    g = at(6)
                    if real(g):
                        need(pool, s_pg, (s_eh, g.n + 1), (s_el, g.n))
                        nc.gpsimd.tensor_tensor(eaa[GA:P, g.slot, :], ea[:, g.slot, :], eaa[0:GA, g.slot, :].bitcast(F32), ALU.subtract).then_inc(s_el, 1)
                rounds(pool, step, 6, 0)

            @block.tensor
            def _(pe):
                mm = nc.tensor.matmul
                pe.wait_ge(s_ld, 80)
                pe.wait_ge(s_cst, 3)
                for k in range(KC):
                    last = mm(wp[:, 0:D], mln2[:, :], fw2[:, k, :], start=(k == 0), stop=(k == KC - 1))
                last.then_inc(s_b, 1)
                pe.wait_ge(s_split, 3)

                def step(at):
                    g = at(4)
                    if real(g):
                        need(pe, None, (s_el, g.n + 1), (s_hid, g.n - 1), own=True)
                        for m in range(KC):
                            z, cols = zp[g.slot][:, m * W2:(m + 1) * W2], slice(m * P, (m + 1) * P)
                            mm(z, w1b[:, cols], eab[:, g.slot, :], start=True, stop=False)
                            last = mm(z, w1a[:, cols], eaa[:, g.slot, :], start=False, stop=True)
                        last.then_inc(s_z, 1)
                    g = at(1)
                    if real(g):
                        need(pe, None, (s_hl, g.n + 1), (s_msg, g.n), own=True)
                        if isinstance(g.n, int) and g.n == 0:
                            pe.wait_ge(s_split, 8)
                        for j in range(IG):
                            w = wp[:, j * D:(j + 1) * D]
                            cols = [slice((k * IG + j) * P, (k * IG + j + 1) * P) for k in range(KC)]
                            for k in range(KC):
                                mm(w, hidl[:, g.slot, cols[k]], w2h[:, k, :], start=(k == 0), stop=False)
                                mm(w, hidh[:, g.slot, cols[k]], w2l[:, k, :], start=False, stop=False)
                            mm(w, share[:, :], b2hl[:, :], start=False, stop=False)
                            for k in range(KC):
                                last = mm(w, hidh[:, g.slot, cols[k]], w2h[:, k, :], start=False, stop=(k == KC - 1))
                        last.then_inc(s_w, 1)
                    g = at(0)
                    if real(g):
                        need(pe, None, (s_msg, g.n + 1), (s_acc, (g.n - 1) * JG), own=True)
                        for j in range(IG):
                            h, half = divmod(j, CT)
                            last = mm(ap[g.slot][:, h * D:(h + 1) * D], hot[:, g.slot, j, :], msg[:, g.slot, j, :], start=(half == 0), stop=(half == CT - 1))
                        last.then_inc(s_agg, 1)
                rounds(pe, step, 4, 0)

            @block.scalar
            def _(act):
                act.preload_act_table_set("natural_log_exp_and_others")
                act.wait_ge(s_cst, 3)

                def step(at):
                    g = at(4)
                    if real(g):
                        need(act, s_ag, (s_z, g.n + 1))
                        nc.scalar.activation(soft[:, g.slot, :], zp[g.slot][:, :], ACT.Exp).then_inc(s_exp, 1)
                        need(act, s_ag, (s_exp, g.n + 1))
                        nc.scalar.activation(soft[:, g.slot, :], soft[:, g.slot, :], ACT.Ln, bias=1.0).then_inc(s_ln, 1)
                    g = at(6)
                    if real(g):
                        need(act, s_ag, (s_ea[g.slot], (g.turn + 1) * 16 * JG), (s_z, g.n - 1))
                        nc.scalar.copy(eab[0:GA, g.slot, :], ea[:, g.slot, :])
                        nc.scalar.copy(eaa[0:GA, g.slot, :], ea[:, g.slot, :]).then_inc(s_eh, 1)
                    g = at(4)
                    if real(g):
                        source_index(c, act, g, idx, s_rows, s_idx)
                    g = at(3)
                    if real(g):
                        need(act, s_ag, (s_hid, g.n + 1), (s_w, g.n - 1))
                        nc.scalar.copy(hidh[:, g.slot, :], hid[:, g.slot, :]).then_inc(s_hh, 1)
                rounds(act, step, 6, 0)

            @block.vector
            def _(dve):
                v = nc.vector
                high, low = lambda to, x: v.tensor_copy(to, x), lambda to, x, h: v.tensor_tensor(to, x, h.bitcast(F32), ALU.subtract)
                link = Chain(dve, s_split)
                dve.wait_ge(s_ld, 80)
                high(w1a[:, :], fw1[:, :])
                link(high(w1b[GA:P, :], fb1[GA:P, :]))
                link(low(w1b[0:GA, :], fw1[0:GA, :], w1a[0:GA, :]))
                link(low(w1b[96:P, :], fb1[96:P, :], w1b[96:P, :]))
                link(high(w2h[:, :, :], fw2[:, :, :]))
                link(low(w2l[:, :, :], fw2[:, :, :], w2h[:, :, :]))
                dve.wait_ge(s_b, 1)
                link(v.tensor_tensor(bias[:, :], bias[:, :], wp[:, 0:D], ALU.add))
                link(high(b2hl[:, :], bias[0:GA, :]))
                link(low(b2hl[32:GA, :], bias[32:GA, :], b2hl[32:GA, :]))
                v.memset(c.agg[:, :, 0:D], 0.0).then_inc(s_zero, 1)

                def one_hot(g):
                    if real(g):
                        need(dve, s_dg, (s_agg, g.n - 1))
                        for j in range(IG):
                            i = g.n * IG + j
                            v.tensor_scalar(hot[:, g.slot, j, :], c.iota_n[:, :], c.dst_rel[:, bass.ds(i, 1)], c.coef[:, bass.ds(i, 1)],
                                            ALU.is_equal, ALU.mult)

                def step(at):
                    g = at(-1)
                    if real(g):
                        wins = item_values(dve, g, c.w_row, NW - 1)
                    for j in range(JG):
                        if real(g):
                            to = c.agg[:, bass.ds(wins[j], 1), 0:D].rearrange("p a d -> p (a d)")
                            need(dve, s_dg, (s_agg, g.n + 1), (s_acc, g.n * JG + j), (s_zero, 1))
                            v.tensor_tensor(to, to, ap[g.slot][:, j * D:(j + 1) * D], ALU.add).then_inc(s_acc, 1)
                        if j == 0:
                            one_hot(at(1))
                    h = at(3)
                    if real(h):
                        need(dve, s_dg, (s_ln, h.n + 1), (s_hl, h.n - 1))
                        v.scalar_tensor_tensor(hid[:, h.slot, :], soft[:, h.slot, :], SP_CAP, zp[h.slot][:, :], ALU.min, ALU.max).then_inc(s_hid, 1)
                    g, h = at(1), at(2)
                    if real(h):
                        need(dve, s_dg, (s_hh, h.n + 1))
                        low(hidl[:, h.slot, :], hid[:, h.slot, :], hidh[:, h.slot, :]).then_inc(s_hl, 1)
                    if real(g):
                        need(dve, s_dg, (s_w, g.n + 1), (s_rows[g.slot4], (g.turn4 + 1) * 64))
                        v.tensor_tensor(msg[:, g.slot, :, :], wp[:, :].rearrange("p (a d) -> p a d", a=IG), rows[:, g.slot4, :, :], ALU.mult).then_inc(s_msg, 1)
                rounds(dve, step, 3, 1)


def nodes_first(c, A):
    nc = c.nc
    c.norm.begin("n1")
    with ExitStack() as s:
        w2 = c.sb("u_w2", [P, KC, D], F32, s)
        w3 = c.sb("u_w3", [P, KC, D], F32, s)
        b2 = c.sb("u_b2", [P, KC], F32, s)
        bias = c.sb("u_bias", [P, D], F32, s)
        mln2 = c.sb("u_mln2", [P, P], F32, s)
        ag = c.sb("u_agg", [P, GT, D], F32, s)
        aT = c.sb("u_aggT", [P, GT, KC, P], F32, s)
        z, soft, hid = (c.sb("u_" + n, [P, GT, KC, P], F32, s) for n in ("z", "soft", "hid"))
        tp, zp, op = ([c.ps(f"u_{n}{b}", [P, 512], F32, s) for b in range(2)] for n in ("tp", "zp", "op"))
        names = ("loaded", "const", "sums", "bias", "agg", "transposed", "aggT", "z", "zbias", "exp", "ln", "hid", "rows", "added", "x", "dgate", "agate", "pgate")
        s_ld, s_cst, s_sum, s_bias, s_ag, s_t, s_aT, s_z, s_zb, s_e, s_ln, s_hid, s_r, s_add, s_x, s_dg, s_agt, s_pg = (c.sem("u_" + n) for n in names)
        by_chunk = lambda t: t[:, 0:D].rearrange("p (k n) -> p k n", k=KC)
        with nc.Block() as block:
            @block.sync
            def _(sp):
                sp.dma_start(w3[:, :, :], A["g_w3T"].rearrange("(k p) n -> p k n", p=P)).then_inc(s_ld, 16)
                sp.dma_start(w2[:, :, :], A["g_w2T"].rearrange("(k p) n -> p k n", p=P)).then_inc(s_ld, 16)
                sp.dma_start(b2[:, :], A["g_b2"]).then_inc(s_ld, 16)
                sp.dma_start(bias[:, :], bcast_rows(A["g_b3"], P)).then_inc(s_ld, 16)

            @block.gpsimd
            def _(pool):
                nc.gpsimd.memset(mln2[:, :], -LN2).then_inc(s_cst, 1)
                pool.wait_ge(s_cst, 1)

                def step(at):
                    t = at(3)
                    if real(t):
                        need(pool, s_pg, (s_t, t.n - GT + 1), (s_add, t.n))
                        nc.gpsimd.tensor_copy(ag[:, t.slot, :], c.agg[:, bass.ds(t.n, 1), 0:D].rearrange("p a d -> p (a d)")).then_inc(s_ag, 1)
                        need(pool, s_pg, (s_ag, t.n + 1), (s_bias, 1))
                        nc.gpsimd.tensor_tensor(window(c.x, t.n), window(c.x, t.n), bias[:, :], ALU.add).then_inc(s_add, 1)
                rounds(pool, step, 3, 0, Window)

            @block.tensor
            def _(pe):
                mm = nc.tensor.matmul
                pe.wait_ge(s_ld, 64)
                pe.wait_ge(s_cst, 1)
                for k in range(KC):
                    last = mm(op[0][:, 0:D], mln2[:, :], w3[:, k, :], start=(k == 0), stop=(k == KC - 1))
                last.then_inc(s_sum, 1)
                pe.wait_ge(s_bias, 1)

                def step(at):
                    t = at(2)
                    if real(t):
                        need(pe, None, (s_ag, t.n + 1), (s_aT, t.free), own=True)
                        transpose_window(nc, by_chunk(tp[t.bank]), ag[:, t.slot, :], c.ident).then_inc(s_t, 1)
                    t = at(1)
                    if real(t):
                        need(pe, None, (s_aT, t.n + 1), (s_e, t.free), (s_zb, t.free), own=True)
                        for m in range(KC):
                            for k in range(KC):
                                last = mm(zp[t.bank][:, m * P:(m + 1) * P], w2[:, k, m * P:(m + 1) * P], aT[:, t.slot, k, :], start=(k == 0), stop=(k == KC - 1))
                        last.then_inc(s_z, 1)
                    t = at(-1)
                    if real(t):
                        need(pe, None, (s_hid, t.n + 1), (s_x, t.free), own=True)
                        for k in range(KC):
                            last = mm(op[t.bank][:, 0:D], hid[:, t.slot, k, :], w3[:, k, :], start=(k == 0), stop=(k == KC - 1))
                        last.then_inc(s_r, 1)
                rounds(pe, step, 2, 1, Window)

            @block.scalar
            def _(act):
                act.preload_act_table_set("natural_log_exp_and_others")
                act.wait_ge(s_ld, 64)

                def step(at):
                    t = at(2)
                    if real(t):
                        need(act, s_agt, (s_t, t.n + 1), (s_z, t.n - GT + 1))
                        nc.scalar.copy(aT[:, t.slot, :, :], by_chunk(tp[t.bank])).then_inc(s_aT, 1)
                    t = at(1)
                    if real(t):
                        need(act, s_agt, (s_zb, t.n + 1), (s_hid, t.n - GT + 1))
                        nc.scalar.activation(soft[:, t.slot, :, :], z[:, t.slot, :, :], ACT.Exp).then_inc(s_e, 1)
                        need(act, s_agt, (s_e, t.n + 1))
                        nc.scalar.activation(soft[:, t.slot, :, :], soft[:, t.slot, :, :], ACT.Ln, bias=1.0).then_inc(s_ln, 1)
                rounds(act, step, 2, 0, Window)
                c.norm.root(act)

            @block.vector
            def _(dve):
                v = nc.vector
                dve.wait_ge(s_ld, 64)
                dve.wait_ge(s_sum, 1)
                v.tensor_tensor(bias[:, :], bias[:, :], op[0][:, 0:D], ALU.add).then_inc(s_bias, 1)
                b2_b = b2[:, :].rearrange("p (k a) -> p k a", a=1).broadcast_to([P, KC, P])

                def step(at):
                    t = at(1)
                    if real(t):
                        need(dve, s_dg, (s_z, t.n + 1), (s_hid, t.n - GT + 1))
                        v.tensor_tensor(z[:, t.slot, :, :], by_chunk(zp[t.bank]), b2_b, ALU.add).then_inc(s_zb, 1)
                    t = at(-1)
                    if real(t):
                        need(dve, s_dg, (s_r, t.n + 1), (s_add, t.n + 1))
                        v.tensor_tensor(window(c.x, t.n), window(c.x, t.n), op[t.bank][:, 0:D], ALU.add).then_inc(s_x, 1)
                    t = at(0)
                    if real(t):
                        need(dve, s_dg, (s_ln, t.n + 1), (s_zb, t.n + 1), (s_r, t.n - GT + 1))
                        v.scalar_tensor_tensor(hid[:, t.slot, :, :], soft[:, t.slot, :, :], SP_CAP, z[:, t.slot, :, :], ALU.min, ALU.max).then_inc(s_hid, 1)
                    t = at(-2)
                    if real(t):
                        need(dve, s_dg, (s_x, t.n + 1))
                        c.norm.observe(t.n)
                rounds(dve, step, 1, 2, Window)
                c.norm.finish(dve)


def experts(c, A, routed):
    nc = c.nc
    name = "m_" if routed else "f_"
    NB = NEXP if routed else HF // D
    NB2 = NB if routed else 1
    gelu = ACT.Gelu if routed else ACT.Gelu_apprx_tanh
    turns = {2 + j: [j] for j in range(GT)} if routed else {1: [0, 1], 2: [2, 3], 3: [4]}
    SLOTS = 4
    with ExitStack() as s:
        stage = c.sb(name + "stage", [P, SLOTS, KC, D], F32, s)
        w1h, w1l, w2h, w2l = (c.sb(name + n, [P, NB, KC, D], F32R, s) for n in ("w1h", "w1l", "w2h", "w2l"))
        b1 = c.sb(name + "b1", [P, NB * KC], F32, s)
        b2 = c.sb(name + "b2", [GA, NB2, D], F32, s)
        b2hl = c.sb(name + "b2hl", [GA, NB2, D], F32R, s)
        share = c.sb(name + "share", [GA, P], F32R, s)
        tok = c.sb(name + "tok", [P, GT, D], F32, s)
        nextT = c.sb(name + "nextT", [P, KC * GN], F32, s)
        xTh, xTl = (c.sb(name + n, [P, KC * GN], F32R, s) for n in ("xTh", "xTl"))
        hid = c.sb(name + "hid", [P, 2, KC * GN], F32, s)
        hidh, hidl = (c.sb(name + n, [P, 2, KC * GN], F32R, s) for n in ("hidh", "hidl"))
        hp = c.ps(name + "hp", [P, KC, 2, 512], F32, s)
        yp = c.ps(name + "yp", [P, 3 * 512], F32, s)
        tp = c.ps(name + "tp", [P, 2, KC, P], F32, s)
        lp = tp[:, 1, 0, 0:GT * NEXP]
        sems = lambda *ns: (c.sem(name + n) for n in ns)
        s_ld, s_cst, s_wt, s_t, s_xc, s_xT, s_h, s_hid, s_lo, s_y, s_acc, s_dg, s_ag = sems(
            "loaded", "const", "weights", "transposed", "nextT", "xT", "h", "hid", "hidlow", "y", "acc", "dgate", "agate")
        s_b2, s_hi, s_res, s_tok = sems("biases", "xThigh", "residual", "tok")
        s_st = [c.sem(f"{name}staged{n}") for n in range(SLOTS)]
        if routed:
            c.norm.begin("n2")
            rw = c.sb(name + "rw", [P, KC, NEXP], F32, s)
            lower = c.sb(name + "lower", [P, NEXP, NEXP], F32, s)
            lg, pr, comb, gates = (c.sb(name + n, [P, GT, NEXP], F32, s) for n in ("lg", "pr", "comb", "gates"))
            top = c.sb(name + "top", [P, GT], F32, s)
            gt = c.sb(name + "gt", [P, GT, NEXP, NEXP], F32, s)
            eq = c.sb(name + "eq", [P, GT, NEXP, NEXP], F32, s)
            s_lg, s_sub, s_exp, s_r, s_comb = sems("logits", "sub", "exp", "routing", "comb")
        loaded = 16 * (3 if routed else 2)
        ROUTING = 14
        first = lambda g: isinstance(g, int) and g == 0
        final = lambda g: isinstance(g, int) and g == NG - 1

        def all_groups(eng, group):
            group(0)
            with eng.Fori(1, NG - 1) as g:
                group(g)
            group(NG - 1)

        with nc.Block() as block:
            @block.sync
            def _(sp):
                if routed:
                    sp.dma_start(rw[:, :, :], A["r_wT"].rearrange("(k p) n -> p k n", p=P)).then_inc(s_ld, 16)
                    sp.dma_start(b2[:, :, :], A["m_b2"].rearrange("(a e) d -> a e d", a=1).broadcast_to([GA, NB, D])).then_inc(s_ld, 16)
                    sp.dma_start(b1[:, :], A["m_b1"]).then_inc(s_ld, 16)
                else:
                    sp.dma_start(b2[:, 0, :], bcast_rows(A["f_b2"], GA)).then_inc(s_ld, 16)
                    sp.dma_start(b1[:, :], A["f_b1"]).then_inc(s_ld, 16)
                for n in range(2 * NB):
                    e, layer = divmod(n, 2)
                    if routed:
                        w = A[("m_w1", "m_w2")[layer]][e]
                    else:
                        w = A["f_w2"][e * D:(e + 1) * D, :] if layer else A["f_w1"][:, e * D:(e + 1) * D]
                    if n >= SLOTS:
                        sp.wait_ge(s_wt, 2 * (n - SLOTS + 1))
                    sp.dma_start(stage[:, n % SLOTS], w.rearrange("(k p) n -> p k n", p=P)).then_inc(s_st[n % SLOTS], 16)
                if not routed:
                    s_out = c.sem("stored")
                    for g in range(NG):
                        sp.wait_ge(s_acc, (g + 1) * NB)
                        sp.dma_start(c.out.rearrange("(t p) d -> p t d", p=P)[:, g * GT:(g + 1) * GT, :], c.x[:, g * GT:(g + 1) * GT, :]).then_inc(s_out, 16)
                    sp.wait_ge(s_out, 16 * NG)

            @block.gpsimd
            def _(pool):
                link = Chain(pool, s_cst)
                link(nc.gpsimd.memset(share[:, :].bitcast(F32), 1.0 / 32))
                if routed:
                    link(pool.iota(lower[:, :, :], pattern=[[-1, NEXP], [1, NEXP]], base=0, channel_multiplier=0,
                                   allow_small_or_imprecise_dtypes=True))
                for n in range(2 * NB):
                    e, layer = divmod(n, 2)
                    high, low = ((w1h, w1l), (w2h, w2l))[layer]
                    pool.wait_ge(s_st[n % SLOTS], 16 * (n // SLOTS + 1))
                    nc.gpsimd.tensor_copy(high[:, e], stage[:, n % SLOTS]).then_inc(s_wt, 1)
                    pool.wait_ge(s_wt, 2 * n + 1)
                    nc.gpsimd.tensor_tensor(low[:, e], stage[:, n % SLOTS], high[:, e].bitcast(F32), ALU.subtract).then_inc(s_wt, 1)
                    pool.wait_ge(s_wt, 2 * n + 2)

            @block.tensor
            def _(pe):
                mm = nc.tensor.matmul

                def transpose(n, windows):
                    need(pe, None, (s_tok, n + 1), (s_xc, n * GT + windows[0]), *([(s_sub, n)] if routed else []), own=True)
                    for j in windows:
                        for k in range(KC):
                            last = nc.tensor.transpose(tp[:, j - windows[0], k, :], tok[:, j, k * P:(k + 1) * P], c.ident[:, :])
                        last.then_inc(s_t, 1)

                def logits(n):
                    need(pe, None, (s_xc, (n + 1) * GT), own=True)
                    for j in range(GT):
                        for k in range(KC):
                            last = mm(lp[:, j * NEXP:(j + 1) * NEXP], nextT[:, k * GN + j * P:k * GN + (j + 1) * P], rw[:, k, :],
                                      start=(k == 0), stop=(k == KC - 1))
                    last.then_inc(s_lg, 1)

                def up(g, e):
                    need(pe, None, (s_xT, g + 1), (s_hid, g * NB + e), own=True)
                    if first(g):
                        pe.wait_ge(s_wt, 4 * e + 2)
                    for m in range(KC):
                        for h in range(2):
                            z = hp[:, m, h, 0:HALF]
                            cols = [slice(k * GN + h * HALF, k * GN + (h + 1) * HALF) for k in range(KC)]
                            out = slice(m * P, (m + 1) * P)
                            for k in range(KC):
                                mm(z, w1h[:, e, k, out], xTl[:, cols[k]], start=(k == 0), stop=False)
                                mm(z, w1l[:, e, k, out], xTh[:, cols[k]], start=False, stop=False)
                            for k in range(KC):
                                last = mm(z, w1h[:, e, k, out], xTh[:, cols[k]], start=False, stop=(k == KC - 1))
                    last.then_inc(s_h, 1)

                def down(g, e):
                    need(pe, None, (s_lo, g * NB + e + 1), (s_acc, g * NB + e), own=True)
                    if first(g):
                        pe.wait_ge(s_wt, 4 * e + 4)
                    for j in range(GT):
                        y = yp[:, j * D:(j + 1) * D]
                        cols = [slice(k * GN + j * P, k * GN + (j + 1) * P) for k in range(KC)]
                        for k in range(KC):
                            mm(y, hidl[:, e % 2, cols[k]], w2h[:, e, k, :], start=(k == 0), stop=False)
                            mm(y, hidh[:, e % 2, cols[k]], w2l[:, e, k, :], start=False, stop=False)
                        if e < NB2:
                            mm(y, share[:, :], b2hl[:, e, :], start=False, stop=False)
                        for k in range(KC):
                            last = mm(y, hidh[:, e % 2, cols[k]], w2h[:, e, k, :], start=False, stop=(k == KC - 1))
                    last.then_inc(s_y, 1)

                def group(g):
                    for e in range(NB):
                        if e in turns and not final(g):
                            transpose(g + 1, turns[e])
                        up(g, e)
                        if routed and e == NB - 1 and not final(g):
                            logits(g + 1)
                        if e >= 1:
                            down(g, e - 1)
                        elif not first(g):
                            down(g - 1, NB - 1)
                    if first(g):
                        pe.wait_ge(s_wt, 4 * NB)
                pe.wait_ge(s_ld, loaded)
                for windows in turns.values():
                    transpose(0, windows)
                if routed:
                    logits(0)
                pe.wait_ge(s_b2, 3 if routed else 2)
                pe.wait_ge(s_cst, 1)
                all_groups(pe, group)
                down(NG - 1, NB - 1)

            @block.scalar
            def _(act):
                a = nc.scalar

                def copies(n, windows):
                    need(act, s_ag, (s_t, n * GT + windows[-1] + 1), (s_xT, n), *([(s_lg, n)] if routed else []))
                    for j in windows:
                        a.copy(nextT[:, :].rearrange("p (k n) -> p k n", k=KC)[:, :, j * P:(j + 1) * P], tp[:, j - windows[0], :, :]).then_inc(s_xc, 1)

                def exponentials(n):
                    need(act, s_ag, (s_sub, n + 1))
                    a.activation(lg[:, :, :], lg[:, :, :], ACT.Exp).then_inc(s_exp, 1)

                def group(g):
                    for e in range(NB):
                        if e in turns and not final(g):
                            copies(g + 1, turns[e])
                        step = g * NB + e
                        need(act, s_ag, (s_h, step + 1), (s_lo, step - 1), (s_y, step - 1))
                        for to in (hid, hidh):
                            for m in range(KC):
                                last = a.activation(to[:, e % 2, m * GN:(m + 1) * GN].rearrange("p (h n) -> p h n", h=2), hp[:, m, :, 0:HALF], gelu,
                                                    bias=b1[:, e * KC + m:e * KC + m + 1])
                        last.then_inc(s_hid, 1)
                    if routed and not final(g):
                        exponentials(g + 1)
                act.wait_ge(s_ld, loaded)
                for windows in turns.values():
                    copies(0, windows)
                if routed:
                    exponentials(0)
                all_groups(act, group)
                if routed:
                    c.norm.root(act)

            @block.vector
            def _(dve):
                v = nc.vector
                high, low = lambda to, x: v.tensor_copy(to, x), lambda to, x, h: v.tensor_tensor(to, x, h.bitcast(F32), ALU.subtract)

                def make_tok(n):
                    if routed:
                        need(dve, s_dg, (s_t, n * GT), (s_res, n))
                        for j in range(GT):
                            last = c.norm.one(n * GT + j, tok[:, j, :])
                        last.then_inc(s_tok, 1)
                    else:
                        need(dve, s_dg, (s_t, n * GT))
                        v.tensor_copy(tok[:, :, :], c.tok[:, bass.ds(n * GT, GT), :]).then_inc(s_tok, 1)

                def split(n):
                    need(dve, s_dg, (s_xc, (n + 1) * GT), (s_h, n * NB))
                    high(xTh[:, :], nextT[:, :]).then_inc(s_hi, 1)
                    need(dve, s_dg, (s_hi, n + 1))
                    low(xTl[:, :], nextT[:, :], xTh[:, :]).then_inc(s_xT, 1)

                def linked(g, n):
                    def link(ins):
                        count[0] += 1
                        ins.then_inc(s_r, 1)
                        alone(dve, s_dg, (s_r, g * ROUTING + count[0]))
                    count = [n]
                    return link, count
                wide = lambda t: t.rearrange("p (t a) -> p t a", a=1).broadcast_to([P, GT, NEXP])

                def shift(n):
                    link, _ = linked(n, 0)
                    need(dve, s_dg, (s_lg, n + 1))
                    link(v.tensor_copy(pr[:, :, :], lp.rearrange("p (t e) -> p t e", t=GT)))
                    link(v.tensor_reduce(top[:, :], pr[:, :, :], AX.X, ALU.max))
                    v.tensor_tensor(lg[:, :, :], pr[:, :, :], wide(top[:, :]), ALU.subtract).then_inc(s_sub, 1)

                def route(g):
                    link, count = linked(g, 2)
                    need(dve, s_dg, (s_exp, g + 1), (s_comb, g))
                    link(v.tensor_reduce(top[:, :], lg[:, :, :], AX.X, ALU.add))
                    link(v.reciprocal(top[:, :], top[:, :]))
                    link(v.tensor_tensor(pr[:, :, :], lg[:, :, :], wide(top[:, :]), ALU.mult))
                    other = pr[:, :, :].rearrange("p t (a f) -> p t a f", a=1).broadcast_to([P, GT, NEXP, NEXP])
                    own = pr[:, :, :].rearrange("p t (e a) -> p t e a", a=1).broadcast_to([P, GT, NEXP, NEXP])
                    below = lower[:, :, :].rearrange("p (a e) f -> p a e f", a=1).broadcast_to([P, GT, NEXP, NEXP])
                    v.tensor_tensor(gt[:, :, :, :], other, own, ALU.is_gt)
                    link(v.tensor_tensor(eq[:, :, :, :], other, own, ALU.is_equal))
                    link(v.tensor_tensor(eq[:, :, :, :], eq[:, :, :, :], below, ALU.mult))
                    link(v.tensor_tensor(gt[:, :, :, :], gt[:, :, :, :], eq[:, :, :, :], ALU.add))
                    link(v.tensor_reduce(comb[:, :, :], gt[:, :, :, :], AX.X, ALU.add))
                    link(v.scalar_tensor_tensor(comb[:, :, :], comb[:, :, :], TOPK - 0.5, pr[:, :, :], ALU.is_lt, ALU.mult))
                    link(v.tensor_reduce(top[:, :], comb[:, :, :], AX.X, ALU.add))
                    link(v.tensor_scalar(top[:, :], top[:, :], 1e-12, None, ALU.max))
                    link(v.reciprocal(top[:, :], top[:, :]))
                    link(v.tensor_tensor(comb[:, :, :], comb[:, :, :], wide(top[:, :]), ALU.mult))
                    assert count[0] == ROUTING, count[0]

                def add_rows(g, e):
                    need(dve, s_dg, (s_y, g * NB + e + 1), (s_acc, g * NB + e), (s_res, g + 1), *([(s_comb, g + 1)] if routed else []))
                    for j in range(GT):
                        gate = gates[:, j, e:e + 1] if routed else c.gate[:, bass.ds(g * GT + j, 1)]
                        to = window(c.x, g * GT + j)
                        last = v.scalar_tensor_tensor(to, yp[:, j * D:(j + 1) * D], gate, to, ALU.mult, ALU.add)
                    last.then_inc(s_acc, 1)

                def observe(g):
                    need(dve, s_dg, (s_acc, (g + 1) * NB))
                    for j in range(GT):
                        c.norm.observe(g * GT + j)

                def group(g):
                    for e in range(NB):
                        if e >= 2:
                            add_rows(g, e - 2)
                        elif not first(g):
                            add_rows(g - 1, NB + e - 2)
                        if routed and e == 0:
                            route(g)
                        if routed and e == 1:
                            need(dve, s_dg, (s_acc, g * NB), (s_r, (g + 1) * ROUTING))
                            v.tensor_copy(gates[:, :, :], comb[:, :, :]).then_inc(s_comb, 1)
                        if e == 1:
                            need(dve, s_dg, (s_acc, g * NB))
                            xg = c.x[:, bass.ds(g * GT, GT), :]
                            v.tensor_tensor(xg, xg, tok[:, :, :] if routed else c.tok[:, bass.ds(g * GT, GT), :], ALU.add).then_inc(s_res, 1)
                        if e == (1 if routed else 0) and not final(g):
                            make_tok(g + 1)
                        if routed and e == 2 and not first(g):
                            observe(g - 1)
                        if e == NB - 1 and not final(g):
                            split(g + 1)
                            if routed:
                                shift(g + 1)
                        need(dve, s_dg, (s_hid, g * NB + e + 1), (s_y, g * NB + e - 1))
                        low(hidl[:, e % 2, :], hid[:, e % 2, :], hidh[:, e % 2, :]).then_inc(s_lo, 1)
                make_tok(0)
                dve.wait_ge(s_ld, loaded)
                link = Chain(dve, s_b2)
                dve.wait_ge(s_cst, 2 if routed else 1)
                if routed:
                    link(v.tensor_scalar(lower[:, :, :], lower[:, :, :], 0.0, None, ALU.is_lt))
                link(high(b2hl[:, :, :], b2[:, :, :]))
                link(low(b2hl[32:GA, :, :], b2[32:GA, :, :], b2hl[32:GA, :, :]))
                split(0)
                if routed:
                    shift(0)
                all_groups(dve, group)
                add_rows(NG - 1, NB - 2)
                add_rows(NG - 1, NB - 1)
                if routed:
                    observe(NG - 1)
                    c.norm.finish(dve)


def project_qkv(c, A):
    nc = c.nc
    with ExitStack() as s:
        w = c.sb("q_w", [P, KC, 3 * D], F32, s)
        wh, wl = (c.sb("q_" + n, [P, KC, 3 * D], F32R, s) for n in ("wh", "wl"))
        b = c.sb("q_b", [P, 3 * D], F32, s)
        xn = c.sb("q_xn", [P, GT, D], F32, s)
        xTh, xTl = (c.sb("q_" + n, [P, GT, KC, P], F32R, s) for n in ("xTh", "xTl"))
        kv = c.sb("q_kv", [P, GT, 2, D], F32, s)
        tp = [c.ps(f"q_tp{n}", [P, 512], F32, s) for n in range(2)]
        qp = [c.ps(f"q_p{n}", [P, 1024], F32, s) for n in range(2)]
        names = ("normed", "loaded", "weights", "transposed", "high", "low", "rows", "sum", "tok", "dgate", "agate", "pgate")
        s_xn, s_ld, s_w, s_t, s_hi, s_lo, s_r, s_s, s_tok, s_dg, s_ag, s_pg = (c.sem("q_" + n) for n in names)
        s_kv = [c.sem(f"q_kv{n}") for n in range(GT)]
        by_chunk = lambda t: t[:, 0:D].rearrange("p (k n) -> p k n", k=KC)
        with nc.Block() as block:
            @block.sync
            def _(sp):
                sp.dma_start(w[:, :, :], A["W_qkv"].rearrange("(k p) n -> p k n", p=P)).then_inc(s_ld, 16)
                sp.dma_start(b[:, :], bcast_rows(A["b_qkv"], P)).then_inc(s_ld, 16)
                for t in range(NW):
                    sp.wait_ge(s_s, t + 1)
                    for n, table in enumerate((c.k_dram, c.v_dram)):
                        sp.dma_start(table[t * P:(t + 1) * P, :], kv[:, t % GT, n, :]).then_inc(s_kv[t % GT], 16)
                for n in range(GT):
                    sp.wait_ge(s_kv[n], 32 * NG)

            @block.gpsimd
            def _(pool):
                def step(at):
                    t = at(0)
                    if real(t):
                        need(pool, s_pg, (s_xn, t.n + 1), (s_tok, t.n))
                        nc.gpsimd.tensor_copy(window(c.tok, t.n), xn[:, t.slot, :]).then_inc(s_tok, 1)
                rounds(pool, step, 0, 0, Window)

            @block.tensor
            def _(pe):
                mm = nc.tensor.matmul

                def step(at):
                    t = at(2)
                    if real(t):
                        need(pe, None, (s_xn, t.n + 1), (s_lo, t.free), own=True)
                        transpose_window(nc, by_chunk(tp[t.bank]), xn[:, t.slot, :], c.ident).then_inc(s_t, 1)
                    t = at(0)
                    if real(t):
                        need(pe, None, (s_lo, t.n + 1), (s_s, t.free), own=True)
                        if isinstance(t.n, int) and t.n == 0:
                            pe.wait_ge(s_w, 2)
                        for lo, hi in ((0, 2 * D), (2 * D, 3 * D)):
                            to = qp[t.bank][:, lo:hi]
                            for k in range(KC):
                                mm(to, xTl[:, t.slot, k, :], wh[:, k, lo:hi], start=(k == 0), stop=False)
                                mm(to, xTh[:, t.slot, k, :], wl[:, k, lo:hi], start=False, stop=False)
                            for k in range(KC):
                                last = mm(to, xTh[:, t.slot, k, :], wh[:, k, lo:hi], start=False, stop=(k == KC - 1))
                        last.then_inc(s_r, 1)
                rounds(pe, step, 2, 0, Window)

            @block.scalar
            def _(act):
                def step(at):
                    t = at(2)
                    if real(t):
                        need(act, s_ag, (s_t, t.n + 1), (s_r, t.n - GT + 1))
                        nc.scalar.copy(xTh[:, t.slot, :, :], by_chunk(tp[t.bank])).then_inc(s_hi, 1)
                act.wait_ge(s_ld, 32)
                nc.scalar.copy(wh[:, :, :], w[:, :, :]).then_inc(s_w, 1)
                rounds(act, step, 2, 0, Window)

            @block.vector
            def _(dve):
                v = nc.vector
                def step(at):
                    t = at(3)
                    if real(t):
                        need(dve, s_dg, (s_t, t.n - GT + 1), (s_tok, t.n - GT + 1))
                        c.norm.one(t.n, xn[:, t.slot, :]).then_inc(s_xn, 1)
                    t = at(0)
                    if real(t):
                        if isinstance(t.n, int) and t.n == 0:
                            dve.wait_ge(s_w, 1)
                            v.tensor_tensor(wl[:, :, :], w[:, :, :], wh[:, :, :].bitcast(F32), ALU.subtract).then_inc(s_w, 1)
                        need(dve, s_dg, (s_ld, 32), (s_r, t.n + 1), (s_kv[t.slot], t.turn * 32))
                        v.tensor_tensor(window(c.q, t.n), qp[t.bank][:, 0:D], b[:, 0:D], ALU.add)
                        v.tensor_tensor(kv[:, t.slot, :, :].rearrange("p a d -> p (a d)"), qp[t.bank][:, D:3 * D], b[:, D:3 * D], ALU.add).then_inc(s_s, 1)
                    t = at(2)
                    if real(t):
                        need(dve, s_dg, (s_hi, t.n + 1))
                        v.tensor_tensor(xTl[:, t.slot, :, :], by_chunk(tp[t.bank]), xTh[:, t.slot, :, :].bitcast(F32), ALU.subtract).then_inc(s_lo, 1)
                rounds(dve, step, 3, 0, Window)


def edge_scores(c, A):
    nc = c.nc
    with ExitStack() as s:
        drow = c.sb("s_drow", [P, 2, IG * P], I32, s)
        spread = c.sb("s_spread", [P, 2, IG, P], F32, s)
        idx = c.sb("s_idx", [P, 4, IG], I32, s)
        rows = c.sb("s_rows", [P, 4, IG, D], F32, s)
        prod = c.sb("s_prod", [P, 2, IG, D], F32, s)
        qp = [c.ps(f"s_q{p}", [P, IG * D], F32, s) for p in range(2)]
        s_dr = [c.sem(f"s_drow{p}") for p in range(2)]
        s_rows = [c.sem(f"s_rows{p}") for p in range(4)]
        names = ("spread", "q", "prod", "score", "idx", "dgate", "pad")
        s_sp, s_q, s_pr, s_sc, s_idx, s_dg, s_pad = (c.sem("s_" + n) for n in names)
        with nc.Block() as block:
            @block.sync
            def _(sp):
                def load(at):
                    g = at(3)
                    if real(g):
                        tiles = item_values(sp, g, c.t_row, NT - 1)
                        need(sp, None, (s_sp, g.n - 1), own=True)
                        for j in range(JG):
                            sp.dma_start(drow[:, g.slot, j * TE:(j + 1) * TE], bcast_rows(A["dst_row"][0:1, bass.ds(tiles[j] * TE, TE)], P)).then_inc(s_dr[g.slot], 16)
                rounds(sp, load, 3, 0)

            @block.gpsimd
            def _(pool):
                nc.gpsimd.memset(c.score[:, NC:NCP, :], 0.0).then_inc(s_pad, 1)

                def step(at):
                    g = at(3)
                    if real(g):
                        gather(c, pool, g, idx, rows, c.k_dram, s_rows, s_idx, s_pr)
                rounds(pool, step, 3, 0)
                pool.wait_ge(s_pad, 1)

            @block.scalar
            def _(act):
                def step(at):
                    g = at(4)
                    if real(g):
                        source_index(c, act, g, idx, s_rows, s_idx)
                rounds(act, step, 4, 0)

            @block.tensor
            def _(pe):
                def step(at):
                    g = at(1)
                    if real(g):
                        wins = item_values(pe, g, c.w_row, NW - 1)
                        need(pe, None, (s_sp, g.n + 1), (s_pr, g.n - 1), own=True)
                        for j in range(IG):
                            last = nc.tensor.matmul(qp[g.slot][:, j * D:(j + 1) * D], spread[:, g.slot, j, :], window(c.q, wins[j // CT]), start=True, stop=True)
                        last.then_inc(s_q, 1)
                rounds(pe, step, 1, 0)

            @block.vector
            def _(dve):
                v = nc.vector

                def step(at):
                    g = at(0)
                    if real(g):
                        need(dve, s_dg, (s_q, g.n + 1), (s_rows[g.slot4], (g.turn4 + 1) * 64), (s_sc, g.n - 1))
                        v.tensor_tensor(prod[:, g.slot, :, :], qp[g.slot][:, :].rearrange("p (a d) -> p a d", a=IG), rows[:, g.slot4, :, :], ALU.mult).then_inc(s_pr, 1)
                    h = at(2)
                    if real(h):
                        need(dve, s_dg, (s_dr[h.slot], (h.turn + 1) * 16 * JG), (s_q, h.n - 1))
                        for j in range(IG):
                            last = v.tensor_scalar(spread[:, h.slot, j, :], drow[:, h.slot, j * P:(j + 1) * P], c.node_id[:, bass.ds(h.n * IG + j, 1)], None, ALU.is_equal)
                        last.then_inc(s_sp, 1)
                    if real(g):
                        need(dve, s_dg, (s_pr, g.n + 1))
                        v.tensor_reduce(c.score[:, bass.ds(g.n * IG, IG), :].rearrange("p a h -> p (a h)"),
                                        prod[:, g.slot, :, :].rearrange("p a (h d) -> p (a h) d", h=H), AX.X, ALU.add).then_inc(s_sc, 1)
                rounds(dve, step, 2, 0)


def segment_exp(c, A):
    nc = c.nc
    NEG = -1.0e30
    with ExitStack() as s:
        sT = c.sb("x_sT", [P, CE], F32, s)
        idT = c.sb("x_idT", [P, CE], F32, s)
        new = c.sb("x_new", [P, CE + 1], F32, s)
        run = c.sb("x_run", [P, CE], F32, s)
        up = c.sb("x_up", [P, P], F32, s)
        down = c.sb("x_down", [P, P], F32, s)
        one = c.sb("x_one", [1, 1], F32, s)
        col = c.sb("x_col", [P, 16], F32, s)
        row = c.sb("x_row", [1, 3, P], F32, s)
        carry = c.sb("x_carry", [P, 2], F32, s)
        tp = [c.ps(f"x_tp{n}", [P, 512], F32, s) for n in range(4)]
        sp_ = c.ps("x_small", [P, 512], F32, s)
        s_cst, s_ord, s_d, s_t, s_ev, s_pe, s_v, s_ex = (c.sem("x_" + n) for n in ("const", "ordered", "chain", "transposed", "evacuated", "pe", "dve", "exp"))
        blocks = [(r, min(4, CI - r)) for r in range(0, CI, 4)]
        ids_by_chunk = c.seg_id[:, :].rearrange("p (c r) -> p r c", c=CH)
        score_by_chunk = c.score[:, :, :].rearrange("p (c r) h -> p r c h", c=CH)
        ex_by_chunk = c.ex[:, :, :].rearrange("p (c r) h -> p r c h", c=CH)
        NBK = len(blocks)
        with nc.Block() as block:
            @block.gpsimd
            def _(pool):
                nc.gpsimd.memset(up[:, :], 0.0).then_inc(s_cst, 1)
                nc.gpsimd.memset(down[:, :], 0.0).then_inc(s_cst, 1)
                pool.wait_ge(s_cst, 2)
                nc.gpsimd.memset(one[:, :], 1.0).then_inc(s_cst, 1)
                pool.wait_ge(s_cst, 3)
                pool.affine_select(out=up[:, :], in_=up[:, :], compare_op=ALU.not_equal, fill=1.0, base=H,
                                   pattern=[[-1, P]], channel_multiplier=1).then_inc(s_cst, 1)
                pool.affine_select(out=down[:, :], in_=down[:, :], compare_op=ALU.not_equal, fill=1.0, base=-H,
                                   pattern=[[-1, P]], channel_multiplier=1).then_inc(s_cst, 1)

            @block.tensor
            def _(pe):
                t = nc.tensor
                pe.wait_ge(s_cst, 5)
                pe.wait_ge(s_ord, 2)
                n = 0
                for what in range(2):
                    for r0, k in blocks:
                        if n >= 4:
                            pe.wait_ge(s_ev, n - 3)
                        for r in range(k):
                            at = (r0 + r) * P
                            last = t.transpose(tp[n % 4][:, r * P:(r + 1) * P], (run, new)[what][:, at:at + P], c.ident[:, :])
                        last.then_inc(s_t, 1)
                        n += 1
                pe.wait_ge(s_v, 1)
                t.matmul(sp_[:, 0:1], up[:, :], col[:, 0:1], start=True, stop=True).then_inc(s_pe, 1)
                t.matmul(sp_[:, 1:2], down[:, :], col[:, 1:2], start=True, stop=True).then_inc(s_pe, 1)
                pe.wait_ge(s_v, 2)
                t.matmul(sp_[:, 2:3], down[:, :], new[:, 0:1], start=True, stop=True).then_inc(s_pe, 1)
                for way in range(2):
                    pe.wait_ge(s_v, 3 + 2 * way)
                    t.matmul(sp_[0:1, 128:256], col[:, 8 + 2 * way:9 + 2 * way], c.ident[:, :], start=True, stop=True)
                    t.matmul(sp_[0:1, 256:384], col[:, 9 + 2 * way:10 + 2 * way], c.ident[:, :], start=True, stop=True).then_inc(s_pe, 1)
                    pe.wait_ge(s_v, 4 + 2 * way)
                    t.matmul(sp_[:, 4:5], row[:, 2, :], one[:, :], start=True, stop=True).then_inc(s_pe, 1)
                pe.wait_ge(s_ex, 1)
                for r0, k in blocks:
                    pe.wait_ge(s_ev, n - 3)
                    for r in range(k):
                        last = t.transpose(tp[n % 4][:, r * P:(r + 1) * P], sT[:, (r0 + r) * P:(r0 + r + 1) * P], c.ident[:, :])
                    last.then_inc(s_t, 1)
                    n += 1

            @block.scalar
            def _(act):
                act.wait_ge(s_v, 7)
                nc.scalar.activation(sT[:, :], run[:, :], ACT.Exp, scale=SCALE).then_inc(s_ex, 1)

            @block.vector
            def _(dve):
                v = nc.vector
                link = Chain(dve, s_d)
                order = lambda t: t[:, 0:CE].rearrange("p (r c h) -> p r c h", c=CH, h=H)
                v.tensor_copy(order(run), score_by_chunk).then_inc(s_ord, 1)
                v.tensor_copy(order(new), ids_by_chunk.rearrange("p r (c a) -> p r c a", a=1).broadcast_to([P, CI, CH, H])).then_inc(s_ord, 1)
                n = 0
                for to in (sT, idT):
                    for r0, k in blocks:
                        dve.wait_ge(s_t, n + 1)
                        v.tensor_copy(to[:, r0 * P:(r0 + k) * P], tp[n % 4][:, 0:k * P]).then_inc(s_ev, 1)
                        n += 1
                dve.wait_ge(s_ev, n)
                first, last = idT[:, 0:1], idT[:, CE - 1:CE]
                v.tensor_copy(col[:, 0:1], last)
                v.tensor_copy(col[:, 1:2], first).then_inc(s_v, 1)
                v.tensor_tensor(new[:, 1:CE], idT[:, 1:CE], idT[:, 0:CE - 1], ALU.not_equal)
                dve.wait_ge(s_pe, 2)
                link(v.tensor_tensor(new[:, 0:1], first, sp_[:, 0:1], ALU.not_equal))
                link(v.tensor_scalar(new[:, 0:CE], new[:, 0:CE], NEG, None, ALU.mult))
                link(v.tensor_tensor(col[:, 2:3], first, last, ALU.not_equal))
                v.tensor_tensor(col[:, 3:4], last, sp_[:, 1:2], ALU.not_equal).then_inc(s_v, 1)
                dve.wait_ge(s_v, 2)
                link(v.tensor_scalar(col[:, 2:4], col[:, 2:4], NEG, None, ALU.mult))
                link(v.tensor_tensor(col[:, 8:9], col[:, 2:3], new[:, 0:1], ALU.add))
                link(v.tensor_tensor(col[:, 10:11], col[:, 2:3], col[:, 3:4], ALU.add))
                dve.wait_ge(s_pe, 3)
                link(v.tensor_copy(new[:, CE:CE + 1], sp_[:, 2:3]))

                def carried(way, end):
                    v.tensor_copy(col[:, 9 + 2 * way:10 + 2 * way], end).then_inc(s_v, 1)
                    dve.wait_ge(s_pe, 4 + 2 * way)
                    link(v.tensor_copy(row[:, 0:2, :], sp_[0:1, 128:384].rearrange("p (a n) -> p a n", a=2)))
                    link(v.memset(row[:, 2, :], NEG))
                    by_head = row[:, :, :].rearrange("p a (c h) -> p a h c", h=H)
                    for h in range(H):
                        if way == 0:
                            last = v.tensor_tensor_scan(by_head[:, 2, h, 1:CH], by_head[:, 0, h, 0:CH - 1], by_head[:, 1, h, 0:CH - 1], NEG, ALU.add, ALU.max)
                        else:
                            last = v.tensor_tensor_scan(by_head[:, 2, h, CH - 2::-1], by_head[:, 0, h, CH - 1:0:-1], by_head[:, 1, h, CH - 1:0:-1], NEG, ALU.add, ALU.max)
                    last.then_inc(s_v, 1)
                    dve.wait_ge(s_pe, 5 + 2 * way)
                    link(v.tensor_copy(carry[:, way:way + 1], sp_[:, 4:5]))
                link(v.tensor_tensor_scan(run[:, :], new[:, 0:CE], sT[:, :], NEG, ALU.add, ALU.max))
                carried(0, run[:, CE - 1:CE])
                link(v.tensor_tensor_scan(run[:, :], new[:, 0:CE], sT[:, :], carry[:, 0:1], ALU.add, ALU.max))
                back = lambda t, lo, hi: t[:, lo:hi][:, ::-1]
                link(v.tensor_tensor_scan(back(idT, 0, CE), back(new, 1, CE + 1), back(run, 0, CE), NEG, ALU.add, ALU.max))
                carried(1, idT[:, 0:1])
                link(v.tensor_tensor_scan(back(idT, 0, CE), back(new, 1, CE + 1), back(run, 0, CE), carry[:, 1:2], ALU.add, ALU.max))
                v.tensor_tensor(run[:, :], sT[:, :], idT[:, :], ALU.subtract).then_inc(s_v, 1)
                for r0, k in blocks:
                    dve.wait_ge(s_t, n + 1)
                    v.tensor_copy(ex_by_chunk[:, r0:r0 + k], tp[n % 4][:, 0:k * P].rearrange("p (r c h) -> p r c h", r=k, h=H)).then_inc(s_ev, 1)
                    n += 1


def edge_messages(c, A):
    nc = c.nc
    DM = D + H
    with ExitStack() as s:
        idx = c.sb("a_idx", [P, 4, IG], I32, s)
        rows = c.sb("a_rows", [P, 4, IG, D], F32, s)
        msg = c.sb("a_msg", [P, 2, IG, DM], F32, s)
        hot = c.sb("a_hot", [P, 2, IG, P], F32, s)
        ap = [c.ps(f"a_agg{p}", [P, JG, 512], F32, s) for p in range(2)]
        s_rows = [c.sem(f"a_rows{p}") for p in range(4)]
        names = ("idx", "zero", "ex", "msg", "agg", "acc", "dgate", "agate")
        s_idx, s_zero, s_ex, s_msg, s_agg, s_acc, s_dg, s_ag = (c.sem("a_" + n) for n in names)
        with nc.Block() as block:
            @block.gpsimd
            def _(pool):
                def step(at):
                    g = at(3)
                    if real(g):
                        gather(c, pool, g, idx, rows, c.v_dram, s_rows, s_idx, s_msg)
                rounds(pool, step, 3, 0)

            @block.tensor
            def _(pe):
                def step(at):
                    g = at(0)
                    if real(g):
                        need(pe, None, (s_msg, g.n + 1), (s_acc, (g.n - 1) * JG), own=True)
                        for j in range(IG):
                            h, half = divmod(j, CT)
                            last = nc.tensor.matmul(ap[g.slot][:, h, 0:DM], hot[:, g.slot, j, :], msg[:, g.slot, j, :], start=(half == 0), stop=(half == CT - 1))
                        last.then_inc(s_agg, 1)
                rounds(pe, step, 0, 0)

            @block.scalar
            def _(act):
                def step(at):
                    g = at(4)
                    if real(g):
                        source_index(c, act, g, idx, s_rows, s_idx)
                    g = at(2)
                    if real(g):
                        need(act, s_ag, (s_agg, g.n - 1))
                        nc.scalar.copy(msg[:, g.slot, :, D:DM], c.ex[:, bass.ds(g.n * IG, IG), :]).then_inc(s_ex, 1)
                rounds(act, step, 4, 0)

            @block.vector
            def _(dve):
                v = nc.vector
                by_head = lambda t: t.rearrange("p t (h d) -> p t h d", h=H)

                def one_hot(g):
                    if real(g):
                        need(dve, s_dg, (s_agg, g.n - 1))
                        for j in range(IG):
                            v.tensor_scalar(hot[:, g.slot, j, :], c.iota_n[:, :], c.dst_rel[:, bass.ds(g.n * IG + j, 1)], None, ALU.is_equal)

                def step(at):
                    g = at(-1)
                    if real(g):
                        wins = item_values(dve, g, c.w_row, NW - 1)
                    for j in range(JG):
                        if real(g):
                            need(dve, s_dg, (s_agg, g.n + 1), (s_acc, g.n * JG + j))
                            to = window(c.agg, wins[j])
                            v.tensor_tensor(to, to, ap[g.slot][:, j, 0:DM], ALU.add).then_inc(s_acc, 1)
                        if j == 0:
                            one_hot(at(1))
                    g = at(1)
                    if real(g):
                        need(dve, s_dg, (s_rows[g.slot4], (g.turn4 + 1) * 64), (s_ex, g.n + 1))
                        ex = c.ex[:, bass.ds(g.n * IG, IG), :].rearrange("p t (h a) -> p t h a", a=1).broadcast_to([P, IG, H, DH])
                        v.tensor_tensor(by_head(msg[:, g.slot, :, 0:D]), by_head(rows[:, g.slot4, :, :]), ex, ALU.mult).then_inc(s_msg, 1)
                v.memset(c.agg[:, :, :], 0.0).then_inc(s_zero, 1)
                dve.wait_ge(s_zero, 1)
                rounds(dve, step, 1, 1)


def attention_out(c, A):
    nc = c.nc
    c.norm.begin("n3")
    with ExitStack() as s:
        w = c.sb("o_w", [P, KC, D], F32, s)
        b = c.sb("o_b", [P, D], F32, s)
        rden = c.sb("o_rden", [P, NW, H], F32, s)
        hc = c.sb("o_hc", [P, GT, D], F32, s)
        sc = c.sb("o_sc", [P, GT, D], F32, s)
        xT = c.sb("o_xT", [P, GT, KC, P], F32, s)
        tp, op = ([c.ps(f"o_{n}{b}", [P, 512], F32, s) for b in range(2)] for n in ("tp", "op"))
        names = ("loaded", "chain", "scaled", "hc", "transposed", "xT", "rows", "added", "x", "dgate", "agate", "pgate")
        s_ld, s_d, s_sc, s_hc, s_t, s_xT, s_r, s_add, s_x, s_dg, s_ag, s_pg = (c.sem("o_" + n) for n in names)
        with nc.Block() as block:
            @block.sync
            def _(sp):
                sp.dma_start(w[:, :, :], A["W_out"].rearrange("(k p) n -> p k n", p=P)).then_inc(s_ld, 16)
                sp.dma_start(b[:, :], bcast_rows(A["b_out"], P)).then_inc(s_ld, 16)

            @block.gpsimd
            def _(pool):
                pool.wait_ge(s_ld, 32)

                def step(at):
                    t = at(0)
                    if real(t):
                        need(pool, s_pg, (s_add, t.n))
                        nc.gpsimd.tensor_tensor(window(c.x, t.n), window(c.x, t.n), b[:, :], ALU.add).then_inc(s_add, 1)
                rounds(pool, step, 0, 0, Window)

            @block.tensor
            def _(pe):
                pe.wait_ge(s_ld, 32)

                def step(at):
                    t = at(1)
                    if real(t):
                        need(pe, None, (s_hc, t.n + 1), (s_xT, t.free), own=True)
                        transpose_window(nc, tp[t.bank][:, 0:D].rearrange("p (k n) -> p k n", k=KC), hc[:, t.slot, :], c.ident).then_inc(s_t, 1)
                    t = at(0)
                    if real(t):
                        need(pe, None, (s_xT, t.n + 1), (s_x, t.free), own=True)
                        for k in range(KC):
                            last = nc.tensor.matmul(op[t.bank][:, 0:D], xT[:, t.slot, k, :], w[:, k, :], start=(k == 0), stop=(k == KC - 1))
                        last.then_inc(s_r, 1)
                rounds(pe, step, 1, 0, Window)

            @block.scalar
            def _(act):
                def step(at):
                    t = at(1)
                    if real(t):
                        need(act, s_ag, (s_t, t.n + 1), (s_r, t.n - GT + 1))
                        nc.scalar.copy(xT[:, t.slot, :, :], tp[t.bank][:, 0:D].rearrange("p (k n) -> p k n", k=KC)).then_inc(s_xT, 1)
                rounds(act, step, 1, 0, Window)
                c.norm.root(act)

            @block.vector
            def _(dve):
                v = nc.vector
                link = Chain(dve, s_d)
                link(v.tensor_scalar(rden[:, :, :], c.agg[:, :, D:D + H], 1e-30, None, ALU.max))
                link(v.reciprocal(rden[:, :, :], rden[:, :, :]))

                def step(at):
                    t = at(3)
                    if real(t):
                        need(dve, s_dg, (s_hc, t.n - GT + 1))
                        v.tensor_tensor(sc[:, t.slot, :].rearrange("p (d h) -> p d h", h=H),
                                        c.agg[:, bass.ds(t.n, 1), 0:D].rearrange("p a (h d) -> p (a d) h", h=H),
                                        rden[:, bass.ds(t.n, 1), :].broadcast_to([P, DH, H]), ALU.mult).then_inc(s_sc, 1)
                    t = at(-1)
                    if real(t):
                        need(dve, s_dg, (s_r, t.n + 1), (s_add, t.n + 1))
                        v.tensor_tensor(window(c.x, t.n), window(c.x, t.n), op[t.bank][:, 0:D], ALU.add).then_inc(s_x, 1)
                    t = at(2)
                    if real(t):
                        need(dve, s_dg, (s_sc, t.n + 1), (s_t, t.n - GT + 1))
                        v.tensor_tensor(hc[:, t.slot, :], sc[:, t.slot, :], window(c.tok, t.n), ALU.add).then_inc(s_hc, 1)
                    t = at(-2)
                    if real(t):
                        need(dve, s_dg, (s_x, t.n + 1))
                        c.norm.observe(t.n)
                rounds(dve, step, 3, 2, Window)
                c.norm.finish(dve)


def select_tokens(c, A):
    nc = c.nc
    DIGITS = [25, 18, 11, 4, 0]
    WIDTH = [7, 7, 7, 7, 4]
    SIGN = -2 ** 31
    with ExitStack() as s:
        wr = c.sb("t_wr", [P, D], F32, s)
        br = c.sb("t_br", [P, 1], F32, s)
        part = c.sb("t_part", [P, 1], I32, s)
        at_digit = c.sb("t_at_digit", [P, len(DIGITS)], I32, s)
        masks = c.sb("t_masks", [P, 2, P], F32, s)
        lower = c.sb("t_lower", [P, P], F32, s)
        ones = c.sb("t_ones", [P, P], F32, s)
        prod = c.sb("t_prod", [P, GT, D], F32, s)
        wcol = c.sb("t_wcol", [P, NW], F32, s)
        side = c.sb("t_side", [P, NP], F32, s)
        key = c.sb("t_key", [P, 4], I32, s)
        num = c.sb("t_num", [P, 4], F32, s)
        tie = c.sb("t_tie", [P, NW], F32, s)
        rank = c.sb("t_rank", [P, NW], F32, s)
        total = c.sb("t_total", [P, NW], F32, s)
        run = c.sb("t_run", [P, NW], F32, s)
        wide = c.ps("t_wide", [P, NP], F32, s)
        small = c.ps("t_small", [P, 2, NW], F32, s)
        names = ("normed", "dgate", "loaded", "cst", "chain", "tokens", "weights", "padded", "wide", "enough", "digit", "ties", "ranks")
        s_xn, s_dg, s_ld, s_cst, s_d, s_tok, s_w, s_pad, s_wide, s_en, s_dig, s_tie, s_rank = (c.sem("t_" + n) for n in names)
        with nc.Block() as block:
            @block.sync
            def _(sp):
                sp.dma_start(wr[:, :], bcast_rows(A["wr"], P)).then_inc(s_ld, 16)
                sp.dma_start(br[:, :], bcast_rows(A["br"], P)).then_inc(s_ld, 16)

            @block.gpsimd
            def _(pool):
                link = Chain(pool, s_cst)
                link(pool.iota(part[:, :], pattern=[[1, 1]], base=0, channel_multiplier=1))
                for t in (masks, lower, ones):
                    link(nc.gpsimd.memset(t[:, :], 1.0) if t is not masks else nc.gpsimd.memset(t[:, :, :], 1.0))
                keep_where = lambda t, base, step, along: link(pool.affine_select(
                    out=t, in_=t, compare_op=ALU.is_ge, fill=0.0, base=base, pattern=[[along, P]], channel_multiplier=step))
                for n in range(2):
                    keep_where(masks[:, n, :], -1, 1, 0)
                keep_where(masks[:, 1, :], 2 ** WIDTH[-1] - 1, -1, 0)
                keep_where(lower[:, :], -1, -1, 1)
                pool.wait_ge(s_w, 1)
                pool.affine_select(out=wcol[:, :], in_=wcol[:, :], compare_op=ALU.is_ge, fill=-BIG / 3, base=N - 1,
                                   pattern=[[-P, NW]], channel_multiplier=-1).then_inc(s_pad, 1)

            @block.tensor
            def _(pe):
                pe.wait_ge(s_pad, 1)
                for t in range(NW):
                    last = nc.tensor.transpose(wide[:, t * P:(t + 1) * P], wcol[:, t:t + 1].broadcast_to([P, P]), c.ident[:, :])
                last.then_inc(s_wide, 1)
                pe.wait_ge(s_cst, 8)
                for n in range(len(DIGITS)):
                    pe.wait_ge(s_en, n + 1)
                    nc.tensor.matmul(small[:, 0, 0:1], masks[:, WIDTH[n] < 7, :], num[:, 1:2], start=True, stop=True).then_inc(s_dig, 1)
                pe.wait_ge(s_tie, 1)
                nc.tensor.matmul(small[:, 0, :], lower[:, :], tie[:, :], start=True, stop=True)
                nc.tensor.matmul(small[:, 1, :], ones[:, :], tie[:, :], start=True, stop=True).then_inc(s_rank, 1)

            @block.vector
            def _(dve):
                v = nc.vector
                link = Chain(dve, s_d)
                dve.wait_ge(s_ld, 32)

                def step(at):
                    t = at(1)
                    if real(t):
                        c.norm.one(t.n, window(c.tok, t.n)).then_inc(s_xn, 1)
                    t = at(0)
                    if real(t):
                        need(dve, s_dg, (s_xn, t.n + 1), (s_tok, t.n - GT + 1))
                        v.scalar_tensor_tensor(prod[:, t.slot, :], window(c.tok, t.n), 1.0, wr[:, :], ALU.mult, ALU.mult,
                                               accum_out=wcol[:, bass.ds(t.n, 1)]).then_inc(s_tok, 1)
                rounds(dve, step, 1, 0, Window)
                dve.wait_ge(s_tok, NW)
                v.tensor_scalar(wcol[:, :], wcol[:, :], br[:, 0:1], None, ALU.add).then_inc(s_w, 1)
                dve.wait_ge(s_cst, 8)
                for n, low in enumerate(DIGITS):
                    link(v.tensor_scalar(at_digit[:, n:n + 1], part[:, :], low, None, ALU.logical_shift_left))
                link(v.memset(at_digit[0:1, 0:1], 1 << 23))
                digits, cand, flips, bits = (key[:, n:n + 1] for n in range(4))

                def number(of):
                    link(v.tensor_scalar(flips, of, 31, -1, ALU.arith_shift_right, ALU.bitwise_xor))
                    link(v.tensor_scalar(flips, flips, SIGN, None, ALU.bitwise_or))
                    link(v.tensor_tensor(bits, of, flips, ALU.bitwise_xor))
                link(v.memset(digits, 0))
                dve.wait_ge(s_wide, 1)
                for n, low in enumerate(DIGITS):
                    link(v.tensor_tensor(cand, digits, at_digit[:, n:n + 1], ALU.bitwise_or))
                    number(cand)
                    link(v.tensor_scalar(side[:, :], wide[:, :], bits.bitcast(F32), 0.0, ALU.is_ge, ALU.add, accum_out=num[:, 0:1]))
                    v.tensor_scalar(num[:, 1:2], num[:, 0:1], KEEP - 0.5, None, ALU.is_gt).then_inc(s_en, 1)
                    dve.wait_ge(s_dig, n + 1)
                    link(v.tensor_copy(cand, small[:, 0, 0:1]))
                    link(v.tensor_scalar(cand, cand, low, None, ALU.logical_shift_left))
                    link(v.tensor_tensor(digits, digits, cand, ALU.bitwise_or))
                number(digits)
                cut = bits.bitcast(F32)
                v.tensor_scalar(tie[:, :], wcol[:, :], cut, None, ALU.is_equal).then_inc(s_tie, 1)
                link(v.tensor_scalar(side[:, :], wide[:, :], cut, 0.0, ALU.is_gt, ALU.add, accum_out=num[:, 2:3]))
                dve.wait_ge(s_rank, 1)
                link(v.tensor_copy(total[:, :], small[:, 1, :]))
                link(v.tensor_tensor_scan(run[:, :], total[:, :], total[:, :], 0.0, ALU.add, ALU.bypass))
                link(v.tensor_tensor(run[:, :], run[:, :], total[:, :], ALU.subtract))
                link(v.tensor_tensor(rank[:, :], run[:, :], small[:, 0, :], ALU.add))
                link(v.tensor_scalar(rank[:, :], rank[:, :], num[:, 2:3], KEEP - 0.5, ALU.add, ALU.is_lt))
                link(v.tensor_tensor(tie[:, :], tie[:, :], rank[:, :], ALU.mult))
                link(v.scalar_tensor_tensor(tie[:, :], wcol[:, :], cut, tie[:, :], ALU.is_gt, ALU.add))
                link(v.tensor_tensor(c.gate[:, :], tie[:, :], wcol[:, :], ALU.mult))


def build_program(nc, A, out, upto=99):
    c = Core(nc)
    n = [0]

    def phase(f, *args):
        n[0] += 1
        if n[0] <= upto:
            f(c, A, *args)
    with c.keep:
        c.out = out
        c.h_dram = nc.dram_tensor("h_table", (NP, D), F32, kind="Internal").ap()
        c.k_dram = nc.dram_tensor("k_table", (NP, D), F32, kind="Internal").ap()
        c.v_dram = nc.dram_tensor("v_table", (NP, D), F32, kind="Internal").ap()
        c.x = c.sb("x", [P, NW, D])
        c.gate = c.sb("gate", [P, NW])
        phase(prepare)
        phase(source_features)
        with ExitStack() as first_gnn:
            c.agg = c.sb("agg", [P, NW, D + H], F32, first_gnn)
            phase(edges_first)
            phase(nodes_first)
        phase(experts, True)
        c.recycle()
        c.tok = c.sb("tok", [P, NW, D])
        with ExitStack() as attention:
            c.score = c.sb("score", [P, NCP, H], F32, attention)
            c.ex = c.sb("ex", [P, NCP, H], F32, attention)
            c.agg = c.sb("agg2", [P, NW, D + H], F32, attention)
            with ExitStack() as queries:
                c.q = c.sb("q", [P, NW, D], F32, queries)
                phase(project_qkv)
                phase(edge_scores)
            phase(segment_exp)
            phase(edge_messages)
            phase(attention_out)
        phase(select_tokens)
        phase(experts, False)
    return c


def layouts(inputs):
    f = lambda n: np.ascontiguousarray(np.asarray(inputs[n]))
    pad_e = lambda a, v: np.concatenate([a, np.full((EP - E,) + a.shape[1:], v, a.dtype)])
    A = {}
    A["x"] = np.concatenate([f("x"), np.zeros((NP - N, D), np.float32)])
    A["src"] = pad_e(f("src"), 0).reshape(NT, TE)
    A["dst"] = pad_e(f("dst"), N).reshape(NT, TE)
    A["dst_row"] = A["dst"].reshape(1, EP)
    A["edge_weight"] = pad_e(f("edge_weight"), 0).reshape(NT, TE)
    A["eaT"] = np.ascontiguousarray(pad_e(f("edge_attr_64"), 0).T)
    A["g_fw1T"] = np.concatenate([f("L0_gnn_fw1").T, f("L0_gnn_fb1")[None]])
    A["g_fw2T"] = np.ascontiguousarray(f("L0_gnn_fw2").T)
    A["g_fb2"] = f("L0_gnn_fb2")
    A["g_w1T"] = np.ascontiguousarray(f("L0_gnn_w1").T)
    A["g_w2T"] = np.ascontiguousarray(f("L0_gnn_w2").T)
    A["g_b2"] = np.ascontiguousarray(f("L0_gnn_b2").reshape(KC, P).T)
    A["g_w3T"] = np.ascontiguousarray(f("L0_gnn_w3").T)
    A["g_b3"] = f("L0_gnn_b3")
    A["r_wT"] = np.ascontiguousarray(f("L0_ffn_router_w").T)
    A["m_w1"] = f("L0_ffn_w1")
    A["m_b1"] = np.ascontiguousarray(f("L0_ffn_b1").reshape(NEXP, KC, P).transpose(2, 0, 1).reshape(P, NEXP * KC))
    A["m_w2"] = f("L0_ffn_w2")
    A["m_b2"] = f("L0_ffn_b2")
    A["W_qkv"] = f("L1_gnn_W_qkv")
    A["b_qkv"] = f("L1_gnn_b_qkv")
    A["W_out"] = f("L1_gnn_W_out")
    A["b_out"] = f("L1_gnn_b_out")
    A["wr"] = f("L1_ffn_wr").reshape(D)
    A["br"] = f("L1_ffn_br")
    A["f_w1"] = f("L1_ffn_w1")
    A["f_b1"] = np.ascontiguousarray(f("L1_ffn_b1").reshape(HF // P, P).T)
    A["f_w2"] = f("L1_ffn_w2")
    A["f_b2"] = f("L1_ffn_b2")
    return A


def kernel(**inputs):
    import concourse.bacc as bacc
    from concourse.bass_utils import run_bass_kernel_spmd

    nc = bacc.Bacc("TRN2", target_bir_lowering=False, num_devices=1)
    arrays = {f"in_{k}": v for k, v in layouts(inputs).items()}
    A = {k[3:]: nc.dram_tensor(k, v.shape, mybir.dt.from_np(v.dtype), kind="ExternalInput").ap() for k, v in arrays.items()}
    out = nc.dram_tensor("out", (NP, D), F32, kind="ExternalOutput").ap()
    build_program(nc, A, out)
    r = run_bass_kernel_spmd(nc, [arrays], core_ids=[0])
    return r.results[0]["out"][:N]
```
